# Optimizing a Trainium2 kernel written in Bass

```python
import numpy as np
import jax
import jax.numpy as jnp

def _softmax(x, axis=-1):
    return jax.nn.softmax(x, axis=axis)

def _gelu(x):
    return jax.nn.gelu(x, approximate=True)

def _silu(x):
    return jax.nn.silu(x)

def _sigmoid(x):
    return jax.nn.sigmoid(x)

def _layernorm(x, axis=-1, eps=1e-05):
    m = jnp.mean(x, axis=axis, keepdims=True)
    v = jnp.var(x, axis=axis, keepdims=True)
    return (x - m) / jnp.sqrt(v + eps)

def _scatter_add(tgt, idx, src, axis=0):
    return tgt.at[idx].add(src)

def _segment_sum(src, seg, n):
    return jax.ops.segment_sum(src, seg, n)
kernel_name = 'mk_gnn_preln_d4_gnn_r8_8488b8'

def setup_inputs(seed: int=0):
    np.random.seed(seed)
    _w = jnp.asarray

    def _rec_inputs():
        import jax
        import jax.numpy as jnp
        _gk = jax.random.key(seed)
        x = -0.000202 + 1 * jax.random.normal(jax.random.fold_in(_gk, 1), (6250, 128), jnp.float32)
        _s = jax.random.randint(jax.random.fold_in(_gk, 2), (50000,), 0, 6250, jnp.int32)
        _d = jax.random.randint(jax.random.fold_in(_gk, 3), (50000,), 0, 6250, jnp.int32)
        _loop = jnp.arange(6250, dtype=jnp.int32)
        src = jnp.concatenate([_s, _d, _loop])
        dst = jnp.concatenate([_d, _s, _loop])
        _o = jnp.argsort(dst, stable=True)
        src = src[_o]
        dst = dst[_o]
        edge_type_8 = jax.random.randint(jax.random.fold_in(_gk, 12), (106250,), 0, 8, jnp.int32)
        return (x, src, dst, edge_type_8)
    x, src, dst, edge_type_8 = _rec_inputs()

    def _L0_gnn_setup():
        import jax, jax.numpy as jnp
        import numpy as np
        N = 6250
        F_IN = 128
        HID = 128
        E = 100000
        BN_EPS = 1e-05
        L2_EPS = 1e-12

        def _mean_aggregate(x, src, dst):
            summed = jax.ops.segment_sum(x[src], dst, num_segments=N)
            deg = jax.ops.segment_sum(jnp.ones((src.shape[0],), x.dtype), dst, num_segments=N)
            return summed / jnp.maximum(deg, 1.0)[:, None]

        def _sage_conv(x, src, dst, Wl, bl, Wr):
            agg = _mean_aggregate(x, src, dst)
            out = agg @ Wl.T + bl + x @ Wr.T
            nrm = jnp.linalg.norm(out, axis=-1, keepdims=True)
            return out / jnp.maximum(nrm, L2_EPS)
        key = jax.random.key(seed)
        ks = jax.random.split(key, 8)
        s = 1.0 / np.sqrt(F_IN)
        return {'x': jax.random.normal(ks[0], (N, F_IN), dtype=jnp.float32), 'edge_index': jax.random.randint(ks[1], (2, E), 0, N, dtype=jnp.int64), 'Wl1': jax.random.normal(ks[2], (HID, F_IN), dtype=jnp.float32) * s, 'bl1': jnp.zeros((HID,), jnp.float32), 'Wr1': jax.random.normal(ks[3], (HID, F_IN), dtype=jnp.float32) * s, 'gamma': jnp.ones((HID,), jnp.float32), 'beta': jnp.zeros((HID,), jnp.float32), 'Wl2': jax.random.normal(ks[4], (HID, HID), dtype=jnp.float32) * s, 'bl2': jnp.zeros((HID,), jnp.float32), 'Wr2': jax.random.normal(ks[5], (HID, HID), dtype=jnp.float32) * s}
    _L0_gnn_all = _L0_gnn_setup()
    _L0_gnn_in = {k: v for k, v in _L0_gnn_all.items() if k in ('Wl1', 'bl1', 'Wr1', 'gamma', 'beta', 'Wl2', 'bl2', 'Wr2')}
    del _L0_gnn_all

    def _L1_gnn_setup():
        import jax, jax.numpy as jnp
        import numpy as np
        NUM_REL = 8
        SELF_WEIGHT = 0.5

        def _rgcn_layer(h, src, dst, et, W, root_w, b, N):
            xw = jnp.einsum('ni,rio->rno', h, W)
            cnt = jnp.zeros((W.shape[0], N), h.dtype).at[et, dst].add(1.0)
            msg = xw[et, src] / cnt[et, dst][:, None]
            agg = jax.ops.segment_sum(msg, dst, num_segments=N)
            return agg + h @ root_w + b
        key = jax.random.key(seed)
        ks = jax.random.split(key, 8)
        N, E, D, NB, HOP, R = (12500, 200000, 128, 4, 2, NUM_REL + 1)
        x = jax.random.normal(ks[0], (N, D), dtype=jnp.float32)
        edge_index = jax.random.randint(ks[1], (2, E), 0, N, dtype=jnp.int64)
        edge_type = jax.random.randint(ks[2], (E,), 0, NUM_REL, dtype=jnp.int64)
        scale = 1.0 / np.sqrt(D)
        bases = jax.random.normal(ks[3], (HOP, NB, D, D), dtype=jnp.float32) * scale
        comp = jax.random.normal(ks[4], (HOP, R, NB), dtype=jnp.float32)
        root = jax.random.normal(ks[5], (HOP, D, D), dtype=jnp.float32) * scale
        bias = jnp.zeros((HOP, D), dtype=jnp.float32)
        return {'x': x, 'edge_index': edge_index, 'edge_type': edge_type, 'bases': bases, 'comp': comp, 'root': root, 'bias': bias}
    _L1_gnn_all = _L1_gnn_setup()
    _L1_gnn_in = {k: v for k, v in _L1_gnn_all.items() if k in ('bases', 'comp', 'root', 'bias')}
    del _L1_gnn_all

    def _L2_gnn_setup():
        import jax, jax.numpy as jnp
        import numpy as np
        N_NODES = 6250
        N_EDGES = 100000
        HIDDEN = 128
        BN_EPS = 1e-05
        key = jax.random.key(seed)
        ks = jax.random.split(key, 4)
        x = jax.random.normal(ks[0], (N_NODES, HIDDEN), dtype=jnp.float32)
        edge_index = jax.random.randint(ks[1], (2, N_EDGES), 0, N_NODES, dtype=jnp.int64)
        scale = 1.0 / np.sqrt(HIDDEN)
        W1 = jax.random.normal(ks[2], (HIDDEN, HIDDEN), dtype=jnp.float32) * scale
        b1 = jnp.zeros((HIDDEN,), dtype=jnp.float32)
        W2 = jax.random.normal(ks[3], (HIDDEN, HIDDEN), dtype=jnp.float32) * scale
        b2 = jnp.zeros((HIDDEN,), dtype=jnp.float32)
        gamma = jnp.ones((HIDDEN,), dtype=jnp.float32)
        beta = jnp.zeros((HIDDEN,), dtype=jnp.float32)
        return {'x': x, 'edge_index': edge_index, 'W1': W1, 'b1': b1, 'W2': W2, 'b2': b2, 'gamma': gamma, 'beta': beta}
    _L2_gnn_all = _L2_gnn_setup()
    _L2_gnn_in = {k: v for k, v in _L2_gnn_all.items() if k in ('W1', 'b1', 'W2', 'b2', 'gamma', 'beta')}
    del _L2_gnn_all

    def _L3_gnn_setup():
        import jax, jax.numpy as jnp
        import numpy as np
        N, E, D, A = (12500, 75000, 128, 5)

        def _glorot(key, shape):
            fan = shape[0] + shape[1]
            s = jnp.sqrt(6.0 / fan)
            return jax.random.uniform(key, shape, jnp.float32, -s, s)
        key = jax.random.key(seed)
        ks = jax.random.split(key, 8)
        x = jax.random.normal(ks[0], (N, D), jnp.float32)
        edge_index = jax.random.randint(ks[1], (2, E), 0, N, dtype=jnp.int64)
        node_anchor = _glorot(ks[2], (A, D))
        attn_w = _glorot(ks[3], (A, D))
        attn_b = jnp.zeros((A,), jnp.float32)
        edge_anchor = _glorot(ks[4], (A, D))
        edge_w = _glorot(ks[5], (A, 2 * D))
        edge_b = jnp.zeros((A,), jnp.float32)
        return dict(x=x, node_anchor=node_anchor, attn_w=attn_w, attn_b=attn_b, edge_anchor=edge_anchor, edge_w=edge_w, edge_b=edge_b, edge_index=edge_index)
    _L3_gnn_all = _L3_gnn_setup()
    _L3_gnn_in = {k: v for k, v in _L3_gnn_all.items() if k in ('node_anchor', 'attn_w', 'attn_b', 'edge_anchor', 'edge_w', 'edge_b')}
    del _L3_gnn_all
    return {'x': x, 'src': src, 'dst': dst, 'edge_type_8': edge_type_8, 'L0_gnn_Wl1': _L0_gnn_in['Wl1'], 'L0_gnn_bl1': _L0_gnn_in['bl1'], 'L0_gnn_Wr1': _L0_gnn_in['Wr1'], 'L0_gnn_gamma': _L0_gnn_in['gamma'], 'L0_gnn_beta': _L0_gnn_in['beta'], 'L0_gnn_Wl2': _L0_gnn_in['Wl2'], 'L0_gnn_bl2': _L0_gnn_in['bl2'], 'L0_gnn_Wr2': _L0_gnn_in['Wr2'], 'L1_gnn_bases': _L1_gnn_in['bases'], 'L1_gnn_comp': _L1_gnn_in['comp'], 'L1_gnn_root': _L1_gnn_in['root'], 'L1_gnn_bias': _L1_gnn_in['bias'], 'L2_gnn_W1': _L2_gnn_in['W1'], 'L2_gnn_b1': _L2_gnn_in['b1'], 'L2_gnn_W2': _L2_gnn_in['W2'], 'L2_gnn_b2': _L2_gnn_in['b2'], 'L2_gnn_gamma': _L2_gnn_in['gamma'], 'L2_gnn_beta': _L2_gnn_in['beta'], 'L3_gnn_node_anchor': _L3_gnn_in['node_anchor'], 'L3_gnn_attn_w': _L3_gnn_in['attn_w'], 'L3_gnn_attn_b': _L3_gnn_in['attn_b'], 'L3_gnn_edge_anchor': _L3_gnn_in['edge_anchor'], 'L3_gnn_edge_w': _L3_gnn_in['edge_w'], 'L3_gnn_edge_b': _L3_gnn_in['edge_b']}

def reference(x, src, dst, edge_type_8, L0_gnn_Wl1, L0_gnn_bl1, L0_gnn_Wr1, L0_gnn_gamma, L0_gnn_beta, L0_gnn_Wl2, L0_gnn_bl2, L0_gnn_Wr2, L1_gnn_bases, L1_gnn_comp, L1_gnn_root, L1_gnn_bias, L2_gnn_W1, L2_gnn_b1, L2_gnn_W2, L2_gnn_b2, L2_gnn_gamma, L2_gnn_beta, L3_gnn_node_anchor, L3_gnn_attn_w, L3_gnn_attn_b, L3_gnn_edge_anchor, L3_gnn_edge_w, L3_gnn_edge_b):
    import jax
    import jax.numpy as jnp

    def _L0_gnn_ref(x, edge_index, Wl1, bl1, Wr1, gamma, beta, Wl2, bl2, Wr2):
        import jax, jax.numpy as jnp
        import numpy as np
        N = 6250
        F_IN = 128
        HID = 128
        E = 100000
        BN_EPS = 1e-05
        L2_EPS = 1e-12

        def _mean_aggregate(x, src, dst):
            summed = jax.ops.segment_sum(x[src], dst, num_segments=N)
            deg = jax.ops.segment_sum(jnp.ones((src.shape[0],), x.dtype), dst, num_segments=N)
            return summed / jnp.maximum(deg, 1.0)[:, None]

        def _sage_conv(x, src, dst, Wl, bl, Wr):
            agg = _mean_aggregate(x, src, dst)
            out = agg @ Wl.T + bl + x @ Wr.T
            nrm = jnp.linalg.norm(out, axis=-1, keepdims=True)
            return out / jnp.maximum(nrm, L2_EPS)
        src, dst = (edge_index[0], edge_index[1])
        h = _sage_conv(x, src, dst, Wl1, bl1, Wr1)
        h = jax.nn.relu(h)
        mu = jnp.mean(h, axis=0)
        var = jnp.var(h, axis=0)
        h = (h - mu) / jnp.sqrt(var + BN_EPS) * gamma + beta
        return _sage_conv(h, src, dst, Wl2, bl2, Wr2)

    def _L1_gnn_ref(x, edge_index, edge_type, bases, comp, root, bias):
        import jax, jax.numpy as jnp
        import numpy as np
        NUM_REL = 8
        SELF_WEIGHT = 0.5

        def _rgcn_layer(h, src, dst, et, W, root_w, b, N):
            xw = jnp.einsum('ni,rio->rno', h, W)
            cnt = jnp.zeros((W.shape[0], N), h.dtype).at[et, dst].add(1.0)
            msg = xw[et, src] / cnt[et, dst][:, None]
            agg = jax.ops.segment_sum(msg, dst, num_segments=N)
            return agg + h @ root_w + b
        N = x.shape[0]
        loop = jnp.arange(N, dtype=edge_index.dtype)
        src = jnp.concatenate([edge_index[0], loop])
        dst = jnp.concatenate([edge_index[1], loop])
        et = jnp.concatenate([edge_type, jnp.full((N,), NUM_REL, dtype=edge_type.dtype)])
        hop = bases.shape[0]
        out = x
        for l in range(hop):
            W = jnp.einsum('rb,bio->rio', comp[l], bases[l])
            h = _rgcn_layer(out, src, dst, et, W, root[l], bias[l], N)
            h = jnp.maximum(h, 0.0) if l < hop - 1 else h
            out = SELF_WEIGHT * out + (1.0 - SELF_WEIGHT) * h
        return out

    def _L2_gnn_ref(x, edge_index, W1, b1, W2, b2, gamma, beta):
        import jax, jax.numpy as jnp
        import numpy as np
        N_NODES = 6250
        N_EDGES = 100000
        HIDDEN = 128
        BN_EPS = 1e-05
        src = edge_index[0]
        dst = edge_index[1]
        agg = jax.ops.segment_sum(x[src], dst, num_segments=x.shape[0])
        h = x + agg
        h = jnp.maximum(h @ W1 + b1, 0.0)
        h = h @ W2 + b2
        mean = jnp.mean(h, axis=0)
        var = jnp.var(h, axis=0)
        h = (h - mean) * jax.lax.rsqrt(var + BN_EPS) * gamma + beta
        return h

    def _L3_gnn_ref(x, node_anchor, attn_w, attn_b, edge_anchor, edge_w, edge_b, edge_index):
        import jax, jax.numpy as jnp
        import numpy as np
        N, E, D, A = (12500, 75000, 128, 5)

        def _glorot(key, shape):
            fan = shape[0] + shape[1]
            s = jnp.sqrt(6.0 / fan)
            return jax.random.uniform(key, shape, jnp.float32, -s, s)
        w = jax.nn.softmax(x @ attn_w.T + attn_b, axis=1)
        xp = x + w @ node_anchor
        src, dst = (edge_index[0], edge_index[1])
        combined = jnp.concatenate([x[src], x[dst]], axis=1)
        b = jax.nn.softmax(jax.nn.leaky_relu(combined @ edge_w.T + edge_b, 0.01), axis=1)
        ep = b @ edge_anchor
        agg = jnp.zeros_like(xp).at[src].add(ep).at[dst].add(ep)
        return xp + 0.5 * agg
    edge_index = jnp.stack([src, dst])
    h = jnp.maximum(_layernorm(x, axis=-1), 0.0)
    x = x + _L0_gnn_ref(h, edge_index, L0_gnn_Wl1, L0_gnn_bl1, L0_gnn_Wr1, L0_gnn_gamma, L0_gnn_beta, L0_gnn_Wl2, L0_gnn_bl2, L0_gnn_Wr2)
    h = jnp.maximum(_layernorm(x, axis=-1), 0.0)
    x = x + _L1_gnn_ref(h, edge_index, edge_type_8, L1_gnn_bases, L1_gnn_comp, L1_gnn_root, L1_gnn_bias)
    h = jnp.maximum(_layernorm(x, axis=-1), 0.0)
    x = x + _L2_gnn_ref(h, edge_index, L2_gnn_W1, L2_gnn_b1, L2_gnn_W2, L2_gnn_b2, L2_gnn_gamma, L2_gnn_beta)
    h = jnp.maximum(_layernorm(x, axis=-1), 0.0)
    x = x + _L3_gnn_ref(h, L3_gnn_node_anchor, L3_gnn_attn_w, L3_gnn_attn_b, L3_gnn_edge_anchor, L3_gnn_edge_w, L3_gnn_edge_b, edge_index)
    return x

_drawn_inputs = setup_inputs


def setup_inputs(seed=0):
    import zlib

    import numpy as np

    out = dict(_drawn_inputs(seed))
    spreads = {'L0_gnn_bl1': (0.0, 2.0),
     'L0_gnn_gamma': (1.0, 0.6),
     'L0_gnn_beta': (0.0, 0.603),
     'L0_gnn_bl2': (0.0, 0.8),
     'L1_gnn_bias': (0.0, 0.282),
     'L2_gnn_b1': (0.0, 2.0),
     'L2_gnn_b2': (0.0, 2.0),
     'L2_gnn_gamma': (1.0, 0.2),
     'L2_gnn_beta': (0.0, 0.27),
     'L3_gnn_attn_b': (0.0, 2.0),
     'L3_gnn_edge_b': (0.0, 0.289)}
    factors = {'L3_gnn_node_anchor': 3.187, 'L3_gnn_attn_w': 5.398, 'L0_gnn_Wl1': 2.995}
    for name, (base, spread) in spreads.items():
        noise = np.random.default_rng([zlib.crc32(name.encode()), seed]).standard_normal(out[name].shape)
        drawn = base * np.exp(spread * noise) if base else spread * noise
        out[name] = jnp.asarray(drawn.astype(out[name].dtype))
    for name, factor in factors.items():
        out[name] = (out[name] * factor).astype(out[name].dtype)
    return out
```

```python
import concourse.bass as bass
from concourse import mybir
from concourse.alu_op_type import AluOpType as ALU
from contextlib import ExitStack

FP = mybir.dt.float32
I32 = mybir.dt.int32
ACT = mybir.ActivationFunctionType
AX = mybir.AxisListType

P = 128
N = 6250
E = 106250
NB = 50
NPAD = NB * P
PAD_NODE = 49 * P - 1
TILES = 832
CHUNKS = 7
COLS = CHUNKS * P
GT = 4
GROUPS = TILES // GT
LOOK = GROUPS + 1
WINDOWS = NB // 2
ITERS = GROUPS // 4
R = 8
A5 = 5
AW = P + R
NCHANNELS = float(P)
LAST = N - 48 * P
EPS = 1e-5
L2_EPS = 1e-12
CREDIT = 4
WEIGHT_LOADS = 27


def gnn_stack(nc, x, src, dst, edge_type, Wl1, bl1, Wr1, gamma0, beta0, Wl2, bl2, Wr2,
              bases, comp, root, bias1, W1, b1, W2, b2, gamma2, beta2,
              node_anchor, attn_w, attn_b, edge_anchor, edge_w, edge_b, out):
    ctx = ExitStack()
    with ctx:
        def sb(name, cols, dt=FP, parts=P):
            return ctx.enter_context(nc.sbuf_tensor(name, [parts, cols], dt))

        def sem(name):
            return ctx.enter_context(nc.semaphore(name))

        def dram(name, shape, dt=FP):
            return nc.dram_tensor(name, shape, dt, kind="Internal").ap()

        h_table = dram("h_table", [NPAD, P])
        xw_table = dram("xw_table", [R * NPAD, P])
        p_table = dram("p_table", [NPAD, R])
        cnt_table = dram("cnt_table", [NPAD, R])
        q_table = dram("q_table", [NPAD, A5])
        dst_rows = dram("dst_rows", [COLS * P], I32)

        X = sb("X", NB * P)
        H = sb("H", NB * P)
        O = sb("O", NB * P)
        T = sb("T", NB * P)
        A = sb("A", NB * AW)
        blocks = lambda t: t[:, 0:NB * P].rearrange("p (b f) -> p b f", f=P)
        by_feature = lambda t: t[:, 0:NB * P].rearrange("p (b f) -> p f b", f=P)
        X3, H3, O3, T3 = blocks(X), blocks(H), blocks(O), blocks(T)
        A3 = A[:, :].rearrange("p (b f) -> p b f", f=AW)
        AF = A3[:, :, 0:P]
        inv_deg = sb("inv_deg", NB)
        inv_cnt = sb("inv_cnt", NB * R)

        src_i = sb("src_i", COLS, I32)
        xw_i = sb("xw_i", COLS, I32)
        et_f = sb("et_f", COLS)
        dl = sb("dl", COLS)
        wt = sb("wt", COLS)
        src_lo = sb("src_lo", COLS)
        src_hi = sb("src_hi", COLS)
        neg_row = [sb(f"neg_row{h}", GROUPS) for h in range(2)]
        blk_i = sb("blk_i", GROUPS, I32)
        lo_g = sb("lo_g", COLS // GT)
        hi_g = sb("hi_g", COLS // GT)

        rest_i = sb("rest_i", 1, I32)
        rest_f = sb("rest_f", 1)
        outside = sb("outside", GT)
        rest4 = sb("rest4", GT)
        rest_base = sb("rest_base", 1)
        rest_w = sb("rest_w", GT)

        stage = [sb(f"stage{g}", GT, I32) for g in range(4)]
        stage16 = [sb(f"stage16_{i}", 4 * GT, I32) for i in range(2)]
        G = [sb(f"G{g}", GT * AW) for g in range(4)]
        G3 = [t[:, :].rearrange("p (j f) -> p j f", f=AW) for t in G]
        S = sb("S", 2 * GT * 2 * P)
        S3 = [S[:, i * GT * 2 * P:(i + 1) * GT * 2 * P].rearrange("p (j d) -> p j d", d=2 * P) for i in range(2)]
        dst_b = [sb(f"dst_b{i}", GT * P, I32) for i in range(2)]

        iota = sb("iota", 2 * P)
        iota_p = sb("iota_p", 1)
        ident = sb("ident", P)
        ones = sb("ones", P)
        row_mask = sb("row_mask", 1)
        WT = sb("WT", 4 * P)
        PRJ = sb("PRJ", P)
        Wcat = [sb(f"Wcat{l}", (R + 1) * P) for l in range(2)]
        W1s, W2s = sb("W1s", P), sb("W2s", P)
        rows = sb("rows", 9 * P)
        BL1, GA0, BE0, BL2, B10, B11, B2, GA2, BE2 = (rows[:, i * P:(i + 1) * P] for i in range(9))
        b1c = sb("b1c", 1)
        comp_b = sb("comp_b", 2 * (R + 1) * 4)
        ab = sb("ab", 2 * A5)
        anchors = sb("anchors", P, FP, 32)
        in_st = [sb(f"in_st{i}", 2 * P) for i in range(2)]
        tT = [sb(f"tT{i}", 2 * P) for i in range(2)]
        zT = [sb(f"zT{i}", P) for i in range(2)]
        stat = sb("stat", NB)
        stat2 = sb("stat2", NB)
        mu = sb("mu", P)
        var = sb("var", P)
        sd = sb("sd", P)
        part = sb("part", P)

        raw_i = [O[:, a * COLS:(a + 1) * COLS].bitcast(I32) for a in range(3)]
        raw3 = [r.rearrange("t (c p) -> t c p", p=P) for r in raw_i]
        raw_f = [O[:, (3 + a) * COLS:(4 + a) * COLS] for a in range(3)]
        blk_t = T[:, 0:COLS].bitcast(I32)
        blk_f = T[:, COLS:2 * COLS]
        tile_lo, tile_hi = T[:, 2 * COLS:2 * COLS + 8], T[:, 2 * COLS + 8:2 * COLS + 16]
        diag = T[:, 2 * COLS + P:2 * COLS + P + 14 * P].rearrange("p (c t) -> p c t", t=P)
        w_raw = T[:, 4800:4800 + 5 * P].rearrange("p (w f) -> p w f", f=P)
        base_s = A[:, 0:2 * 4 * P].rearrange("p (l n o) -> p l n o", l=2, n=4)
        root_s = A[:, 8 * P:10 * P].rearrange("p (l o) -> p l o", l=2)
        src_t = A[:, 1400:1400 + COLS].bitcast(I32)
        tmp_i = A[:, 1400 + COLS:1400 + 2 * COLS].bitcast(I32)
        src_f = A[:, 1400 + 2 * COLS:1400 + 3 * COLS]
        dst_f = A[:, 1400 + 3 * COLS:1400 + 4 * COLS]
        tmp_f = A[:, 1400 + 4 * COLS:1400 + 5 * COLS]
        xw_out = [T[:, i * R * P:(i + 1) * R * P] for i in range(2)]
        oht = [[T[:, (2 * s + h) * GT * P:(2 * s + h + 1) * GT * P] for h in range(2)] for s in range(2)]
        ohe = [T[:, 4096 + s * GT * R:4096 + (s + 1) * GT * R].rearrange("p (j r) -> p j r", r=R) for s in range(2)]
        wsel = [T[:, 4224 + s * GT * R:4224 + (s + 1) * GT * R].rearrange("p (j r) -> p j r", r=R) for s in range(2)]
        L16 = 4 * GT
        S_l3 = T[:, 0:L16 * 2 * P].rearrange("p (j d) -> p j d", d=2 * P)
        PRo = T[:, 4096:4096 + NB * 15].rearrange("p (b a) -> p b a", a=15)
        PT = T[:, 4900:4900 + NB * R].rearrange("p (b a) -> p b a", a=R)
        U = S[:, 0:NB * 32]
        U3 = U[:, :].rearrange("p (b a) -> p b a", a=32)
        M_l3 = O[:, 0:L16 * 245].rearrange("p (j m) -> p j m", m=245)
        lo_l3 = O[:, 3920:3920 + L16 * P].rearrange("p (j d) -> p j d", d=P)
        oht_l3 = A[:, 0:4096].rearrange("p (g h e) -> p g h e", g=4, h=2)
        hi_l3 = A[:, 4096:4096 + L16 * 49].rearrange("p (j d) -> p j d", d=49)
        sums5 = A[:, 4900:4900 + NB * A5]
        Q = A[:, 5200:5200 + NB * A5]
        Q3 = Q.rearrange("p (b a) -> p b a", a=A5)
        p_rows = [A[:, 5500 + i * L16 * R:5500 + (i + 1) * L16 * R].rearrange("p (j a) -> p j a", a=R) for i in range(2)]
        zeros = O[:, 5968:5968 + NB * A5]
        z5 = A[:, 5800:5800 + L16 * A5].rearrange("p (j a) -> p j a", a=A5)
        y5 = A[:, 5900:5900 + L16 * A5].rearrange("p (j a) -> p j a", a=A5)
        b5 = A[:, 6000:6000 + L16 * A5].rearrange("p (j a) -> p j a", a=A5)
        m5 = A[:, 6100:6100 + L16]
        r5 = A[:, 6120:6120 + L16]
        n5 = [A[:, 6200 + i * NB * A5:6200 + (i + 1) * NB * A5].rearrange("p (b a) -> p b a", a=A5) for i in range(2)]

        bank = [ctx.enter_context(nc.psum_tensor(f"bank{i}", [P, 512], FP)) for i in range(8)]

        consts = sem("consts")
        cleared = sem("cleared")
        x_in = sem("x_in")
        edges_in = sem("edges_in")
        weights_in = sem("weights_in")
        dst_out = sem("dst_out")
        edges_f = sem("edges_f")
        ident_done = sem("ident_done")
        edges_t = sem("edges_t")
        edges_c = sem("edges_c")
        ranges_d = sem("ranges_d")
        ranges_b = sem("ranges_b")
        w_t = sem("w_t")
        w_c = sem("w_c")
        prep_done = sem("prep_done")
        to_root = sem("to_root")
        rooted = sem("rooted")
        h_ready = sem("h_ready")
        table_in = sem("table_in")
        to_sum = sem("to_sum")
        summed = sem("summed")
        dve_done = sem("dve_done")
        idx_staged = sem("idx_staged")
        sp_turn = sem("sp_turn")
        pe_turn = sem("pe_turn")
        dve_turn = sem("dve_turn")
        pool_turn = sem("pool_turn")
        gathered = [sem(f"gathered{g}") for g in range(4)]
        windows_ready = sem("windows_ready")
        windows_summed = sem("windows_summed")
        sums_added = sem("sums_added")
        dst_in = [sem(f"dst_in{i}") for i in range(2)]
        oht_abs = sem("oht_abs")
        oht_ready = sem("oht_ready")
        looked_up = sem("looked_up")
        wt_picked = sem("wt_picked")
        wt_done = sem("wt_done")
        staged_d = sem("staged_d")
        staged_a = sem("staged_a")
        transposed = sem("transposed")
        t_copied = sem("t_copied")
        multiplied = sem("multiplied")
        evac_d = sem("evac_d")
        evac_a = sem("evac_a")
        hidden = sem("hidden")
        hidden_c = sem("hidden_c")
        xw_stored = [sem(f"xw_stored{i}") for i in range(2)]
        p_ready = sem("p_ready")
        idx16 = sem("idx16")
        gathered16 = [sem(f"gathered16_{u}") for u in range(2)]
        q_looked = sem("q_looked")
        logits_done = sem("logits_done")
        soft_step = sem("soft_step")
        soft_in = sem("soft_in")
        soft_exp = sem("soft_exp")
        soft_mul = sem("soft_mul")
        ready5 = sem("ready5")
        scattered = sem("scattered")
        added5 = sem("added5")
        zeros_done = sem("zeros_done")
        scat_all = sem("scat_all")
        rest_table = sem("rest_table")
        rest_table_in = sem("rest_table_in")
        rest_staged = sem("rest_staged")
        rest_gathered = [sem(f"rest_gathered{z}") for z in range(7)]
        rest_step = [sem(f"rest_step{z}") for z in range(7)]
        rest_windows = sem("rest_windows")
        rest_summed = sem("rest_summed")
        rest_added = sem("rest_added")
        rest_shift = sem("rest_shift")
        rest_soft = sem("rest_soft")
        rest_exp = sem("rest_exp")
        rest_ready5 = sem("rest_ready5")
        u_ready = sem("u_ready")
        out_ready = sem("out_ready")
        stored = sem("stored")

        block = ctx.enter_context(nc.Block())

        SAGE1, SAGE2, HOP1, HOP2, GIN, PROJ, ANCHOR = range(7)
        BY_DVE, BY_ACT = (SAGE1, SAGE2, GIN), (SAGE1, SAGE2, HOP1, HOP2, PROJ, ANCHOR)
        staged_d_before = lambda i: NB * sum(l < i for l in BY_DVE)
        staged_a_before = lambda i: NB * sum(l < i for l in BY_ACT)

        def in_pairs(eng, body):
            for b in range(4):
                body(b, b % 2, b // 2)
            with eng.Fori(2, NB // 2) as it:
                body(it * 2, 0, it)
                body(it * 2 + 1, 1, it)

        class Chain:
            def __init__(self, eng, sem):
                self.eng, self.sem, self.n = eng, sem, 0

            def __call__(self, ins):
                self.n += 1
                ins.then_inc(self.sem, 1)
                self.eng.wait_ge(self.sem, self.n)

        def width_in(i):
            return {SAGE1: 2 * P, SAGE2: 2 * P, ANCHOR: 32}.get(i, P)

        REST_SAGE1, REST_SAGE2, REST_WT, REST_HOP1, REST_HOP2, REST_GIN, REST_L3 = range(7)
        rest_sums_before = lambda z: {REST_SAGE1: 0, REST_SAGE2: 1, REST_HOP1: 2, REST_HOP2: 3, REST_GIN: 4, REST_L3: 5}[z]

        def if_rest(eng):
            return eng.If(eng.value_load(rest_i[0:1, 0:1], min_val=0, max_val=1) > 0)

        @block.sync
        def _(sp):
            full = 6 * P * P
            whole = (E - full) // P
            rest = E - full - whole * P
            sp.wait_ge(cleared, 6)
            for a, arr in enumerate((src, dst, edge_type)):
                sp.dma_start(raw3[a][:, 0:6, :], arr[0:full].rearrange("(c t p) -> t c p", p=P, c=6)).then_inc(edges_in, 16)
                sp.dma_start(raw3[a][0:whole, 6, :], arr[full:full + whole * P].rearrange("(t p) -> t p", p=P)).then_inc(edges_in, 16)
                sp.dma_start(raw3[a][whole:whole + 1, 6, 0:rest], arr[full + whole * P:E].rearrange("(o p) -> o p", o=1)).then_inc(edges_in, 16)
            sp.dma_start(X3[:, 0:48, :], x[0:48 * P, :].rearrange("(b p) f -> p b f", p=P)).then_inc(x_in, 16)
            sp.dma_start(X3[0:LAST, 48, :], x[48 * P:N, :]).then_inc(x_in, 16)
            loads = [(w_raw[:, i, :], w) for i, w in enumerate((Wl1, Wr1, Wl2, Wr2))]
            loads += [(w_raw[0:A5, 4, :], attn_w), (w_raw[A5:2 * A5, 4, :], edge_w[:, 0:P]),
                      (w_raw[2 * A5:3 * A5, 4, :], edge_w[:, P:2 * P])]
            loads += [(base_s[:, l], bases[l].rearrange("n i o -> i n o")) for l in range(2)]
            loads += [(root_s, root.rearrange("l i o -> i l o")),
                      (comp_b[:, :], comp.rearrange("l r n -> (l r n)").partition_broadcast(P)),
                      (W1s[:, :], W1), (W2s[:, :], W2)]
            loads += [(row, v.partition_broadcast(P)) for row, v in (
                (BL1, bl1), (GA0, gamma0), (BE0, beta0), (BL2, bl2), (B10, bias1[0, :]), (B11, bias1[1, :]),
                (B2, b2), (GA2, gamma2), (BE2, beta2), (ab[:, 0:A5], attn_b), (ab[:, A5:], edge_b))]
            loads += [(b1c[:, :], b1.rearrange("(p o) -> p o", o=1)),
                      (anchors[0:A5, :], node_anchor), (anchors[A5:2 * A5, :], edge_anchor)]
            assert len(loads) == WEIGHT_LOADS
            for to, of in loads:
                sp.dma_start(to, of).then_inc(weights_in, 16)
            sp.wait_ge(edges_in, 9 * 16)
            sp.dma_start(dst_rows.rearrange("(c t p) -> t c p", p=P, c=CHUNKS), raw3[1]).then_inc(dst_out, 16)

            def group_destinations(q):
                with sp.Fori(0, GROUPS // 2) as it:
                    for s in range(2):
                        k = it * 2 + s
                        edge = sp.snap(k * (GT * P), min_val=0, max_val=(GROUPS - 1) * GT * P)
                        sp.wait_ge(oht_abs, q * GROUPS + k + 1)
                        sp.dma_start(dst_b[s][:, :], dst_rows[bass.ds(edge, GT * P)].partition_broadcast(P)).then_inc(dst_in[s], 16)

            def store_h(v):
                sp.wait_ge(h_ready, v)
                sp.dma_start(h_table.rearrange("(b p) f -> p b f", p=P), H3).then_inc(table_in, 16)

            store_h(1)
            store_h(2)
            sp.wait_ge(dst_out, 16)
            group_destinations(0)
            sp.wait_ge(prep_done, 1)
            with if_rest(sp):
                sp.wait_ge(rest_table, 1)
                sp.dma_start(cnt_table.rearrange("(b p) r -> p b r", p=P),
                             inv_cnt[:, :].rearrange("p (b r) -> p b r", r=R)).then_inc(rest_table_in, 16)
            for l in range(2):
                with sp.Fori(0, NB // 2) as it:
                    for s in range(2):
                        b = it * 2 + s
                        node = sp.snap(b * P, min_val=0, max_val=(NB - 1) * P)
                        sp.wait_ge(evac_d, NB * (HOP1 + l) + b + 3)
                        sp.sem_inc(sp_turn, 1)
                        sp.wait_ge(evac_a, NB * l + b + 1)
                        sp.dma_start(xw_table.rearrange("(r n) f -> n r f", r=R)[bass.ds(node, P), :, :],
                                     xw_out[s].rearrange("p (r f) -> p r f", f=P)).then_inc(xw_stored[s], 16)
            store_h(5)
            sp.wait_ge(p_ready, 1)
            sp.dma_start(p_table.rearrange("(b p) a -> p b a", p=P), PT).then_inc(table_in, 16)
            group_destinations(1)
            with if_rest(sp):
                sp.wait_ge(rest_table, 2)
                sp.dma_start(q_table.rearrange("(b p) a -> p b a", p=P), Q3).then_inc(rest_table_in, 16)
            sp.wait_ge(out_ready, 1)
            sp.dma_start(out[0:48 * P, :].rearrange("(b p) f -> p b f", p=P), X3[:, 0:48, :]).then_inc(stored, 16)
            sp.dma_start(out[48 * P:N, :], X3[0:LAST, 48, :]).then_inc(stored, 16)
            sp.wait_ge(stored, 32)

        @block.gpsimd
        def _(pool):
            nc.gpsimd.iota(iota[:, :], [[1, 2 * P]], base=0, channel_multiplier=0,
                           allow_small_or_imprecise_dtypes=True).then_inc(consts, 1)
            nc.gpsimd.iota(iota_p[:, :], [[0, 1]], base=0, channel_multiplier=1,
                           allow_small_or_imprecise_dtypes=True).then_inc(consts, 1)

            def gather(to, table, idx, done):
                nc.gpsimd.indirect_dma_start(out=to, out_offset=None, in_=table,
                                             in_offset=bass.IndirectOffsetOnAxis(ap=idx, axis=0)).then_inc(done, 16)

            def gather_pass(q, table):
                with pool.Fori(0, ITERS) as it:
                    for g in range(4):
                        pool.wait_ge(idx_staged, GROUPS * q + it * 4 + g + 1)
                        pool.sem_inc(pool_turn, 1)
                        for j in range(GT):
                            gather(G3[g][:, j, 0:P], table, stage[g][:, j:j + 1], gathered[g])

            def gather_rest(z, *tables):
                with if_rest(pool):
                    if z in (REST_WT, REST_L3):
                        pool.wait_ge(rest_table_in, 16 if z == REST_WT else 32)
                    with pool.Fori(0, GROUPS) as k:
                        pool.wait_ge(rest_staged, (k + 1) * len(tables) + z * GROUPS)
                        pool.sem_inc(pool_turn, 1)
                        for i, (t, w) in enumerate(tables):
                            for j in range(GT):
                                gather(G3[i][:, j, 0:w], t, stage[i][:, j:j + 1], rest_gathered[z])

            pool.wait_ge(prep_done, 1)
            pool.wait_ge(table_in, 16)
            gather_pass(0, h_table)
            gather_rest(REST_SAGE1, (h_table, P))
            pool.wait_ge(table_in, 32)
            gather_pass(1, h_table)
            gather_rest(REST_SAGE2, (h_table, P))
            gather_rest(REST_WT, (cnt_table, R))
            for l in range(2):
                for s in range(2):
                    pool.wait_ge(xw_stored[s], 16 * (NB // 2) * (l + 1))
                gather_pass(2 + l, xw_table)
                gather_rest(REST_HOP1 + l, (xw_table, P))
            pool.wait_ge(table_in, 48)
            gather_pass(4, h_table)
            gather_rest(REST_GIN, (h_table, P))
            pool.wait_ge(table_in, 64)
            with pool.Fori(0, ITERS // 2) as i2:
                for u in range(2):
                    it = i2 * 2 + u
                    pool.wait_ge(idx16, it + 1)
                    pool.wait_ge(logits_done, it + 1)
                    pool.sem_inc(pool_turn, 1)
                    for t in range(L16):
                        gather(p_rows[u][:, t, :], p_table, stage16[u][:, t:t + 1], gathered16[u])
            gather_rest(REST_L3, (p_table, R), (q_table, A5))

        @block.scalar
        def _(act):
            def sqrt(to, of, v):
                act.wait_ge(to_root, v)
                nc.scalar.activation(to, of, ACT.Sqrt).then_inc(rooted, 1)

            def stage_pass(q, idx, more=None):
                with act.Fori(0, ITERS) as it:
                    for g in range(4):
                        act.wait_ge(windows_summed, GROUPS * q + it * 4 + g + 1)
                        nc.scalar.activation(stage[g][:, :], idx[:, bass.ds((it * 4 + g) * GT, GT)],
                                             ACT.Copy).then_inc(idx_staged, 1)
                        if more:
                            more(it, g)

            def one_hot_rows(q, it, g, to, used, used_at):
                k = it * 4 + g
                act.wait_ge(dst_in[g % 2], 16 * ((GROUPS // 2) * q + it * 2 + g // 2 + 1))
                act.wait_ge(used, used_at)
                nc.scalar.activation(to[0], dst_b[g % 2][:, :], ACT.Abs, bias=neg_row[0][:, bass.ds(k, 1)])
                nc.scalar.activation(to[1], dst_b[g % 2][:, :], ACT.Abs, bias=neg_row[1][:, bass.ds(k, 1)]).then_inc(oht_abs, 1)
                act.wait_ge(oht_abs, q * GROUPS + k + 3)
                nc.scalar.activation(to[0], to[0], ACT.Relu, bias=1.0, scale=-1.0)
                nc.scalar.activation(to[1], to[1], ACT.Relu, bias=1.0, scale=-1.0).then_inc(oht_ready, 1)

            def block_loop(i, stage_block=None, late=None):
                w = width_in(i)
                parts = 32 if i == ANCHOR else P

                def body(b, s, pair):
                    n = NB * i + b
                    if stage_block:
                        act.wait_ge(transposed, n + 1)
                        stage_block(b, s).then_inc(staged_a, 1)
                    act.wait_ge(transposed, n + 3)
                    act.wait_ge(multiplied, n + 1)
                    cols = P if i == ANCHOR else w
                    nc.scalar.activation(tT[s][0:parts, 0:cols], bank[6 + s][0:parts, 0:cols], ACT.Copy).then_inc(t_copied, 1)
                    if late and not (isinstance(b, int) and b == 0):
                        late(b - 1, 1 - s, pair - 1 + s)

                in_pairs(act, body)
                if late:
                    late(NB - 1, 1, NB // 2 - 1)

            def stage_h(cols):
                return lambda b, s: nc.scalar.activation(in_st[s][:, cols], H[:, bass.ds(b * P, P)], ACT.Copy)

            act.sem_inc(oht_abs, 2)
            act.sem_inc(t_copied, 2)
            for c in range(6):
                act.wait_ge(edges_t, c + 1)
                to = (src_f, dst_f, et_f)[c // 2]
                w = 4 * P if c % 2 == 0 else 3 * P
                nc.scalar.activation(to[:, (c % 2) * 4 * P:(c % 2) * 4 * P + w], bank[c % 2][:, 0:w], ACT.Copy).then_inc(edges_c, 1)
            act.wait_ge(w_t, 1)
            nc.scalar.activation(WT[:, :], bank[2][:, :], ACT.Copy).then_inc(w_c, 1)
            nc.scalar.activation(PRJ[:, :], bank[3][:, 0:P], ACT.Copy).then_inc(w_c, 1)
            sqrt(stat2[:, :], stat[:, :], 1)
            act.wait_ge(prep_done, 1)
            stage_pass(0, src_i)
            block_loop(SAGE1, stage_h(slice(P, 2 * P)))
            sqrt(stat2[:, :], stat[:, :], 2)
            sqrt(sd[:, :], var[:, :], 3)
            act.wait_ge(h_ready, 2)
            stage_pass(1, src_i, lambda it, g: one_hot_rows(0, it, g, oht[g % 2], looked_up, it * 4 + g + 1))
            block_loop(SAGE2, stage_h(slice(P, 2 * P)))
            sqrt(stat2[:, :], stat[:, :], 4)
            sqrt(stat2[:, :], stat[:, :], 5)
            for l in range(2):
                def evacuate(m, s, pair):
                    act.wait_ge(multiplied, NB * (HOP1 + l) + m + 3)
                    if not (l == 0 and isinstance(pair, int) and pair == 0):
                        act.wait_ge(xw_stored[s], 16 * ((NB // 2) * l + pair))
                    nc.scalar.activation(xw_out[s][:, 4 * P:8 * P], bank[3 + 2 * s][:, :], ACT.Copy).then_inc(evac_a, 1)

                act.wait_ge(h_ready, 3 + l)
                block_loop(HOP1 + l, stage_h(slice(0, P)), evacuate)
                stage_pass(2 + l, xw_i)
            sqrt(stat2[:, :], stat[:, :], 6)
            act.wait_ge(h_ready, 5)
            stage_pass(4, src_i)

            def relu_hidden(m, s, pair):
                act.wait_ge(hidden, m + 1)
                act.wait_ge(multiplied, NB * GIN + m + 1)
                nc.scalar.activation(zT[s][:, :], bank[4 + s][:, 0:P], ACT.Relu, bias=b1c[:, :]).then_inc(hidden_c, 1)

            block_loop(GIN, late=relu_hidden)
            sqrt(sd[:, :], var[:, :], 7)
            sqrt(stat2[:, :], stat[:, :], 8)
            act.wait_ge(h_ready, 6)
            block_loop(PROJ, stage_h(slice(0, P)))
            act.wait_ge(soft_in, 1)
            nc.scalar.activation(n5[0], n5[0], ACT.Exp).then_inc(soft_exp, 1)

            def stage_16(it, u):
                act.wait_ge(logits_done, it + 1)
                nc.scalar.activation(stage16[u][:, :], src_i[:, bass.ds(it * L16, L16)], ACT.Copy).then_inc(idx16, 1)

            stage_16(0, 0)
            act.wait_ge(zeros_done, 1)
            with act.Fori(0, ITERS // 2) as i2:
                for u in range(2):
                    it = i2 * 2 + u
                    stage_16(it + 1, 1 - u)
                    for g in range(4):
                        one_hot_rows(1, it, g, [oht_l3[:, g, h, :] for h in range(2)], q_looked, it * 4 + g + 1)
                    act.wait_ge(soft_in, it + 2)
                    nc.scalar.activation(y5, z5, ACT.Exp).then_inc(soft_exp, 1)

            with if_rest(act):
                with act.Fori(0, GROUPS) as k:
                    act.wait_ge(rest_soft, k + 1)
                    nc.scalar.activation(y5[:, 0:GT, :], z5[:, 0:GT, :], ACT.Exp).then_inc(rest_exp, 1)
            act.wait_ge(u_ready, 1)
            block_loop(ANCHOR, lambda b, s: nc.scalar.activation(in_st[s][:, 0:32], U[:, bass.ds(b * 32, 32)], ACT.Copy))

        @block.tensor
        def _(pe):
            pe.sem_inc(transposed, 2)
            pe.sem_inc(multiplied, 2)
            pe.sem_inc(windows_summed, CREDIT)
            pe.sem_inc(looked_up, 2)
            pe.sem_inc(q_looked, 4)
            pe.sem_inc(scattered, 4)

            pe.wait_ge(ident_done, 2)
            pe.wait_ge(edges_f, 3)
            for c in range(6):
                if c >= 2:
                    pe.wait_ge(edges_c, c - 1)
                chunks = range(4) if c % 2 == 0 else range(4, CHUNKS)
                for n, ch in enumerate(chunks):
                    last = nc.tensor.transpose(bank[c % 2][:, n * P:(n + 1) * P],
                                               raw_f[c // 2][:, ch * P:(ch + 1) * P], ident[:, :])
                last.then_inc(edges_t, 1)
            pe.wait_ge(ranges_d, 14)
            for i in range(2):
                for c in range(CHUNKS):
                    last = nc.tensor.matmul(bank[4 + 2 * i + c // 4][:, (c % 4) * P:(c % 4 + 1) * P], ones[:, :],
                                            diag[:, i * CHUNKS + c, :], start=True, stop=True)
            last.then_inc(ranges_b, 1)
            pe.wait_ge(weights_in, 16 * WEIGHT_LOADS)
            for i in range(4):
                nc.tensor.transpose(bank[2][:, i * P:(i + 1) * P], w_raw[:, i, :], ident[:, :])
            nc.tensor.transpose(bank[3][:, 0:P], w_raw[:, 4, :], ident[:, :]).then_inc(w_t, 1)

            def sum_pass(q, cols, more=None):
                with pe.Fori(0, ITERS) as it:
                    at = [pe.value_load(blk_i[0:1, bass.ds(it * 4 + g, 1)], min_val=0, max_val=NB - 2)
                          for g in range(4)] if more else None
                    for g in range(4):
                        k = it * 4 + g
                        pe.wait_ge(windows_ready, LOOK * q + k + 1)
                        pe.wait_ge(gathered[g], 64 * (ITERS * q + it + 1))
                        pe.wait_ge(sums_added, LOOK * q + k + 1)
                        for h in range(2):
                            for j in range(GT):
                                last = nc.tensor.matmul(bank[g % 2][:, h * AW:h * AW + cols],
                                                        S3[g % 2][:, j, h * P:(h + 1) * P], G3[g][:, j, 0:cols],
                                                        start=(j == 0), stop=(j == GT - 1))
                        last.then_inc(windows_summed, 1)
                        if more:
                            more(k, g, at[g])

            def rest_pass(z, cols):
                with if_rest(pe):
                    with pe.Fori(0, GROUPS) as k:
                        pe.wait_ge(rest_gathered[z], 16 * GT * (k + 1))
                        pe.sem_inc(pe_turn, 1)
                        with pe.Fori(0, WINDOWS) as w:
                            pe.wait_ge(rest_windows, (k + rest_sums_before(z) * GROUPS) * WINDOWS + w + 1)
                            for h in range(2):
                                for j in range(GT):
                                    last = nc.tensor.matmul(bank[0][:, h * AW:h * AW + cols], S3[0][:, j, h * P:(h + 1) * P],
                                                            G3[0][:, j, 0:cols], start=(j == 0), stop=(j == GT - 1))
                            last.then_inc(rest_summed, 1)

            def look_up_counts(k, g, at):
                pe.wait_ge(oht_ready, k + 1)
                pe.wait_ge(wt_done, k + 1)
                for j in range(GT):
                    for h in range(2):
                        last = nc.tensor.matmul(bank[4 + g % 2][:, j * R:(j + 1) * R],
                                                oht[g % 2][h][:, j * P:(j + 1) * P],
                                                inv_cnt[:, bass.ds(at * R + h * R, R)], start=(h == 0), stop=(h == 1))
                last.then_inc(looked_up, 1)

            def block_loop(i, products):
                w = width_in(i)

                def body(b, s, pair):
                    n = NB * i + b
                    if i in BY_DVE:
                        pe.wait_ge(staged_d, staged_d_before(i) + b + 1)
                    if i in BY_ACT:
                        pe.wait_ge(staged_a, staged_a_before(i) + b + 1)
                    pe.wait_ge(t_copied, n + 1)
                    if i in (HOP1, HOP2):
                        pe.wait_ge(evac_d, n + 1)
                    if w == 2 * P:
                        nc.tensor.transpose(bank[6 + s][:, 0:P], in_st[s][:, 0:P], ident[:, :])
                        last = nc.tensor.transpose(bank[6 + s][:, P:2 * P], in_st[s][:, P:2 * P], ident[:, :])
                    else:
                        last = nc.tensor.transpose(bank[6 + s][0:w, 0:P], in_st[s][:, 0:w], ident[:, :])
                    last.then_inc(transposed, 1)
                    if not (isinstance(b, int) and b == 0):
                        product(b - 1, 1 - s)

                def product(m, s):
                    pe.wait_ge(t_copied, NB * i + m + 3)
                    pe.wait_ge(evac_d, NB * i + m + 1)
                    products(m, s).then_inc(multiplied, 1)

                in_pairs(pe, body)
                product(NB - 1, 1)

            def sage(wl, wr):
                def products(m, s):
                    nc.tensor.matmul(bank[2 + s][:, 0:P], tT[s][:, 0:P], WT[:, wl * P:(wl + 1) * P], start=True, stop=False)
                    return nc.tensor.matmul(bank[2 + s][:, 0:P], tT[s][:, P:2 * P], WT[:, wr * P:(wr + 1) * P], start=False, stop=True)
                return products

            def hop(l):
                def products(m, s):
                    if not (isinstance(m, int) and m < 2):
                        pe.wait_ge(evac_a, NB * l + m - 1)
                    nc.tensor.matmul(bank[2 + 2 * s][:, :], tT[s][:, 0:P], Wcat[l][:, 0:4 * P], start=True, stop=True)
                    nc.tensor.matmul(bank[3 + 2 * s][:, :], tT[s][:, 0:P], Wcat[l][:, 4 * P:8 * P], start=True, stop=True)
                    return nc.tensor.matmul(bank[6 + s][:, 2 * P:3 * P], tT[s][:, 0:P], Wcat[l][:, 8 * P:9 * P], start=True, stop=True)
                return products

            def gin(m, s):
                nc.tensor.matmul(bank[4 + s][:, 0:P], W1s[:, :], tT[s][:, 0:P], start=True, stop=True).then_inc(hidden, 1)
                pe.wait_ge(hidden_c, m + 1)
                return nc.tensor.matmul(bank[2 + s][:, 0:P], zT[s][:, :], W2s[:, :], start=True, stop=True)

            def node_sums(v):
                pe.wait_ge(to_sum, v)
                nc.tensor.matmul(bank[4][:, 0:P], ones[:, :], part[:, :], start=True, stop=True).then_inc(summed, 1)

            pe.wait_ge(prep_done, 1)
            sum_pass(0, AW)
            rest_pass(REST_SAGE1, AW)
            block_loop(SAGE1, sage(0, 1))
            node_sums(1)
            node_sums(2)
            sum_pass(1, P, look_up_counts)
            rest_pass(REST_SAGE2, P)
            block_loop(SAGE2, sage(2, 3))
            for l in range(2):
                block_loop(HOP1 + l, hop(l))
                sum_pass(2 + l, P)
                rest_pass(REST_HOP1 + l, P)
            sum_pass(4, P)
            rest_pass(REST_GIN, P)
            block_loop(GIN, gin)
            node_sums(3)
            node_sums(4)
            block_loop(PROJ, lambda m, s: nc.tensor.matmul(bank[2 + s][:, 0:15], tT[s][:, 0:P], PRJ[:, 0:15], start=True, stop=True))

            pe.wait_ge(zeros_done, 1)
            nc.tensor.matmul(bank[2][:, 0:245], ident[:, :], zeros[:, 0:245], start=True, stop=False, skip_group_check=True)
            with pe.Fori(0, ITERS) as it:
                at = [pe.value_load(blk_i[0:1, bass.ds(it * 4 + g, 1)], min_val=0, max_val=NB - 2) for g in range(4)]
                pe.wait_ge(logits_done, it + 2)
                for g in range(4):
                    pe.wait_ge(oht_ready, GROUPS + it * 4 + g + 1)
                    for j in range(GT):
                        for h in range(2):
                            last = nc.tensor.matmul(bank[4][:, (g * GT + j) * A5:(g * GT + j + 1) * A5],
                                                    oht_l3[:, g, h, j * P:(j + 1) * P],
                                                    Q[:, bass.ds(at[g] * A5 + h * A5, A5)], start=(h == 0), stop=(h == 1))
                    last.then_inc(q_looked, 1)
                for g in range(4):
                    n = it * 4 + g
                    pe.wait_ge(ready5, n + 1)
                    pe.wait_ge(added5, n + 1)
                    for h in range(2):
                        for j in range(GT):
                            nc.tensor.matmul(bank[g % 2][:, h * A5:(h + 1) * A5], S_l3[:, g * GT + j, h * P:(h + 1) * P],
                                             b5[:, g * GT + j, :], start=(j == 0), stop=(j == GT - 1))
                    for j in range(GT):
                        last = nc.tensor.matmul(bank[2][:, 0:245], lo_l3[:, g * GT + j, :], M_l3[:, g * GT + j, :],
                                                start=False, stop=False, skip_group_check=True)
                    last.then_inc(scattered, 1)
            with if_rest(pe):
                with pe.Fori(0, GROUPS) as k:
                    pe.wait_ge(rest_ready5, k + 1)
                    for j in range(GT):
                        nc.tensor.matmul(bank[2][:, 0:245], lo_l3[:, j, :], M_l3[:, j, :], start=False, stop=False, skip_group_check=True)
                    with pe.Fori(0, WINDOWS) as w:
                        pe.wait_ge(rest_windows, (k + rest_sums_before(REST_L3) * GROUPS) * WINDOWS + w + 1)
                        for h in range(2):
                            for j in range(GT):
                                last = nc.tensor.matmul(bank[0][:, h * A5:(h + 1) * A5], S_l3[:, j, h * P:(h + 1) * P],
                                                        b5[:, j, :], start=(j == 0), stop=(j == GT - 1))
                        last.then_inc(rest_summed, 1)
            nc.tensor.matmul(bank[2][:, 0:245], ident[:, :], zeros[:, 0:245], start=False, stop=True, skip_group_check=True).then_inc(scat_all, 1)
            block_loop(ANCHOR, lambda m, s: nc.tensor.matmul(bank[2 + s][:, 0:P], tT[s][0:32, 0:P], anchors[:, :], start=True, stop=True))

        @block.vector
        def _(dve):
            V = nc.vector
            ch = Chain(dve, dve_done)
            over = lambda t, a, b: t.unsqueeze(2).broadcast_to([P, a, b])
            by_block = lambda t: over(t, NB, P)
            by_feat = lambda t: t.unsqueeze(1).broadcast_to([P, NB, P])
            roots = [0]
            sums = [0]

            def root(ins):
                roots[0] += 1
                ins.then_inc(to_root, 1)
                dve.wait_ge(rooted, roots[0])

            def node_sum(ins):
                sums[0] += 1
                ins.then_inc(to_sum, 1)
                dve.wait_ge(summed, sums[0])

            dve.sem_inc(sums_added, 1)
            dve.sem_inc(wt_done, 2)
            dve.sem_inc(evac_d, 2)
            dve.sem_inc(logits_done, 2)
            dve.sem_inc(added5, 2)
            V.memset(raw_i[0], PAD_NODE).then_inc(cleared, 1)
            V.memset(raw_i[1], PAD_NODE).then_inc(cleared, 1)
            V.memset(raw_i[2], 0).then_inc(cleared, 1)
            V.memset(X3[:, 48:NB, :], 0.0).then_inc(cleared, 1)
            V.memset(w_raw[:, 4, :], 0.0).then_inc(cleared, 1)
            V.memset(anchors[:, :], 0.0).then_inc(cleared, 1)
            ch(V.memset(wt[:, :], 0.0))
            V.memset(ones[:, :], 1.0).then_inc(ident_done, 1)
            dve.wait_ge(consts, 2)
            V.tensor_scalar(ident[:, :], iota[:, 0:P], iota_p[:, :], None, ALU.is_equal).then_inc(ident_done, 1)
            ch(V.tensor_scalar(row_mask[:, :], iota_p[:, :], float(LAST), None, ALU.is_lt))

            dve.wait_ge(edges_in, 9 * 16)
            for a in range(3):
                V.tensor_copy(raw_f[a], raw_i[a]).then_inc(edges_f, 1)
            ch(V.tensor_scalar(blk_t, raw_i[1], 7, None, ALU.logical_shift_right))
            ch(V.tensor_copy(blk_f, blk_t))
            blk3 = blk_f.rearrange("t (c p) -> t c p", p=P)
            ch(V.tensor_reduce(tile_lo[:, 0:CHUNKS], blk3, AX.X, ALU.min))
            ch(V.tensor_reduce(tile_hi[:, 0:CHUNKS], blk3, AX.X, ALU.max))
            dve.wait_ge(ident_done, 2)
            for i, t in enumerate((tile_lo, tile_hi)):
                for c in range(CHUNKS):
                    V.tensor_scalar(diag[:, i * CHUNKS + c, :], ident[:, :], t[:, c:c + 1], None, ALU.mult).then_inc(ranges_d, 1)
            dve.wait_ge(ranges_b, 1)
            for i, (to, op) in enumerate(((lo_g, ALU.min), (hi_g, ALU.max))):
                for half, cols in enumerate((4 * P, 3 * P)):
                    ch(V.tensor_reduce(to[:, half * P:half * P + cols // GT],
                                       bank[4 + 2 * i + half][:, 0:cols].rearrange("p (g j) -> p g j", j=GT), AX.X, op))
            ch(V.tensor_copy(blk_i[:, :], lo_g[:, 0:GROUPS]))
            NG = COLS // GT
            dve.wait_ge(edges_c, 6)
            grouped = lambda t: t.rearrange("p (g j) -> p g j", j=GT)
            ch(V.scalar_tensor_tensor(grouped(dl[:, :]), over(lo_g[:, :], NG, GT), -float(P), grouped(dst_f), ALU.mult, ALU.add))
            ch(V.tensor_copy(src_i[:, :], src_f))
            ch(V.scalar_tensor_tensor(tmp_f, et_f[:, :], float(NPAD), src_f, ALU.mult, ALU.add))
            ch(V.tensor_copy(xw_i[:, :], tmp_f))
            ch(V.tensor_scalar(tmp_i, src_i[:, :], 7, None, ALU.logical_shift_right))
            ch(V.tensor_copy(src_hi[:, :], tmp_i))
            ch(V.scalar_tensor_tensor(src_lo[:, :], src_hi[:, :], -float(P), src_f, ALU.mult, ALU.add))
            ch(V.tensor_scalar(tmp_f, dl[:, :], 2.0 * P, None, ALU.is_lt))
            ch(V.scalar_tensor_tensor(src_lo[:, :], src_lo[:, :], 1.0, tmp_f, ALU.add, ALU.mult))
            ch(V.tensor_scalar(src_lo[:, :], src_lo[:, :], 1.0, None, ALU.subtract))
            for h in range(2):
                ch(V.tensor_scalar(neg_row[h][:, :], lo_g[:, 0:GROUPS], -float(P), iota_p[:, :], ALU.mult, ALU.subtract))
                if h:
                    ch(V.tensor_scalar(neg_row[h][:, :], neg_row[h][:, :], float(P), None, ALU.subtract))
            ch(V.tensor_tensor(tmp_f[:, 0:GROUPS], hi_g[:, 0:GROUPS], lo_g[:, 0:GROUPS], ALU.subtract))
            ch(V.reduce_max(rest_f[:, :], tmp_f[:, 0:GROUPS], AX.X))
            ch(V.tensor_scalar(rest_f[:, :], rest_f[:, :], 2.0, None, ALU.is_ge))
            ch(V.tensor_copy(rest_i[:, :], rest_f[:, :]))
            dve.wait_ge(weights_in, 16 * WEIGHT_LOADS)
            for l in range(2):
                for n in range(4):
                    for r in range(R + 1):
                        w = Wcat[l][:, r * P:(r + 1) * P]
                        c = comp_b[:, (l * (R + 1) + r) * 4 + n:(l * (R + 1) + r) * 4 + n + 1]
                        if n == 0:
                            ch(V.tensor_scalar(w, base_s[:, l, n, :], c, None, ALU.mult))
                        else:
                            ch(V.scalar_tensor_tensor(w, base_s[:, l, n, :], c, w, ALU.mult, ALU.add))
                w = Wcat[l][:, R * P:(R + 1) * P]
                ch(V.tensor_tensor(w, w, root_s[:, l, :], ALU.add))
            dve.wait_ge(w_c, 2)
            dve.wait_ge(dst_out, 16)
            V.memset(stat[:, :], 0.0).then_inc(prep_done, 1)
            dve.wait_ge(prep_done, 1)

            def layer_norm():
                ch(V.reduce_sum(stat[:, :], X3, AX.X))
                ch(V.tensor_scalar(stat[:, :], stat[:, :], 1.0 / NCHANNELS, None, ALU.mult))
                ch(V.tensor_tensor(T3, X3, by_block(stat[:, :]), ALU.subtract))
                ch(V.tensor_tensor(H3, T3, T3, ALU.mult))
                ch(V.reduce_sum(stat[:, :], H3, AX.X))
                root(V.tensor_scalar(stat[:, :], stat[:, :], 1.0 / NCHANNELS, EPS, ALU.mult, ALU.add))
                ch(V.reciprocal(stat2[:, :], stat2[:, :]))
                V.scalar_tensor_tensor(H3, T3, 0.0, by_block(stat2[:, :]), ALU.max, ALU.mult).then_inc(h_ready, 1)

            def batch_norm(gamma, beta):
                def mask(t3):
                    ch(V.tensor_scalar(t3[:, 48, :], t3[:, 48, :], row_mask[:, :], None, ALU.mult))
                    ch(V.memset(t3[:, 49, :], 0.0))
                mask(O3)
                node_sum(V.reduce_sum(part[:, :], by_feature(O), AX.X))
                ch(V.tensor_scalar(mu[:, :], bank[4][:, 0:P], 1.0 / N, None, ALU.mult))
                ch(V.tensor_tensor(T3, O3, by_feat(mu[:, :]), ALU.subtract))
                mask(T3)
                ch(V.tensor_tensor(H3, T3, T3, ALU.mult))
                node_sum(V.reduce_sum(part[:, :], by_feature(H), AX.X))
                root(V.tensor_scalar(var[:, :], bank[4][:, 0:P], 1.0 / N, EPS, ALU.mult, ALU.add))
                ch(V.reciprocal(sd[:, :], sd[:, :]))
                ch(V.tensor_tensor(sd[:, :], sd[:, :], gamma, ALU.mult))
                ch(V.tensor_tensor(T3, T3, by_feat(sd[:, :]), ALU.mult))
                return T3, by_feat(beta)

            def sum_pass(q, weights=None, more=None):
                cols = AW if q == 0 else P

                def windows(k, gslot, s):
                    relation = over(et_f[:, bass.ds(k * GT, GT)], GT, R)
                    if q == 0:
                        V.tensor_tensor(G3[gslot][:, :, P:AW], iota[:, 0:R].unsqueeze(1).broadcast_to([P, GT, R]), relation, ALU.is_equal)
                    if q == 1:
                        V.tensor_tensor(ohe[s], iota[:, 0:R].unsqueeze(1).broadcast_to([P, GT, R]), relation, ALU.is_equal)
                    for j in range(GT):
                        row = dl[:, bass.ds(k * GT + j, 1)]
                        if weights is None:
                            last = V.tensor_scalar(S3[s][:, j, :], iota[:, :], row, None, ALU.is_equal)
                        else:
                            last = V.tensor_scalar(S3[s][:, j, :], iota[:, :], row, weights[:, bass.ds(k * GT + j, 1)], ALU.is_equal, ALU.mult)
                    last.then_inc(windows_ready, 1)

                V.memset(A[:, :], 0.0).then_inc(sums_added, 1)
                windows(0, 0, 0)
                with dve.Fori(0, ITERS) as it:
                    at = [dve.value_load(blk_i[0:1, bass.ds(it * 4 + g, 1)], min_val=0, max_val=NB - 2) for g in range(4)]
                    for g in range(4):
                        k = it * 4 + g
                        windows(k + 1, (g + 1) % 4, (g + 1) % 2)
                        dve.wait_ge(windows_summed, GROUPS * q + k + 1 + CREDIT)
                        dve.wait_ge(sums_added, LOOK * q + k + 2)
                        to = A[:, bass.ds(at[g] * AW, 2 * AW)].rearrange("p (h f) -> p h f", f=AW)[:, :, 0:cols]
                        V.tensor_tensor(to, to, bank[g % 2][:, 0:2 * AW].rearrange("p (h f) -> p h f", f=AW)[:, :, 0:cols],
                                        ALU.add).then_inc(sums_added, 1)
                        if more:
                            more(k, g)
                dve.wait_ge(sums_added, LOOK * (q + 1) + 1)

            class Steps:
                def __init__(self, sem, k, steps):
                    self.sem, self.at, self.n, self.steps = sem, k * steps, 0, steps

                def __call__(self, ins):
                    self.n += 1
                    assert self.n <= self.steps
                    ins.then_inc(self.sem, 1)
                    dve.wait_ge(self.sem, self.at + self.n)

            def take_rest(then, k):
                dl4 = dl[:, bass.ds(k * GT, GT)]
                then(V.tensor_scalar(outside[:, :], dl4, 2.0 * P, None, ALU.is_ge))
                then(V.tensor_scalar(rest_base[:, :], lo_g[:, bass.ds(k, 1)], float(P), 1.0, ALU.mult, ALU.add))
                then(V.scalar_tensor_tensor(rest4[:, :], dl4, rest_base[:, :], outside[:, :], ALU.add, ALU.mult))
                then(V.tensor_scalar(rest4[:, :], rest4[:, :], 1.0, None, ALU.subtract))

            def rest_window(z, k, w, to, sums, weights=None, columns=None):
                n = (k + rest_sums_before(z) * GROUPS) * WINDOWS + w + 1
                for j in range(GT):
                    if weights is None:
                        last = V.tensor_scalar(columns[:, j, :], iota[:, :], rest4[:, j:j + 1], None, ALU.is_equal)
                    else:
                        last = V.tensor_scalar(columns[:, j, :], iota[:, :], rest4[:, j:j + 1],
                                               weights[:, bass.ds(k * GT + j, 1)], ALU.is_equal, ALU.mult)
                last.then_inc(rest_windows, 1)
                dve.wait_ge(rest_summed, n)
                V.tensor_tensor(to, to, sums, ALU.add).then_inc(rest_added, 1)
                dve.wait_ge(rest_added, n)
                V.tensor_scalar(rest4[:, :], rest4[:, :], 2.0 * P, None, ALU.subtract).then_inc(rest_shift, 1)
                dve.wait_ge(rest_shift, n)

            def rest_pass(z, idx, cols, weights=None):
                with if_rest(dve):
                    with dve.Fori(0, GROUPS) as k:
                        then = Steps(rest_step[z], k, 5)
                        V.tensor_copy(stage[0][:, :], idx[:, bass.ds(k * GT, GT)]).then_inc(rest_staged, 1)
                        take_rest(then, k)
                        if cols == AW:
                            then(V.tensor_tensor(G3[0][:, :, P:AW], iota[:, 0:R].unsqueeze(1).broadcast_to([P, GT, R]),
                                                 over(et_f[:, bass.ds(k * GT, GT)], GT, R), ALU.is_equal))
                        else:
                            then(V.tensor_copy(rest_w[:, :], rest4[:, :]))
                        dve.sem_inc(dve_turn, 1)
                        with dve.Fori(0, WINDOWS) as w:
                            pair = lambda t: t.rearrange("p (h f) -> p h f", f=AW)[:, :, 0:cols]
                            rest_window(z, k, w, pair(A[:, bass.ds(w * 2 * AW, 2 * AW)]), pair(bank[0][:, 0:2 * AW]), weights, S3[0])

            def rest_weights():
                with if_rest(dve):
                    V.memset(rest_w[:, :], 0.0).then_inc(rest_table, 1)
                    dve.wait_ge(rest_table, 1)
                    with dve.Fori(0, GROUPS) as k:
                        then = Steps(rest_step[REST_WT], k, 10)
                        take_rest(then, k)
                        then(V.tensor_scalar(rest4[:, :], rest4[:, :], 0.0, None, ALU.max))
                        V.tensor_copy(stage[0][:, :], rest4[:, :]).then_inc(rest_staged, 1)
                        then(V.tensor_tensor(ohe[0], iota[:, 0:R].unsqueeze(1).broadcast_to([P, GT, R]),
                                             over(et_f[:, bass.ds(k * GT, GT)], GT, R), ALU.is_equal))
                        dve.wait_ge(rest_gathered[REST_WT], 16 * GT * (k + 1))
                        then(V.tensor_tensor(wsel[0], G3[0][:, :, 0:R], ohe[0], ALU.mult))
                        then(V.reduce_sum(rest_w[:, :], wsel[0], AX.X))
                        then(V.tensor_tensor(rest_w[:, :], rest_w[:, :], outside[:, :], ALU.mult))
                        w4 = wt[:, bass.ds(k * GT, GT)]
                        then(V.tensor_tensor(w4, w4, rest_w[:, :], ALU.add))

            def rest_attention():
                with if_rest(dve):
                    V.memset(rest_w[:, :], 0.0).then_inc(rest_table, 1)
                    dve.wait_ge(rest_table, 2)
                    with dve.Fori(0, GROUPS) as k:
                        then = Steps(rest_step[REST_L3], k, 17)
                        V.tensor_copy(stage[0][:, :], src_i[:, bass.ds(k * GT, GT)]).then_inc(rest_staged, 1)
                        take_rest(then, k)
                        then(V.tensor_scalar(rest_w[:, :], rest4[:, :], 0.0, None, ALU.max))
                        V.tensor_copy(stage[1][:, :], rest_w[:, :]).then_inc(rest_staged, 1)
                        z4, y4, b4, m4, r4 = z5[:, 0:GT, :], y5[:, 0:GT, :], b5[:, 0:GT, :], m5[:, 0:GT], r5[:, 0:GT]
                        dve.wait_ge(rest_gathered[REST_L3], 32 * GT * (k + 1))
                        then(V.tensor_tensor(z4, G3[0][:, :, 0:A5], G3[1][:, :, 0:A5], ALU.add))
                        then(V.tensor_tensor(z4, z4, ab[:, A5:].unsqueeze(1).broadcast_to([P, GT, A5]), ALU.add))
                        then(V.scalar_tensor_tensor(z4, z4, 0.01, z4, ALU.mult, ALU.max))
                        then(V.reduce_max(m4, z4, AX.X))
                        V.tensor_tensor(z4, z4, over(m4, GT, A5), ALU.subtract).then_inc(rest_soft, 1)
                        dve.wait_ge(rest_exp, k + 1)
                        then(V.reduce_sum(r4, y4, AX.X))
                        then(V.reciprocal(r4, r4))
                        then(V.tensor_tensor(b4, y4, over(r4, GT, A5), ALU.mult))
                        hi4 = src_hi[:, bass.ds(k * GT, GT)]
                        then(V.tensor_scalar(rest_w[:, :], hi4, -float(P), 1.0, ALU.mult, ALU.add))
                        then(V.tensor_tensor(rest_w[:, :], rest_w[:, :], src_i[:, bass.ds(k * GT, GT)], ALU.add))
                        then(V.tensor_tensor(rest_w[:, :], rest_w[:, :], outside[:, :], ALU.mult))
                        then(V.tensor_scalar(rest_w[:, :], rest_w[:, :], 1.0, None, ALU.subtract))
                        then(V.tensor_tensor(hi_l3[:, 0:GT, :], iota[:, 0:49].unsqueeze(1).broadcast_to([P, GT, 49]), over(hi4, GT, 49), ALU.is_equal))
                        for j in range(GT):
                            V.tensor_scalar(lo_l3[:, j, :], iota[:, 0:P], rest_w[:, j:j + 1], None, ALU.is_equal)
                            last = V.tensor_tensor(M_l3[:, j, :].rearrange("p (d a) -> p d a", a=A5), over(hi_l3[:, j, :], 49, A5),
                                                   b5[:, j, :].unsqueeze(1).broadcast_to([P, 49, A5]), ALU.mult)
                        last.then_inc(rest_ready5, 1)
                        with dve.Fori(0, WINDOWS) as w:
                            rest_window(REST_L3, k, w, A[:, bass.ds(w * 2 * A5 + 4900, 2 * A5)], bank[0][:, 0:2 * A5], None, S_l3)

            def pick_weights(k, g):
                dve.wait_ge(looked_up, k + 3)
                V.tensor_tensor(wsel[g % 2], bank[4 + g % 2][:, 0:GT * R].rearrange("p (j r) -> p j r", r=R),
                                ohe[g % 2], ALU.mult).then_inc(wt_picked, 1)
                dve.wait_ge(wt_picked, k + 1)
                V.reduce_sum(wt[:, bass.ds(k * GT, GT)], wsel[g % 2], AX.X).then_inc(wt_done, 1)

            def block_loop(i, evacuate, stage_block=None):
                def body(b, s, pair):
                    if stage_block:
                        dve.wait_ge(transposed, NB * i + b + 1)
                        stage_block(b, s).then_inc(staged_d, 1)
                    if not (isinstance(b, int) and b == 0):
                        out_of_psum(b - 1, 1 - s, pair - 1 + s)

                def out_of_psum(m, s, pair):
                    dve.wait_ge(multiplied, NB * i + m + 3)
                    evacuate(m, s, pair).then_inc(evac_d, 1)

                in_pairs(dve, body)
                out_of_psum(NB - 1, 1, NB // 2 - 1)
                dve.wait_ge(evac_d, NB * (i + 1) + 2)

            def at_block(t, b):
                return t[:, bass.ds(b * P, P)]

            def sage(i, bias):
                block_loop(
                    i, lambda m, s, pair: V.tensor_tensor(at_block(O, m), bank[2 + s][:, 0:P], bias, ALU.add),
                    lambda b, s: V.tensor_scalar(in_st[s][:, 0:P], A[:, bass.ds(b * AW, P)], inv_deg[:, bass.ds(b, 1)], None, ALU.mult))
                ch(V.tensor_tensor(T3, O3, O3, ALU.mult))
                root(V.reduce_sum(stat[:, :], T3, AX.X))
                ch(V.tensor_scalar(stat2[:, :], stat2[:, :], L2_EPS, None, ALU.max))
                ch(V.reciprocal(stat2[:, :], stat2[:, :]))

            dve.wait_ge(x_in, 32)
            layer_norm()
            dve.wait_ge(h_ready, 1)
            sum_pass(0)
            rest_pass(REST_SAGE1, src_i, AW)
            cnt3 = A3[:, :, P:AW]
            inv3 = inv_cnt[:, :].rearrange("p (b r) -> p b r", r=R)
            ch(V.reduce_sum(inv_deg[:, :], cnt3, AX.X))
            ch(V.tensor_scalar(inv_deg[:, :], inv_deg[:, :], 1.0, None, ALU.max))
            ch(V.reciprocal(inv_deg[:, :], inv_deg[:, :]))
            ch(V.tensor_scalar(inv3, cnt3, 1.0, None, ALU.max))
            ch(V.reciprocal(inv_cnt[:, :], inv_cnt[:, :]))
            sage(SAGE1, BL1)
            ch(V.scalar_tensor_tensor(O3, O3, 0.0, by_block(stat2[:, :]), ALU.max, ALU.mult))
            normed, beta = batch_norm(GA0, BE0)
            V.tensor_tensor(H3, normed, beta, ALU.add).then_inc(h_ready, 1)
            dve.wait_ge(h_ready, 2)
            sum_pass(1, more=pick_weights)
            dve.wait_ge(wt_done, GROUPS + 2)
            rest_pass(REST_SAGE2, src_i, P)
            rest_weights()
            sage(SAGE2, BL2)
            ch(V.tensor_tensor(T3, O3, by_block(stat2[:, :]), ALU.mult))
            ch(V.tensor_tensor(X3, X3, T3, ALU.add))
            layer_norm()
            for l in range(2):
                def evacuate(m, s, pair):
                    if not (l == 0 and isinstance(pair, int) and pair == 0):
                        dve.wait_ge(xw_stored[s], 16 * ((NB // 2) * l + pair))
                    V.tensor_copy(xw_out[s][:, 0:4 * P], bank[2 + 2 * s][:, :])
                    return V.tensor_tensor(at_block(O, m), bank[6 + s][:, 2 * P:3 * P], (B10, B11)[l], ALU.add)

                block_loop(HOP1 + l, evacuate)
                sum_pass(2 + l, weights=wt)
                rest_pass(REST_HOP1 + l, xw_i, P, wt)
                ch(V.tensor_tensor(T3, AF, O3, ALU.add))
                if l == 0:
                    ch(V.tensor_scalar(T3, T3, 0.0, 0.5, ALU.max, ALU.mult))
                    V.scalar_tensor_tensor(H3, H3, 0.5, T3, ALU.mult, ALU.add).then_inc(h_ready, 1)
                    dve.wait_ge(h_ready, 4)
                else:
                    ch(V.tensor_scalar(T3, T3, 0.5, None, ALU.mult))
                    ch(V.scalar_tensor_tensor(T3, H3, 0.5, T3, ALU.mult, ALU.add))
                    ch(V.tensor_tensor(X3, X3, T3, ALU.add))
            layer_norm()
            dve.wait_ge(h_ready, 5)
            sum_pass(4)
            rest_pass(REST_GIN, src_i, P)
            block_loop(GIN, lambda m, s, pair: V.tensor_tensor(at_block(O, m), bank[2 + s][:, 0:P], B2, ALU.add),
                       lambda b, s: V.tensor_tensor(in_st[s][:, 0:P], A[:, bass.ds(b * AW, P)], at_block(H, b), ALU.add))
            normed, beta = batch_norm(GA2, BE2)
            ch(V.tensor_tensor(T3, normed, beta, ALU.add))
            ch(V.tensor_tensor(X3, X3, T3, ALU.add))
            layer_norm()
            dve.wait_ge(h_ready, 6)
            block_loop(PROJ, lambda m, s, pair: V.tensor_copy(T[:, bass.ds(m * 15 + 4096, 15)], bank[2 + s][:, 0:15]))
            ch(V.memset(PT, 0.0))
            V.tensor_copy(PT[:, :, 0:A5], PRo[:, :, A5:2 * A5]).then_inc(p_ready, 1)
            ch(V.tensor_copy(Q3, PRo[:, :, 2 * A5:3 * A5]))
            ch(V.memset(U[:, :], 0.0))
            ch(V.memset(sums5, 0.0))
            V.memset(zeros, 0.0).then_inc(zeros_done, 1)
            anchors_of = lambda t: t.unsqueeze(1).broadcast_to([P, NB, A5])
            ch(V.tensor_tensor(n5[0], PRo[:, :, 0:A5], anchors_of(ab[:, 0:A5]), ALU.add))
            ch(V.reduce_max(stat[:, :], n5[0], AX.X))
            V.tensor_tensor(n5[0], n5[0], over(stat[:, :], NB, A5), ALU.subtract).then_inc(soft_in, 1)
            dve.wait_ge(soft_exp, 1)
            ch(V.reduce_sum(stat[:, :], n5[0], AX.X))
            ch(V.reciprocal(stat2[:, :], stat[:, :]))
            ch(V.tensor_tensor(U3[:, :, 0:A5], n5[0], over(stat2[:, :], NB, A5), ALU.mult))
            STEPS = 6
            with dve.Fori(0, ITERS // 2) as i2:
                for u in range(2):
                    it = i2 * 2 + u
                    step = [0]

                    def then(ins):
                        step[0] += 1
                        ins.then_inc(soft_step, 1)
                        dve.wait_ge(soft_step, it * STEPS + step[0])

                    at = [dve.value_load(blk_i[0:1, bass.ds(it * 4 + g, 1)], min_val=0, max_val=NB - 2) for g in range(4)]
                    for g in range(4):
                        dve.wait_ge(scattered, it * 4 + g + 1)
                        for t in range(g * GT, (g + 1) * GT):
                            col = it * L16 + t
                            V.tensor_scalar(S_l3[:, t, :], iota[:, :], dl[:, bass.ds(col, 1)], None, ALU.is_equal)
                            V.tensor_scalar(lo_l3[:, t, :], iota[:, 0:P], src_lo[:, bass.ds(col, 1)], None, ALU.is_equal)
                    then(V.tensor_tensor(hi_l3, iota[:, 0:49].unsqueeze(1).broadcast_to([P, L16, 49]),
                                         over(src_hi[:, bass.ds(it * L16, L16)], L16, 49), ALU.is_equal))
                    dve.wait_ge(gathered16[u], 16 * L16 * (i2 + 1))
                    dve.wait_ge(q_looked, it * 4 + 4 + 4)
                    then(V.tensor_tensor(z5, bank[4][:, 0:L16 * A5].rearrange("p (j a) -> p j a", a=A5), p_rows[u][:, :, 0:A5], ALU.add))
                    V.tensor_tensor(z5, z5, ab[:, A5:].unsqueeze(1).broadcast_to([P, L16, A5]), ALU.add).then_inc(logits_done, 1)
                    dve.wait_ge(logits_done, it + 3)
                    then(V.scalar_tensor_tensor(z5, z5, 0.01, z5, ALU.mult, ALU.max))
                    then(V.reduce_max(m5, z5, AX.X))
                    V.tensor_tensor(z5, z5, over(m5, L16, A5), ALU.subtract).then_inc(soft_in, 1)
                    dve.wait_ge(soft_exp, it + 2)
                    then(V.reduce_sum(r5, y5, AX.X))
                    V.reciprocal(r5, r5).then_inc(soft_step, 1)
                    dve.wait_ge(soft_step, it * STEPS + STEPS)
                    V.tensor_tensor(b5, y5, over(r5, L16, A5), ALU.mult).then_inc(soft_mul, 1)
                    dve.wait_ge(soft_mul, it + 1)
                    for g in range(4):
                        for t in range(g * GT, (g + 1) * GT):
                            last = V.tensor_tensor(M_l3[:, t, :].rearrange("p (d a) -> p d a", a=A5),
                                                   over(hi_l3[:, t, :], 49, A5),
                                                   b5[:, t, :].unsqueeze(1).broadcast_to([P, 49, A5]), ALU.mult)
                        last.then_inc(ready5, 1)
                    for g in range(4):
                        n = it * 4 + g
                        dve.wait_ge(scattered, n + 1 + 4)
                        dve.wait_ge(added5, n + 2)
                        to = A[:, bass.ds(at[g] * A5 + 4900, 2 * A5)]
                        V.tensor_tensor(to, to, bank[g % 2][:, 0:2 * A5], ALU.add).then_inc(added5, 1)
            dve.wait_ge(added5, GROUPS + 2)
            rest_attention()
            dve.wait_ge(scat_all, 1)
            ch(V.tensor_tensor(n5[1][:, 0:49, :], bank[2][:, 0:245].rearrange("p (b a) -> p b a", a=A5),
                               sums5[:, 0:245].rearrange("p (b a) -> p b a", a=A5), ALU.add))
            V.tensor_scalar(U3[:, 0:49, A5:2 * A5], n5[1][:, 0:49, :], 0.5, None, ALU.mult).then_inc(u_ready, 1)
            block_loop(ANCHOR, lambda m, s, pair: V.tensor_tensor(at_block(X, m), at_block(X, m), bank[2 + s][:, 0:P], ALU.add))
            V.tensor_tensor(X3, X3, H3, ALU.add).then_inc(out_ready, 1)


_INS = ['x', 'src', 'dst', 'edge_type_8', 'L0_gnn_Wl1', 'L0_gnn_bl1', 'L0_gnn_Wr1', 'L0_gnn_gamma', 'L0_gnn_beta',
        'L0_gnn_Wl2', 'L0_gnn_bl2', 'L0_gnn_Wr2', 'L1_gnn_bases', 'L1_gnn_comp', 'L1_gnn_root', 'L1_gnn_bias',
        'L2_gnn_W1', 'L2_gnn_b1', 'L2_gnn_W2', 'L2_gnn_b2', 'L2_gnn_gamma', 'L2_gnn_beta', 'L3_gnn_node_anchor',
        'L3_gnn_attn_w', 'L3_gnn_attn_b', 'L3_gnn_edge_anchor', 'L3_gnn_edge_w', 'L3_gnn_edge_b']


def kernel(**inputs):
    import numpy as _np
    import concourse.bacc as _bacc
    from concourse import mybir as _mybir
    from concourse.bass_utils import run_bass_kernel_spmd as _run

    nc = _bacc.Bacc("TRN2", target_bir_lowering=False, num_devices=1)
    arrays, args = {}, []
    for name in _INS:
        a = _np.ascontiguousarray(inputs[name])
        arrays[f"in_{name}"] = a
        args.append(nc.dram_tensor(f"in_{name}", a.shape, _mybir.dt.from_np(a.dtype), kind="ExternalInput").ap())
    args.append(nc.dram_tensor("out_x", (N, P), FP, kind="ExternalOutput").ap())
    gnn_stack(nc, *args)
    r = _run(nc, [arrays], core_ids=[0])
    return r.results[0]["out_x"]
```

```python
import concourse.bass as bass
from concourse import mybir
from concourse.alu_op_type import AluOpType as ALU
from contextlib import ExitStack

FP = mybir.dt.float32
I32 = mybir.dt.int32
BF = mybir.dt.bfloat16
ACT = mybir.ActivationFunctionType
AX = mybir.AxisListType

P = 128
N = 6250
E = 106250
NB = 50
NPAD = NB * P
PAD_NODE = 49 * P - 1
TILES = 832
CHUNKS = 7
COLS = CHUNKS * P
GT = 4
GROUPS = TILES // GT
LOOK = GROUPS + 1
WINDOWS = NB // 2
ITERS = GROUPS // 4
R = 8
A5 = 5
PARTS = 3
B5 = PARTS * A5
DR = PARTS * R
D5 = 16
AW = P + R
NCHANNELS = float(P)
LAST = N - 48 * P
EPS = 1e-5
L2_EPS = 1e-12
CREDIT = 4
WEIGHT_LOADS = 27


def gnn_stack(nc, x, src, dst, edge_type, Wl1, bl1, Wr1, gamma0, beta0, Wl2, bl2, Wr2,
              bases, comp, root, bias1, W1, b1, W2, b2, gamma2, beta2,
              node_anchor, attn_w, attn_b, edge_anchor, edge_w, edge_b, out):
    ctx = ExitStack()
    with ctx:
        def sb(name, cols, dt=FP, parts=P):
            return ctx.enter_context(nc.sbuf_tensor(name, [parts, cols], dt))

        def sem(name):
            return ctx.enter_context(nc.semaphore(name))

        def dram(name, shape, dt=FP):
            return nc.dram_tensor(name, shape, dt, kind="Internal").ap()

        h_table = dram("h_table", [NPAD, P])
        xw_table = dram("xw_table", [R * NPAD, P])
        p_table = dram("p_table", [NPAD, R])
        cnt_table = dram("cnt_table", [NPAD, R])
        q_table = dram("q_table", [NPAD, A5])
        dst_rows = dram("dst_rows", [COLS * P], I32)

        X = sb("X", NB * P)
        H = sb("H", NB * P)
        O = sb("O", NB * P)
        T = sb("T", NB * P)
        A = sb("A", NB * AW)
        blocks = lambda t: t[:, 0:NB * P].rearrange("p (b f) -> p b f", f=P)
        by_feature = lambda t: t[:, 0:NB * P].rearrange("p (b f) -> p f b", f=P)
        X3, H3, O3, T3 = blocks(X), blocks(H), blocks(O), blocks(T)
        A3 = A[:, :].rearrange("p (b f) -> p b f", f=AW)
        AF = A3[:, :, 0:P]
        inv_deg = sb("inv_deg", NB)
        inv_cnt = sb("inv_cnt", NB * R)
        digits = sb("digits", NB * PARTS * R, BF)
        digits4 = digits[:, :].rearrange("p (b t r) -> p b t r", t=PARTS, r=R)

        src_i = sb("src_i", COLS, I32)
        xw_i = sb("xw_i", COLS, I32)
        et_f = sb("et_f", COLS)
        dl = sb("dl", COLS)
        wt = sb("wt", COLS)
        neg_lo = sb("neg_lo", COLS)
        src_hi = sb("src_hi", COLS)
        neg_row = [sb(f"neg_row{h}", GROUPS + 4) for h in range(2)]
        blk_i = sb("blk_i", GROUPS + 4, I32)
        lo_g = sb("lo_g", COLS // GT)
        hi_g = sb("hi_g", COLS // GT)

        rest_i = sb("rest_i", 1, I32)
        rest_f = sb("rest_f", 1)
        outside = sb("outside", GT)
        rest4 = sb("rest4", GT)
        rest_base = sb("rest_base", 1)
        rest_w = sb("rest_w", GT)

        stage = [sb(f"stage{g}", GT, I32) for g in range(4)]
        stage16 = [sb(f"stage16_{i}", 4 * GT, I32) for i in range(2)]
        G = [sb(f"G{g}", GT * AW) for g in range(4)]
        G3 = [t[:, :].rearrange("p (j f) -> p j f", f=AW) for t in G]
        S = sb("S", 2 * GT * 2 * P)
        S3 = [S[:, i * GT * 2 * P:(i + 1) * GT * 2 * P].rearrange("p (j d) -> p j d", d=2 * P) for i in range(2)]
        dst_b = [sb(f"dst_b{i}", GT * P, I32) for i in range(2)]

        iota = sb("iota", 2 * P)
        iota_p = sb("iota_p", 1)
        ident = sb("ident", P)
        ones = sb("ones", P)
        row_mask = sb("row_mask", 1)
        WT = sb("WT", 4 * P)
        PRJ = sb("PRJ", P)
        Wcat = [sb(f"Wcat{l}", (R + 1) * P) for l in range(2)]
        W1s, W2s = sb("W1s", P), sb("W2s", P)
        rows = sb("rows", 9 * P)
        BL1, GA0, BE0, BL2, B10, B11, B2, GA2, BE2 = (rows[:, i * P:(i + 1) * P] for i in range(9))
        b1c = sb("b1c", 1)
        comp_b = sb("comp_b", 2 * (R + 1) * 4)
        ab = sb("ab", 2 * A5)
        anchors = sb("anchors", P, FP, 32)
        in_st = [sb(f"in_st{i}", 2 * P) for i in range(2)]
        tT = [sb(f"tT{i}", 2 * P) for i in range(2)]
        zT = [dst_b[i][:, 0:P].bitcast(FP) for i in range(2)]
        stat = sb("stat", NB)
        stat2 = sb("stat2", NB)
        mu = sb("mu", P)
        var = sb("var", P)
        sd = sb("sd", P)
        part = sb("part", P)

        raw_i = [O[:, a * COLS:(a + 1) * COLS].bitcast(I32) for a in range(3)]
        raw3 = [r.rearrange("t (c p) -> t c p", p=P) for r in raw_i]
        raw_f = [O[:, (3 + a) * COLS:(4 + a) * COLS] for a in range(3)]
        blk_t = T[:, 0:COLS].bitcast(I32)
        blk_f = T[:, COLS:2 * COLS]
        tile_lo, tile_hi = T[:, 2 * COLS:2 * COLS + 8], T[:, 2 * COLS + 8:2 * COLS + 16]
        diag = T[:, 2 * COLS + P:2 * COLS + P + 14 * P].rearrange("p (c t) -> p c t", t=P)
        w_raw = T[:, 4800:4800 + 5 * P].rearrange("p (w f) -> p w f", f=P)
        base_s = A[:, 0:2 * 4 * P].rearrange("p (l n o) -> p l n o", l=2, n=4)
        root_s = A[:, 8 * P:10 * P].rearrange("p (l o) -> p l o", l=2)
        src_t = A[:, 1400:1400 + COLS].bitcast(I32)
        tmp_i = A[:, 1400 + COLS:1400 + 2 * COLS].bitcast(I32)
        src_f = A[:, 1400 + 2 * COLS:1400 + 3 * COLS]
        dst_f = A[:, 1400 + 3 * COLS:1400 + 4 * COLS]
        tmp_f = A[:, 1400 + 4 * COLS:1400 + 5 * COLS]
        xw_out = [T[:, i * R * P:(i + 1) * R * P] for i in range(2)]
        cnt_i, cnt_d = (T[:, i * NB * R:(i + 1) * NB * R].bitcast(I32) for i in range(2))
        oht = [[T[:, (2 * s + h) * GT * P // 2:(2 * s + h + 1) * GT * P // 2].bitcast(BF) for h in range(2)] for s in range(2)]
        ohe = [T[:, 4096 + s * GT * R:4096 + (s + 1) * GT * R].rearrange("p (j r) -> p j r", r=R) for s in range(2)]
        wsel = [T[:, 4224 + s * GT * PARTS * R:4224 + (s + 1) * GT * PARTS * R] for s in range(2)]
        rest_sel = wsel[0][:, 0:GT * R].rearrange("p (j r) -> p j r", r=R)
        L16 = 4 * GT
        S_l3 = T[:, 0:L16 * P].bitcast(BF).rearrange("p (j d) -> p j d", d=2 * P)
        PRo = T[:, 4096:4096 + NB * 15].rearrange("p (b a) -> p b a", a=15)
        PT = T[:, 4900:4900 + NB * R].rearrange("p (b a) -> p b a", a=R)
        U = S[:, 0:NB * 32]
        U3 = U[:, :].rearrange("p (b a) -> p b a", a=32)
        M_l3 = O[:, 0:L16 * 245].rearrange("p (j m) -> p j m", m=245)
        lo_l3 = [t.rearrange("p (j d) -> p j d", d=P) for t in (O[:, 3920:3920 + L16 * P], A[:, 2048:2048 + L16 * P])]
        oht_l3 = A[:, 0:2048].bitcast(BF).rearrange("p (g h e) -> p g h e", g=4, h=2)
        hi_l3 = A[:, 4096:4096 + L16 * 49].rearrange("p (j d) -> p j d", d=49)
        Qp = A[:, 4880:4880 + NB * B5 // 2].bitcast(BF)
        Qp3 = Qp.rearrange("p (b a) -> p b a", a=B5)
        Q = A[:, 5260:5260 + NB * A5]
        Q3 = Q.rearrange("p (b a) -> p b a", a=A5)
        of_tiles = lambda at, a: A[:, at:at + L16 * a].rearrange("p (j a) -> p j a", a=a)
        p_rows = [of_tiles(5520 + i * L16 * R, R) for i in range(2)]
        z5, y5, b5, d5 = (of_tiles(5800 + i * L16 * A5, A5) for i in range(4))
        m5 = A[:, 6120:6120 + L16]
        r5 = A[:, 6136:6136 + L16]
        b5p = A[:, 6152:6152 + L16 * B5 // 2].bitcast(BF).rearrange("p (j a) -> p j a", a=B5)
        n5 = [T[:, 5300 + i * NB * A5:5300 + (i + 1) * NB * A5].rearrange("p (b a) -> p b a", a=A5) for i in range(3)]
        zeros = Wcat[0][:, 0:4 * P]

        psum = ctx.enter_context(nc.psum_tensor("psum", [P, 8 * 512], FP))
        bank = [psum[:, i * 512:(i + 1) * 512] for i in range(8)]
        by_dst = psum[:, 0:2 * 512]

        consts = sem("consts")
        cleared = sem("cleared")
        x_in = sem("x_in")
        edges_in = sem("edges_in")
        weights_in = sem("weights_in")
        dst_out = sem("dst_out")
        edges_f = sem("edges_f")
        ident_done = sem("ident_done")
        edges_t = sem("edges_t")
        edges_c = sem("edges_c")
        ranges_d = sem("ranges_d")
        ranges_b = sem("ranges_b")
        w_t = sem("w_t")
        w_c = sem("w_c")
        prep_done = sem("prep_done")
        to_root = sem("to_root")
        rooted = sem("rooted")
        h_ready = sem("h_ready")
        table_in = sem("table_in")
        to_sum = sem("to_sum")
        summed = sem("summed")
        dve_done = sem("dve_done")
        idx_staged = sem("idx_staged")
        sp_turn = sem("sp_turn")
        pe_turn = sem("pe_turn")
        dve_turn = sem("dve_turn")
        pool_turn = sem("pool_turn")
        gathered = [sem(f"gathered{g}") for g in range(4)]
        windows_ready = sem("windows_ready")
        windows_summed = sem("windows_summed")
        sums_added = sem("sums_added")
        dst_in = [sem(f"dst_in{i}") for i in range(2)]
        oht_abs = sem("oht_abs")
        oht_ready = sem("oht_ready")
        looked_up = sem("looked_up")
        wt_picked = sem("wt_picked")
        wt_done = sem("wt_done")
        staged_d = sem("staged_d")
        staged_a = sem("staged_a")
        transposed = sem("transposed")
        t_copied = sem("t_copied")
        multiplied = sem("multiplied")
        evac_d = sem("evac_d")
        evac_a = sem("evac_a")
        hidden = sem("hidden")
        hidden_c = sem("hidden_c")
        xw_stored = [sem(f"xw_stored{i}") for i in range(2)]
        p_ready = sem("p_ready")
        idx16 = sem("idx16")
        gathered16 = [sem(f"gathered16_{u}") for u in range(2)]
        q_looked = sem("q_looked")
        logits_done = sem("logits_done")
        soft_step = sem("soft_step")
        soft_in = sem("soft_in")
        soft_exp = sem("soft_exp")
        soft_mul = sem("soft_mul")
        lo_abs = sem("lo_abs")
        lo_ready = sem("lo_ready")
        ready5 = sem("ready5")
        parts5 = sem("parts5")
        scattered = sem("scattered")
        scattered_d = sem("scattered_d")
        zeros_done = sem("zeros_done")
        scat_all = sem("scat_all")
        rest_table = sem("rest_table")
        rest_table_in = sem("rest_table_in")
        rest_staged = sem("rest_staged")
        rest_gathered = [sem(f"rest_gathered{z}") for z in range(7)]
        rest_step = [sem(f"rest_step{z}") for z in range(7)]
        rest_windows = sem("rest_windows")
        rest_summed = sem("rest_summed")
        rest_added = sem("rest_added")
        rest_shift = sem("rest_shift")
        rest_soft = sem("rest_soft")
        rest_exp = sem("rest_exp")
        rest_ready5 = sem("rest_ready5")
        u_ready = sem("u_ready")
        out_ready = sem("out_ready")
        stored = sem("stored")

        block = ctx.enter_context(nc.Block())

        SAGE1, SAGE2, HOP1, HOP2, GIN, PROJ, ANCHOR = range(7)
        BY_DVE, BY_ACT = (SAGE1, SAGE2, GIN), (SAGE1, SAGE2, HOP1, HOP2, PROJ, ANCHOR)
        staged_d_before = lambda i: NB * sum(l < i for l in BY_DVE)
        staged_a_before = lambda i: NB * sum(l < i for l in BY_ACT)

        def in_pairs(eng, body):
            for b in range(4):
                body(b, b % 2, b // 2)
            with eng.Fori(2, NB // 2 - 1) as it:
                body(it * 2, 0, it)
                body(it * 2 + 1, 1, it)
            for b in (NB - 2, NB - 1):
                body(b, b % 2, b // 2)

        def is_block(b, *these):
            return isinstance(b, int) and b in these

        class Chain:
            def __init__(self, eng, sem):
                self.eng, self.sem, self.n = eng, sem, 0

            def __call__(self, ins):
                self.n += 1
                ins.then_inc(self.sem, 1)
                self.eng.wait_ge(self.sem, self.n)

        def width_in(i):
            return {SAGE1: 2 * P, SAGE2: 2 * P, ANCHOR: 32}.get(i, P)

        REST_SAGE1, REST_SAGE2, REST_WT, REST_HOP1, REST_HOP2, REST_GIN, REST_L3 = range(7)
        rest_sums_before = lambda z: {REST_SAGE1: 0, REST_SAGE2: 1, REST_HOP1: 2, REST_HOP2: 3, REST_GIN: 4, REST_L3: 5}[z]

        def if_rest(eng):
            return eng.If(eng.value_load(rest_i[0:1, 0:1], min_val=0, max_val=1) > 0)

        @block.sync
        def _(sp):
            full = 6 * P * P
            whole = (E - full) // P
            rest = E - full - whole * P
            sp.wait_ge(cleared, 6)
            for a, arr in enumerate((src, dst, edge_type)):
                sp.dma_start(raw3[a][:, 0:6, :], arr[0:full].rearrange("(c t p) -> t c p", p=P, c=6)).then_inc(edges_in, 16)
                sp.dma_start(raw3[a][0:whole, 6, :], arr[full:full + whole * P].rearrange("(t p) -> t p", p=P)).then_inc(edges_in, 16)
                sp.dma_start(raw3[a][whole:whole + 1, 6, 0:rest], arr[full + whole * P:E].rearrange("(o p) -> o p", o=1)).then_inc(edges_in, 16)
            sp.dma_start(X3[:, 0:48, :], x[0:48 * P, :].rearrange("(b p) f -> p b f", p=P)).then_inc(x_in, 16)
            sp.dma_start(X3[0:LAST, 48, :], x[48 * P:N, :]).then_inc(x_in, 16)
            loads = [(w_raw[:, i, :], w) for i, w in enumerate((Wl1, Wr1, Wl2, Wr2))]
            loads += [(w_raw[0:A5, 4, :], attn_w), (w_raw[A5:2 * A5, 4, :], edge_w[:, 0:P]),
                      (w_raw[2 * A5:3 * A5, 4, :], edge_w[:, P:2 * P])]
            loads += [(base_s[:, l], bases[l].rearrange("n i o -> i n o")) for l in range(2)]
            loads += [(root_s, root.rearrange("l i o -> i l o")),
                      (comp_b[:, :], comp.rearrange("l r n -> (l r n)").partition_broadcast(P)),
                      (W1s[:, :], W1), (W2s[:, :], W2)]
            loads += [(row, v.partition_broadcast(P)) for row, v in (
                (BL1, bl1), (GA0, gamma0), (BE0, beta0), (BL2, bl2), (B10, bias1[0, :]), (B11, bias1[1, :]),
                (B2, b2), (GA2, gamma2), (BE2, beta2), (ab[:, 0:A5], attn_b), (ab[:, A5:], edge_b))]
            loads += [(b1c[:, :], b1.rearrange("(p o) -> p o", o=1)),
                      (anchors[0:A5, :], node_anchor), (anchors[A5:2 * A5, :], edge_anchor)]
            assert len(loads) == WEIGHT_LOADS
            for to, of in loads:
                sp.dma_start(to, of).then_inc(weights_in, 16)
            sp.wait_ge(edges_in, 9 * 16)
            sp.dma_start(dst_rows.rearrange("(c t p) -> t c p", p=P, c=CHUNKS), raw3[1]).then_inc(dst_out, 16)

            def group_destinations(q, groups):
                with sp.Fori(0, groups // 2) as it:
                    for s in range(2):
                        k = it * 2 + s
                        edge = sp.snap(k * (GT * P), min_val=0, max_val=(groups - 1) * GT * P)
                        sp.wait_ge(oht_abs, q * GROUPS + k + 1)
                        sp.dma_start(dst_b[s][:, :], dst_rows[bass.ds(edge, GT * P)].partition_broadcast(P)).then_inc(dst_in[s], 16)

            def store_h(v):
                sp.wait_ge(h_ready, v)
                sp.dma_start(h_table.rearrange("(b p) f -> p b f", p=P), H3).then_inc(table_in, 16)

            store_h(1)
            store_h(2)
            sp.wait_ge(dst_out, 16)
            group_destinations(0, GROUPS)
            sp.wait_ge(prep_done, 1)
            with if_rest(sp):
                sp.wait_ge(rest_table, 1)
                sp.dma_start(cnt_table.rearrange("(b p) r -> p b r", p=P),
                             inv_cnt[:, :].rearrange("p (b r) -> p b r", r=R)).then_inc(rest_table_in, 16)
            for l in range(2):
                with sp.Fori(0, NB // 2) as it:
                    for s in range(2):
                        b = it * 2 + s
                        node = sp.snap(b * P, min_val=0, max_val=(NB - 1) * P)
                        sp.wait_ge(evac_d, NB * (HOP1 + l) + b + 3)
                        sp.sem_inc(sp_turn, 1)
                        sp.wait_ge(evac_a, NB * l + b + 1)
                        sp.dma_start(xw_table.rearrange("(r n) f -> n r f", r=R)[bass.ds(node, P), :, :],
                                     xw_out[s].rearrange("p (r f) -> p r f", f=P)).then_inc(xw_stored[s], 16)
            store_h(5)
            sp.wait_ge(p_ready, 1)
            sp.dma_start(p_table.rearrange("(b p) a -> p b a", p=P), PT).then_inc(table_in, 16)
            group_destinations(1, GROUPS + 4)
            with if_rest(sp):
                sp.wait_ge(rest_table, 2)
                sp.dma_start(q_table.rearrange("(b p) a -> p b a", p=P), Q3).then_inc(rest_table_in, 16)
            sp.wait_ge(out_ready, 1)
            sp.dma_start(out[0:48 * P, :].rearrange("(b p) f -> p b f", p=P), X3[:, 0:48, :]).then_inc(stored, 16)
            sp.dma_start(out[48 * P:N, :], X3[0:LAST, 48, :]).then_inc(stored, 16)
            sp.wait_ge(stored, 32)

        @block.gpsimd
        def _(pool):
            nc.gpsimd.iota(iota[:, :], [[1, 2 * P]], base=0, channel_multiplier=0,
                           allow_small_or_imprecise_dtypes=True).then_inc(consts, 1)
            nc.gpsimd.iota(iota_p[:, :], [[0, 1]], base=0, channel_multiplier=1,
                           allow_small_or_imprecise_dtypes=True).then_inc(consts, 1)

            def gather(to, table, idx, done):
                nc.gpsimd.indirect_dma_start(out=to, out_offset=None, in_=table,
                                             in_offset=bass.IndirectOffsetOnAxis(ap=idx, axis=0)).then_inc(done, 16)

            def gather_pass(q, table):
                with pool.Fori(0, ITERS) as it:
                    for g in range(4):
                        pool.wait_ge(idx_staged, GROUPS * q + it * 4 + g + 1)
                        pool.sem_inc(pool_turn, 1)
                        for j in range(GT):
                            gather(G3[g][:, j, 0:P], table, stage[g][:, j:j + 1], gathered[g])

            def gather_rest(z, *tables):
                with if_rest(pool):
                    if z in (REST_WT, REST_L3):
                        pool.wait_ge(rest_table_in, 16 if z == REST_WT else 32)
                    with pool.Fori(0, GROUPS) as k:
                        pool.wait_ge(rest_staged, (k + 1) * len(tables) + z * GROUPS)
                        pool.sem_inc(pool_turn, 1)
                        for i, (t, w) in enumerate(tables):
                            for j in range(GT):
                                gather(G3[i][:, j, 0:w], t, stage[i][:, j:j + 1], rest_gathered[z])

            pool.wait_ge(prep_done, 1)
            pool.wait_ge(table_in, 16)
            gather_pass(0, h_table)
            gather_rest(REST_SAGE1, (h_table, P))
            pool.wait_ge(table_in, 32)
            gather_pass(1, h_table)
            gather_rest(REST_SAGE2, (h_table, P))
            gather_rest(REST_WT, (cnt_table, R))
            for l in range(2):
                for s in range(2):
                    pool.wait_ge(xw_stored[s], 16 * (NB // 2) * (l + 1))
                gather_pass(2 + l, xw_table)
                gather_rest(REST_HOP1 + l, (xw_table, P))
            pool.wait_ge(table_in, 48)
            gather_pass(4, h_table)
            gather_rest(REST_GIN, (h_table, P))
            pool.wait_ge(table_in, 64)
            with pool.Fori(0, ITERS // 2) as i2:
                for u in range(2):
                    it = i2 * 2 + u
                    pool.wait_ge(idx16, it + 1)
                    pool.wait_ge(logits_done, it + 1)
                    pool.sem_inc(pool_turn, 1)
                    for t in range(L16):
                        gather(p_rows[u][:, t, :], p_table, stage16[u][:, t:t + 1], gathered16[u])
            gather_rest(REST_L3, (p_table, R), (q_table, A5))

        @block.scalar
        def _(act):
            def sqrt(to, of, v):
                act.wait_ge(to_root, v)
                nc.scalar.activation(to, of, ACT.Sqrt).then_inc(rooted, 1)

            def stage_pass(q, idx, more=None):
                with act.Fori(0, ITERS) as it:
                    for g in range(4):
                        act.wait_ge(windows_summed, GROUPS * q + it * 4 + g + 1)
                        nc.scalar.activation(stage[g][:, :], idx[:, bass.ds((it * 4 + g) * GT, GT)],
                                             ACT.Copy).then_inc(idx_staged, 1)
                        if more:
                            more(it, g)

            def one_hot_rows(q, it, g, to, used, used_at, meanwhile=None):
                k = it * 4 + g
                act.wait_ge(dst_in[g % 2], 16 * ((GROUPS // 2) * q + it * 2 + g // 2 + 1))
                act.wait_ge(used, used_at)
                nc.scalar.activation(to[0], dst_b[g % 2][:, :], ACT.Abs, bias=neg_row[0][:, bass.ds(k, 1)])
                nc.scalar.activation(to[1], dst_b[g % 2][:, :], ACT.Abs, bias=neg_row[1][:, bass.ds(k, 1)]).then_inc(oht_abs, 1)
                if meanwhile:
                    meanwhile()
                act.wait_ge(oht_abs, q * GROUPS + k + 3)
                nc.scalar.activation(to[0], to[0], ACT.Relu, bias=1.0, scale=-1.0)
                nc.scalar.activation(to[1], to[1], ACT.Relu, bias=1.0, scale=-1.0).then_inc(oht_ready, 1)

            def block_loop(i, stage_block=None, late=None):
                w = width_in(i)
                parts = 32 if i == ANCHOR else P

                def body(b, s, pair):
                    n = NB * i + b
                    if stage_block and is_block(b, 0):
                        act.wait_ge(transposed, n + 2)
                        stage_block(b, s).then_inc(staged_a, 1)
                    act.wait_ge(transposed, n + 3)
                    if i != GIN:
                        act.wait_ge(multiplied, n + 1)
                    elif not is_block(b, 0, 1):
                        act.wait_ge(hidden, b - 1)
                    cols = P if i == ANCHOR else w
                    nc.scalar.activation(tT[s][0:parts, 0:cols], bank[6 + s][0:parts, 0:cols], ACT.Copy).then_inc(t_copied, 1)
                    if stage_block and not is_block(b, NB - 1):
                        stage_block(b + 1, 1 - s).then_inc(staged_a, 1)
                    if late and not is_block(b, 0):
                        late(b - 1, 1 - s, pair - 1 + s)

                in_pairs(act, body)
                if late:
                    late(NB - 1, 1, NB // 2 - 1)

            def stage_h(cols):
                return lambda b, s: nc.scalar.activation(in_st[s][:, cols], H[:, bass.ds(b * P, P)], ACT.Copy)

            act.sem_inc(oht_abs, 2)
            act.sem_inc(t_copied, 2)
            for c in range(6):
                act.wait_ge(edges_t, c + 1)
                to = (src_f, dst_f, et_f)[c // 2]
                w = 4 * P if c % 2 == 0 else 3 * P
                nc.scalar.activation(to[:, (c % 2) * 4 * P:(c % 2) * 4 * P + w], bank[c % 2][:, 0:w], ACT.Copy).then_inc(edges_c, 1)
            act.wait_ge(w_t, 1)
            nc.scalar.activation(WT[:, :], bank[2][:, :], ACT.Copy).then_inc(w_c, 1)
            nc.scalar.activation(PRJ[:, :], bank[3][:, 0:P], ACT.Copy).then_inc(w_c, 1)
            sqrt(stat2[:, :], stat[:, :], 1)
            act.wait_ge(prep_done, 1)
            stage_pass(0, src_i)
            block_loop(SAGE1, stage_h(slice(P, 2 * P)))
            sqrt(stat2[:, :], stat[:, :], 2)
            sqrt(sd[:, :], var[:, :], 3)
            act.wait_ge(h_ready, 2)
            stage_pass(1, src_i, lambda it, g: one_hot_rows(0, it, g, oht[g % 2], looked_up, it * 4 + g + 1))
            block_loop(SAGE2, stage_h(slice(P, 2 * P)))
            sqrt(stat2[:, :], stat[:, :], 4)
            sqrt(stat2[:, :], stat[:, :], 5)
            for l in range(2):
                def evacuate(m, s, pair):
                    act.wait_ge(multiplied, NB * (HOP1 + l) + m + 3)
                    if not (l == 0 and isinstance(pair, int) and pair == 0):
                        act.wait_ge(xw_stored[s], 16 * ((NB // 2) * l + pair))
                    nc.scalar.activation(xw_out[s][:, 4 * P:8 * P], bank[3 + 2 * s][:, :], ACT.Copy).then_inc(evac_a, 1)

                act.wait_ge(h_ready, 3 + l)
                block_loop(HOP1 + l, stage_h(slice(0, P)), evacuate)
                stage_pass(2 + l, xw_i)
            sqrt(stat2[:, :], stat[:, :], 6)
            act.wait_ge(h_ready, 5)
            stage_pass(4, src_i)

            def relu_hidden(m, s, pair):
                act.wait_ge(hidden, m + 1)
                act.wait_ge(multiplied, NB * GIN + m + 1)
                nc.scalar.activation(zT[s][:, :], bank[4 + s][:, 0:P], ACT.Relu, bias=b1c[:, :]).then_inc(hidden_c, 1)

            block_loop(GIN, late=relu_hidden)
            sqrt(sd[:, :], var[:, :], 7)
            sqrt(stat2[:, :], stat[:, :], 8)
            act.wait_ge(h_ready, 6)
            block_loop(PROJ, stage_h(slice(0, P)))
            act.wait_ge(soft_in, 1)
            nc.scalar.activation(n5[0], n5[0], ACT.Exp).then_inc(soft_exp, 1)

            def stage_16(it, u):
                act.wait_ge(logits_done, it + 1)
                nc.scalar.activation(stage16[u][:, :], src_i[:, bass.ds(it * L16, L16)], ACT.Copy).then_inc(idx16, 1)

            def rows_ahead(it, u, g):
                lo = lo_l3[u][:, g * GT:(g + 1) * GT, :]

                def source_distances():
                    act.wait_ge(scattered, 4 if isinstance(it, int) else it * 4 + g - 3)
                    for j in range(GT):
                        last = nc.scalar.activation(lo[:, j, :], iota[:, 0:P], ACT.Abs,
                                                    bias=neg_lo[:, bass.ds(it * L16 + g * GT + j, 1)])
                    last.then_inc(lo_abs, 1)

                one_hot_rows(1, it, g, [oht_l3[:, g, h, :] for h in range(2)], q_looked, it * 4 + g + 1,
                             source_distances if g < 2 else None)
                if g < 2:
                    act.wait_ge(lo_abs, it * 2 + g + 1)
                    nc.scalar.activation(lo, lo, ACT.Relu, bias=1.0, scale=-1.0).then_inc(lo_ready, 1)

            stage_16(0, 0)
            stage_16(1, 1)
            act.wait_ge(zeros_done, 1)
            for g in range(4):
                rows_ahead(0, 0, g)
            with act.Fori(0, ITERS // 2) as i2:
                for u in range(2):
                    it = i2 * 2 + u
                    rows_ahead(it + 1, 1 - u, 0)
                    act.wait_ge(soft_in, it + 2)
                    nc.scalar.activation(y5, z5, ACT.Exp).then_inc(soft_exp, 1)
                    stage_16(it + 2, u)
                    for g in range(1, 4):
                        rows_ahead(it + 1, 1 - u, g)

            with if_rest(act):
                with act.Fori(0, GROUPS) as k:
                    act.wait_ge(rest_soft, k + 1)
                    nc.scalar.activation(y5[:, 0:GT, :], z5[:, 0:GT, :], ACT.Exp).then_inc(rest_exp, 1)
            act.wait_ge(u_ready, 1)
            block_loop(ANCHOR, lambda b, s: nc.scalar.activation(in_st[s][:, 0:32], U[:, bass.ds(b * 32, 32)], ACT.Copy))

        @block.tensor
        def _(pe):
            pe.sem_inc(transposed, 2)
            pe.sem_inc(multiplied, 2)
            pe.sem_inc(windows_summed, CREDIT)
            pe.sem_inc(looked_up, 2)
            pe.sem_inc(q_looked, 4)
            pe.sem_inc(scattered, 4)
            pe.sem_inc(scattered_d, 4)

            pe.wait_ge(ident_done, 2)
            pe.wait_ge(edges_f, 3)
            for c in range(6):
                if c >= 2:
                    pe.wait_ge(edges_c, c - 1)
                chunks = range(4) if c % 2 == 0 else range(4, CHUNKS)
                for n, ch in enumerate(chunks):
                    last = nc.tensor.transpose(bank[c % 2][:, n * P:(n + 1) * P],
                                               raw_f[c // 2][:, ch * P:(ch + 1) * P], ident[:, :])
                last.then_inc(edges_t, 1)
            pe.wait_ge(ranges_d, 14)
            for i in range(2):
                for c in range(CHUNKS):
                    last = nc.tensor.matmul(bank[4 + 2 * i + c // 4][:, (c % 4) * P:(c % 4 + 1) * P], ones[:, :],
                                            diag[:, i * CHUNKS + c, :], start=True, stop=True)
            last.then_inc(ranges_b, 1)
            pe.wait_ge(weights_in, 16 * WEIGHT_LOADS)
            for i in range(4):
                nc.tensor.transpose(bank[2][:, i * P:(i + 1) * P], w_raw[:, i, :], ident[:, :])
            nc.tensor.transpose(bank[3][:, 0:P], w_raw[:, 4, :], ident[:, :]).then_inc(w_t, 1)

            def first_blocks(k, groups):
                return nc.values_load_multi_w_load_instructions(
                    blk_i[0:1, bass.ds(k, groups)], engines=[mybir.EngineType.PE], min_val=0, max_val=NB - 2)[1]

            def sum_pass(q, cols, more=None):
                with pe.Fori(0, ITERS) as it:
                    at = first_blocks(it * 4, 4) if more else None
                    for g in range(4):
                        k = it * 4 + g
                        if more:
                            more(k, g, at[g])
                        pe.wait_ge(windows_ready, LOOK * q + k + 1)
                        pe.wait_ge(gathered[g], 64 * (ITERS * q + it + 1))
                        pe.wait_ge(sums_added, LOOK * q + k + 1)
                        for h in range(2):
                            for j in range(GT):
                                last = nc.tensor.matmul(bank[g % 2][:, h * AW:h * AW + cols],
                                                        S3[g % 2][:, j, h * P:(h + 1) * P], G3[g][:, j, 0:cols],
                                                        start=(j == 0), stop=(j == GT - 1))
                        last.then_inc(windows_summed, 1)

            def rest_pass(z, cols):
                with if_rest(pe):
                    with pe.Fori(0, GROUPS) as k:
                        pe.wait_ge(rest_gathered[z], 16 * GT * (k + 1))
                        pe.sem_inc(pe_turn, 1)
                        with pe.Fori(0, WINDOWS) as w:
                            pe.wait_ge(rest_windows, (k + rest_sums_before(z) * GROUPS) * WINDOWS + w + 1)
                            for h in range(2):
                                for j in range(GT):
                                    last = nc.tensor.matmul(bank[0][:, h * AW:h * AW + cols], S3[0][:, j, h * P:(h + 1) * P],
                                                            G3[0][:, j, 0:cols], start=(j == 0), stop=(j == GT - 1))
                            last.then_inc(rest_summed, 1)

            def look_up_counts(k, g, at):
                pe.wait_ge(oht_ready, k + 1)
                pe.wait_ge(wt_done, k + 1)
                for j in range(GT):
                    for h in range(2):
                        last = nc.tensor.matmul(bank[4 + g % 2][:, j * DR:(j + 1) * DR],
                                                oht[g % 2][h][:, j * P:(j + 1) * P],
                                                digits[:, bass.ds(at * DR + h * DR, DR)], start=(h == 0), stop=(h == 1))
                last.then_inc(looked_up, 1)

            def block_loop(i, products, first=None):
                w = width_in(i)
                lag = 2 if first else 1

                def body(b, s, pair):
                    n = NB * i + b
                    if i in BY_DVE:
                        pe.wait_ge(staged_d, staged_d_before(i) + b + 1)
                    if i in BY_ACT:
                        pe.wait_ge(staged_a, staged_a_before(i) + b + 1)
                    pe.wait_ge(t_copied, n + 1)
                    if w == 2 * P:
                        nc.tensor.transpose(bank[6 + s][:, 0:P], in_st[s][:, 0:P], ident[:, :])
                        last = nc.tensor.transpose(bank[6 + s][:, P:2 * P], in_st[s][:, P:2 * P], ident[:, :])
                    else:
                        last = nc.tensor.transpose(bank[6 + s][0:w, 0:P], in_st[s][:, 0:w], ident[:, :])
                    last.then_inc(transposed, 1)
                    if first and not is_block(b, 0):
                        early(b - 1, 1 - s)
                    if not is_block(b, *range(lag)):
                        product(b - lag, (s + lag) % 2)

                def early(m, s):
                    pe.wait_ge(t_copied, NB * i + m + 3)
                    first(m, s)

                def product(m, s):
                    if not first:
                        pe.wait_ge(t_copied, NB * i + m + 3)
                    pe.wait_ge(evac_d, NB * i + m + 1)
                    products(m, s).then_inc(multiplied, 1)

                in_pairs(pe, body)
                if first:
                    early(NB - 1, 1)
                for m in range(NB - lag, NB):
                    product(m, m % 2)

            def sage(wl, wr):
                def products(m, s):
                    nc.tensor.matmul(bank[2 + s][:, 0:P], tT[s][:, 0:P], WT[:, wl * P:(wl + 1) * P], start=True, stop=False)
                    return nc.tensor.matmul(bank[2 + s][:, 0:P], tT[s][:, P:2 * P], WT[:, wr * P:(wr + 1) * P], start=False, stop=True)
                return products

            def hop(l):
                def products(m, s):
                    if not (isinstance(m, int) and m < 2):
                        pe.wait_ge(evac_a, NB * l + m - 1)
                    nc.tensor.matmul(bank[2 + 2 * s][:, :], tT[s][:, 0:P], Wcat[l][:, 0:4 * P], start=True, stop=True)
                    nc.tensor.matmul(bank[3 + 2 * s][:, :], tT[s][:, 0:P], Wcat[l][:, 4 * P:8 * P], start=True, stop=True)
                    return nc.tensor.matmul(bank[s][:, 0:P], tT[s][:, 0:P], Wcat[l][:, 8 * P:9 * P], start=True, stop=True)
                return products

            def gin_hidden(m, s):
                if not is_block(m, 0, 1):
                    pe.wait_ge(hidden_c, m - 1)
                nc.tensor.matmul(bank[4 + s][:, 0:P], W1s[:, :], tT[s][:, 0:P], start=True, stop=True).then_inc(hidden, 1)

            def gin(m, s):
                pe.wait_ge(hidden_c, m + 1)
                return nc.tensor.matmul(bank[2 + s][:, 0:P], zT[s][:, :], W2s[:, :], start=True, stop=True)

            def node_sums(v):
                pe.wait_ge(to_sum, v)
                nc.tensor.matmul(bank[4][:, 0:P], ones[:, :], part[:, :], start=True, stop=True).then_inc(summed, 1)

            pe.wait_ge(prep_done, 1)
            sum_pass(0, AW)
            rest_pass(REST_SAGE1, AW)
            block_loop(SAGE1, sage(0, 1))
            node_sums(1)
            node_sums(2)
            sum_pass(1, P, look_up_counts)
            rest_pass(REST_SAGE2, P)
            block_loop(SAGE2, sage(2, 3))
            for l in range(2):
                block_loop(HOP1 + l, hop(l))
                sum_pass(2 + l, P)
                rest_pass(REST_HOP1 + l, P)
            sum_pass(4, P)
            rest_pass(REST_GIN, P)
            block_loop(GIN, gin, gin_hidden)
            node_sums(3)
            node_sums(4)
            block_loop(PROJ, lambda m, s: nc.tensor.matmul(bank[2 + s][:, 0:15], tT[s][:, 0:P], PRJ[:, 0:15], start=True, stop=True))

            def look_up_logits(it, u, at):
                def group(g):
                    pe.wait_ge(oht_ready, GROUPS + it * 4 + g + 1)
                    for j in range(GT):
                        t = g * GT + j
                        for h in range(2):
                            last = nc.tensor.matmul(bank[4 + u][:, t * B5:(t + 1) * B5], oht_l3[:, g, h, j * P:(j + 1) * P],
                                                    Qp[:, bass.ds(at[g] * B5 + h * B5, B5)], start=(h == 0), stop=(h == 1))
                    last.then_inc(q_looked, 1)
                return group

            def by_source(u, t):
                return nc.tensor.matmul(bank[2][:, 0:245], lo_l3[u][:, t, :], M_l3[:, t, :],
                                        start=False, stop=False, skip_group_check=True)

            def by_destination(t, at):
                for h in range(2):
                    last = nc.tensor.matmul(by_dst[:, bass.ds(at * D5 + h * D5, B5)], S_l3[:, t, h * P:(h + 1) * P],
                                            b5p[:, t, :], start=False, stop=False, skip_group_check=True)
                return last

            def add_zeros(start):
                for i, cols in enumerate((4 * P, 4 * P, 245)):
                    last = nc.tensor.matmul(bank[i][:, 0:cols], ident[:, :], zeros[:, 0:cols],
                                            start=start, stop=not start, skip_group_check=True)
                return last

            pe.wait_ge(zeros_done, 1)
            add_zeros(True)
            lookup = look_up_logits(0, 0, first_blocks(0, 4))
            for g in range(4):
                lookup(g)
            with pe.Fori(0, ITERS // 2) as i2:
                for u in range(2):
                    it = i2 * 2 + u
                    at = first_blocks(it * 4, 8)
                    pe.wait_ge(logits_done, it + 2)
                    lookup = look_up_logits(it + 1, 1 - u, at[4:])
                    lookup(0)
                    for g in range(4):
                        if g < 3:
                            lookup(g + 1)
                        pe.wait_ge(ready5, it * 4 + g + 1)
                        if g < 2:
                            pe.wait_ge(lo_ready, it * 2 + g + 1)
                        for j in range(GT):
                            last = by_source(u, g * GT + j)
                        last.then_inc(scattered, 1)
                    pe.wait_ge(parts5, it + 2)
                    for g in range(4):
                        for j in range(GT):
                            last = by_destination(g * GT + j, at[g])
                        last.then_inc(scattered_d, 1)
            with if_rest(pe):
                with pe.Fori(0, GROUPS) as k:
                    pe.wait_ge(rest_ready5, k + 1)
                    for j in range(GT):
                        by_source(0, j)
                    with pe.Fori(0, WINDOWS) as w:
                        pe.wait_ge(rest_windows, (k + rest_sums_before(REST_L3) * GROUPS) * WINDOWS + w + 1)
                        for j in range(GT):
                            last = by_destination(j, w * 2)
                        last.then_inc(rest_summed, 1)
            add_zeros(False).then_inc(scat_all, 1)
            block_loop(ANCHOR, lambda m, s: nc.tensor.matmul(bank[2 + s][:, 0:P], tT[s][0:32, 0:P], anchors[:, :], start=True, stop=True))

        @block.vector
        def _(dve):
            V = nc.vector
            ch = Chain(dve, dve_done)
            over = lambda t, a, b: t.unsqueeze(2).broadcast_to([P, a, b])
            by_block = lambda t: over(t, NB, P)
            by_feat = lambda t: t.unsqueeze(1).broadcast_to([P, NB, P])
            roots = [0]
            sums = [0]

            def root(ins):
                roots[0] += 1
                ins.then_inc(to_root, 1)
                dve.wait_ge(rooted, roots[0])

            def node_sum(ins):
                sums[0] += 1
                ins.then_inc(to_sum, 1)
                dve.wait_ge(summed, sums[0])

            dve.sem_inc(sums_added, 1)
            dve.sem_inc(wt_done, 2)
            dve.sem_inc(evac_d, 2)
            dve.sem_inc(logits_done, 2)
            dve.sem_inc(parts5, 1)
            V.memset(raw_i[0], PAD_NODE).then_inc(cleared, 1)
            V.memset(raw_i[1], PAD_NODE).then_inc(cleared, 1)
            V.memset(raw_i[2], 0).then_inc(cleared, 1)
            V.memset(X3[:, 48:NB, :], 0.0).then_inc(cleared, 1)
            V.memset(w_raw[:, 4, :], 0.0).then_inc(cleared, 1)
            V.memset(anchors[:, :], 0.0).then_inc(cleared, 1)
            ch(V.memset(wt[:, :], 0.0))
            V.memset(ones[:, :], 1.0).then_inc(ident_done, 1)
            dve.wait_ge(consts, 2)
            V.tensor_scalar(ident[:, :], iota[:, 0:P], iota_p[:, :], None, ALU.is_equal).then_inc(ident_done, 1)
            ch(V.tensor_scalar(row_mask[:, :], iota_p[:, :], float(LAST), None, ALU.is_lt))

            dve.wait_ge(edges_in, 9 * 16)
            for a in range(3):
                V.tensor_copy(raw_f[a], raw_i[a]).then_inc(edges_f, 1)
            ch(V.tensor_scalar(blk_t, raw_i[1], 7, None, ALU.logical_shift_right))
            ch(V.tensor_copy(blk_f, blk_t))
            blk3 = blk_f.rearrange("t (c p) -> t c p", p=P)
            ch(V.tensor_reduce(tile_lo[:, 0:CHUNKS], blk3, AX.X, ALU.min))
            ch(V.tensor_reduce(tile_hi[:, 0:CHUNKS], blk3, AX.X, ALU.max))
            dve.wait_ge(ident_done, 2)
            for i, t in enumerate((tile_lo, tile_hi)):
                for c in range(CHUNKS):
                    V.tensor_scalar(diag[:, i * CHUNKS + c, :], ident[:, :], t[:, c:c + 1], None, ALU.mult).then_inc(ranges_d, 1)
            dve.wait_ge(ranges_b, 1)
            for i, (to, op) in enumerate(((lo_g, ALU.min), (hi_g, ALU.max))):
                for half, cols in enumerate((4 * P, 3 * P)):
                    ch(V.tensor_reduce(to[:, half * P:half * P + cols // GT],
                                       bank[4 + 2 * i + half][:, 0:cols].rearrange("p (g j) -> p g j", j=GT), AX.X, op))
            ch(V.tensor_copy(blk_i[:, :], lo_g[:, 0:GROUPS + 4]))
            NG = COLS // GT
            dve.wait_ge(edges_c, 6)
            grouped = lambda t: t.rearrange("p (g j) -> p g j", j=GT)
            ch(V.scalar_tensor_tensor(grouped(dl[:, :]), over(lo_g[:, :], NG, GT), -float(P), grouped(dst_f), ALU.mult, ALU.add))
            ch(V.tensor_copy(src_i[:, :], src_f))
            ch(V.scalar_tensor_tensor(tmp_f, et_f[:, :], float(NPAD), src_f, ALU.mult, ALU.add))
            ch(V.tensor_copy(xw_i[:, :], tmp_f))
            ch(V.tensor_scalar(tmp_i, src_i[:, :], 7, None, ALU.logical_shift_right))
            ch(V.tensor_copy(src_hi[:, :], tmp_i))
            ch(V.scalar_tensor_tensor(neg_lo[:, :], src_hi[:, :], -float(P), src_f, ALU.mult, ALU.add))
            ch(V.tensor_scalar(tmp_f, dl[:, :], 2.0 * P, None, ALU.is_lt))
            ch(V.scalar_tensor_tensor(neg_lo[:, :], neg_lo[:, :], 1.0, tmp_f, ALU.add, ALU.mult))
            ch(V.tensor_scalar(neg_lo[:, :], neg_lo[:, :], -1.0, 1.0, ALU.mult, ALU.add))
            for h in range(2):
                ch(V.tensor_scalar(neg_row[h][:, :], lo_g[:, 0:GROUPS + 4], -float(P), iota_p[:, :], ALU.mult, ALU.subtract))
                if h:
                    ch(V.tensor_scalar(neg_row[h][:, :], neg_row[h][:, :], float(P), None, ALU.subtract))
            ch(V.tensor_tensor(tmp_f[:, 0:GROUPS], hi_g[:, 0:GROUPS], lo_g[:, 0:GROUPS], ALU.subtract))
            ch(V.reduce_max(rest_f[:, :], tmp_f[:, 0:GROUPS], AX.X))
            ch(V.tensor_scalar(rest_f[:, :], rest_f[:, :], 2.0, None, ALU.is_ge))
            ch(V.tensor_copy(rest_i[:, :], rest_f[:, :]))
            dve.wait_ge(weights_in, 16 * WEIGHT_LOADS)
            for l in range(2):
                for n in range(4):
                    for r in range(R + 1):
                        w = Wcat[l][:, r * P:(r + 1) * P]
                        c = comp_b[:, (l * (R + 1) + r) * 4 + n:(l * (R + 1) + r) * 4 + n + 1]
                        if n == 0:
                            ch(V.tensor_scalar(w, base_s[:, l, n, :], c, None, ALU.mult))
                        else:
                            ch(V.scalar_tensor_tensor(w, base_s[:, l, n, :], c, w, ALU.mult, ALU.add))
                w = Wcat[l][:, R * P:(R + 1) * P]
                ch(V.tensor_tensor(w, w, root_s[:, l, :], ALU.add))
            dve.wait_ge(w_c, 2)
            dve.wait_ge(dst_out, 16)
            V.memset(stat[:, :], 0.0).then_inc(prep_done, 1)
            dve.wait_ge(prep_done, 1)

            def layer_norm():
                ch(V.reduce_sum(stat[:, :], X3, AX.X))
                ch(V.tensor_scalar(stat[:, :], stat[:, :], 1.0 / NCHANNELS, None, ALU.mult))
                ch(V.tensor_tensor(T3, X3, by_block(stat[:, :]), ALU.subtract))
                ch(V.tensor_tensor(H3, T3, T3, ALU.mult))
                ch(V.reduce_sum(stat[:, :], H3, AX.X))
                root(V.tensor_scalar(stat[:, :], stat[:, :], 1.0 / NCHANNELS, EPS, ALU.mult, ALU.add))
                ch(V.reciprocal(stat2[:, :], stat2[:, :]))
                V.scalar_tensor_tensor(H3, T3, 0.0, by_block(stat2[:, :]), ALU.max, ALU.mult).then_inc(h_ready, 1)

            def batch_norm(gamma, beta):
                def mask(t3):
                    ch(V.tensor_scalar(t3[:, 48, :], t3[:, 48, :], row_mask[:, :], None, ALU.mult))
                    ch(V.memset(t3[:, 49, :], 0.0))
                mask(O3)
                node_sum(V.reduce_sum(part[:, :], by_feature(O), AX.X))
                ch(V.tensor_scalar(mu[:, :], bank[4][:, 0:P], 1.0 / N, None, ALU.mult))
                ch(V.tensor_tensor(T3, O3, by_feat(mu[:, :]), ALU.subtract))
                mask(T3)
                ch(V.tensor_tensor(H3, T3, T3, ALU.mult))
                node_sum(V.reduce_sum(part[:, :], by_feature(H), AX.X))
                root(V.tensor_scalar(var[:, :], bank[4][:, 0:P], 1.0 / N, EPS, ALU.mult, ALU.add))
                ch(V.reciprocal(sd[:, :], sd[:, :]))
                ch(V.tensor_tensor(sd[:, :], sd[:, :], gamma, ALU.mult))
                ch(V.tensor_tensor(T3, T3, by_feat(sd[:, :]), ALU.mult))
                return T3, by_feat(beta)

            def sum_pass(q, weights=None, more=None):
                cols = AW if q == 0 else P

                def windows(k, gslot, s):
                    relation = over(et_f[:, bass.ds(k * GT, GT)], GT, R)
                    if q == 0:
                        V.tensor_tensor(G3[gslot][:, :, P:AW], iota[:, 0:R].unsqueeze(1).broadcast_to([P, GT, R]), relation, ALU.is_equal)
                    if q == 1:
                        V.tensor_tensor(ohe[s], iota[:, 0:R].unsqueeze(1).broadcast_to([P, GT, R]), relation, ALU.is_equal)
                    for j in range(GT):
                        row = dl[:, bass.ds(k * GT + j, 1)]
                        if weights is None:
                            last = V.tensor_scalar(S3[s][:, j, :], iota[:, :], row, None, ALU.is_equal)
                        else:
                            last = V.tensor_scalar(S3[s][:, j, :], iota[:, :], row, weights[:, bass.ds(k * GT + j, 1)], ALU.is_equal, ALU.mult)
                    last.then_inc(windows_ready, 1)

                V.memset(A[:, :], 0.0).then_inc(sums_added, 1)
                windows(0, 0, 0)
                with dve.Fori(0, ITERS) as it:
                    at = [dve.value_load(blk_i[0:1, bass.ds(it * 4 + g, 1)], min_val=0, max_val=NB - 2) for g in range(4)]
                    for g in range(4):
                        k = it * 4 + g
                        windows(k + 1, (g + 1) % 4, (g + 1) % 2)
                        dve.wait_ge(windows_summed, GROUPS * q + k + 1 + CREDIT)
                        dve.wait_ge(sums_added, LOOK * q + k + 2)
                        to = A[:, bass.ds(at[g] * AW, 2 * AW)].rearrange("p (h f) -> p h f", f=AW)[:, :, 0:cols]
                        V.tensor_tensor(to, to, bank[g % 2][:, 0:2 * AW].rearrange("p (h f) -> p h f", f=AW)[:, :, 0:cols],
                                        ALU.add).then_inc(sums_added, 1)
                        if more:
                            more(k, g)
                dve.wait_ge(sums_added, LOOK * (q + 1) + 1)

            class Steps:
                def __init__(self, sem, k, steps):
                    self.sem, self.at, self.n, self.steps = sem, k * steps, 0, steps

                def __call__(self, ins):
                    self.n += 1
                    assert self.n <= self.steps
                    ins.then_inc(self.sem, 1)
                    dve.wait_ge(self.sem, self.at + self.n)

            def take_rest(then, k):
                dl4 = dl[:, bass.ds(k * GT, GT)]
                then(V.tensor_scalar(outside[:, :], dl4, 2.0 * P, None, ALU.is_ge))
                then(V.tensor_scalar(rest_base[:, :], lo_g[:, bass.ds(k, 1)], float(P), 1.0, ALU.mult, ALU.add))
                then(V.scalar_tensor_tensor(rest4[:, :], dl4, rest_base[:, :], outside[:, :], ALU.add, ALU.mult))
                then(V.tensor_scalar(rest4[:, :], rest4[:, :], 1.0, None, ALU.subtract))

            def rest_window(z, k, w, to, sums, weights=None, columns=None):
                n = (k + rest_sums_before(z) * GROUPS) * WINDOWS + w + 1
                for j in range(GT):
                    if weights is None:
                        last = V.tensor_scalar(columns[:, j, :], iota[:, :], rest4[:, j:j + 1], None, ALU.is_equal)
                    else:
                        last = V.tensor_scalar(columns[:, j, :], iota[:, :], rest4[:, j:j + 1],
                                               weights[:, bass.ds(k * GT + j, 1)], ALU.is_equal, ALU.mult)
                last.then_inc(rest_windows, 1)
                dve.wait_ge(rest_summed, n)
                if to is not None:
                    V.tensor_tensor(to, to, sums, ALU.add).then_inc(rest_added, 1)
                    dve.wait_ge(rest_added, n)
                V.tensor_scalar(rest4[:, :], rest4[:, :], 2.0 * P, None, ALU.subtract).then_inc(rest_shift, 1)
                dve.wait_ge(rest_shift, n)

            def rest_pass(z, idx, cols, weights=None):
                with if_rest(dve):
                    with dve.Fori(0, GROUPS) as k:
                        then = Steps(rest_step[z], k, 5)
                        V.tensor_copy(stage[0][:, :], idx[:, bass.ds(k * GT, GT)]).then_inc(rest_staged, 1)
                        take_rest(then, k)
                        if cols == AW:
                            then(V.tensor_tensor(G3[0][:, :, P:AW], iota[:, 0:R].unsqueeze(1).broadcast_to([P, GT, R]),
                                                 over(et_f[:, bass.ds(k * GT, GT)], GT, R), ALU.is_equal))
                        else:
                            then(V.tensor_copy(rest_w[:, :], rest4[:, :]))
                        dve.sem_inc(dve_turn, 1)
                        with dve.Fori(0, WINDOWS) as w:
                            pair = lambda t: t.rearrange("p (h f) -> p h f", f=AW)[:, :, 0:cols]
                            rest_window(z, k, w, pair(A[:, bass.ds(w * 2 * AW, 2 * AW)]), pair(bank[0][:, 0:2 * AW]), weights, S3[0])

            def rest_weights():
                with if_rest(dve):
                    V.memset(rest_w[:, :], 0.0).then_inc(rest_table, 1)
                    dve.wait_ge(rest_table, 1)
                    with dve.Fori(0, GROUPS) as k:
                        then = Steps(rest_step[REST_WT], k, 11)
                        take_rest(then, k)
                        then(V.tensor_scalar(rest4[:, :], rest4[:, :], 0.0, None, ALU.max))
                        V.tensor_copy(stage[0][:, :], rest4[:, :]).then_inc(rest_staged, 1)
                        then(V.tensor_tensor(ohe[0], iota[:, 0:R].unsqueeze(1).broadcast_to([P, GT, R]),
                                             over(et_f[:, bass.ds(k * GT, GT)], GT, R), ALU.is_equal))
                        dve.wait_ge(rest_gathered[REST_WT], 16 * GT * (k + 1))
                        then(V.tensor_tensor(rest_sel, G3[0][:, :, 0:R], ohe[0], ALU.mult))
                        then(V.reduce_sum(rest_w[:, :], rest_sel, AX.X))
                        then(V.tensor_tensor(rest_w[:, :], rest_w[:, :], outside[:, :], ALU.mult))
                        w4 = wt[:, bass.ds(k * GT, GT)]
                        then(V.tensor_tensor(w4, w4, outside[:, :], ALU.subtract))
                        then(V.tensor_tensor(w4, w4, rest_w[:, :], ALU.add))

            def split(of, rest, parts, then):
                then(V.tensor_copy(parts[:, :, 0:A5], of))
                then(V.tensor_tensor(rest, of, parts[:, :, 0:A5], ALU.subtract))
                then(V.tensor_copy(parts[:, :, A5:2 * A5], rest))
                then(V.tensor_tensor(rest, rest, parts[:, :, A5:2 * A5], ALU.subtract))
                then(V.tensor_copy(parts[:, :, 2 * A5:], rest))

            def rest_attention():
                with if_rest(dve):
                    V.memset(rest_w[:, :], 0.0).then_inc(rest_table, 1)
                    dve.wait_ge(rest_table, 2)
                    with dve.Fori(0, GROUPS) as k:
                        then = Steps(rest_step[REST_L3], k, 21)
                        V.tensor_copy(stage[0][:, :], src_i[:, bass.ds(k * GT, GT)]).then_inc(rest_staged, 1)
                        take_rest(then, k)
                        then(V.tensor_scalar(rest_w[:, :], rest4[:, :], 0.0, None, ALU.max))
                        V.tensor_copy(stage[1][:, :], rest_w[:, :]).then_inc(rest_staged, 1)
                        z4, y4, b4, m4, r4 = z5[:, 0:GT, :], y5[:, 0:GT, :], b5[:, 0:GT, :], m5[:, 0:GT], r5[:, 0:GT]
                        dve.wait_ge(rest_gathered[REST_L3], 32 * GT * (k + 1))
                        then(V.tensor_tensor(z4, G3[0][:, :, 0:A5], G3[1][:, :, 0:A5], ALU.add))
                        then(V.scalar_tensor_tensor(z4, z4, 0.01, z4, ALU.mult, ALU.max))
                        then(V.reduce_max(m4, z4, AX.X))
                        V.tensor_tensor(z4, z4, over(m4, GT, A5), ALU.subtract).then_inc(rest_soft, 1)
                        dve.wait_ge(rest_exp, k + 1)
                        then(V.reduce_sum(r4, y4, AX.X))
                        then(V.reciprocal(r4, r4))
                        then(V.tensor_tensor(b4, y4, over(r4, GT, A5), ALU.mult))
                        split(b4, d5[:, 0:GT, :], b5p[:, 0:GT, :], then)
                        hi4 = src_hi[:, bass.ds(k * GT, GT)]
                        then(V.tensor_scalar(rest_w[:, :], hi4, -float(P), 1.0, ALU.mult, ALU.add))
                        then(V.tensor_tensor(rest_w[:, :], rest_w[:, :], src_i[:, bass.ds(k * GT, GT)], ALU.add))
                        then(V.tensor_tensor(rest_w[:, :], rest_w[:, :], outside[:, :], ALU.mult))
                        then(V.tensor_scalar(rest_w[:, :], rest_w[:, :], 1.0, None, ALU.subtract))
                        then(V.tensor_tensor(hi_l3[:, 0:GT, :], iota[:, 0:49].unsqueeze(1).broadcast_to([P, GT, 49]), over(hi4, GT, 49), ALU.is_equal))
                        for j in range(GT):
                            V.tensor_scalar(lo_l3[0][:, j, :], iota[:, 0:P], rest_w[:, j:j + 1], None, ALU.is_equal)
                            last = V.tensor_tensor(M_l3[:, j, :].rearrange("p (d a) -> p d a", a=A5), over(hi_l3[:, j, :], 49, A5),
                                                   b5[:, j, :].unsqueeze(1).broadcast_to([P, 49, A5]), ALU.mult)
                        last.then_inc(rest_ready5, 1)
                        with dve.Fori(0, WINDOWS) as w:
                            rest_window(REST_L3, k, w, None, None, None, S_l3)

            def pick_weights(k, g):
                dve.wait_ge(looked_up, k + 3)
                by_digit = lambda t: t.rearrange("p (j t r) -> p j t r", t=PARTS, r=R)
                V.tensor_tensor(by_digit(wsel[g % 2]), by_digit(bank[4 + g % 2][:, 0:GT * DR]),
                                ohe[g % 2].unsqueeze(2).broadcast_to([P, GT, PARTS, R]), ALU.mult).then_inc(wt_picked, 1)
                dve.wait_ge(wt_picked, k + 1)
                V.reduce_sum(wt[:, bass.ds(k * GT, GT)], wsel[g % 2].rearrange("p (j d) -> p j d", d=DR), AX.X).then_inc(wt_done, 1)

            def block_loop(i, evacuate, stage_block=None, lag=1):
                def body(b, s, pair):
                    if stage_block and is_block(b, 0):
                        dve.wait_ge(transposed, NB * i + 2)
                        stage_block(b, s).then_inc(staged_d, 1)
                    if stage_block and not is_block(b, NB - 1):
                        dve.wait_ge(transposed, NB * i + b + 2)
                        stage_block(b + 1, 1 - s).then_inc(staged_d, 1)
                    if not is_block(b, *range(lag)):
                        out_of_psum(b - lag, (s + lag) % 2, pair - 1 if lag == 2 else pair - 1 + s)

                def out_of_psum(m, s, pair):
                    dve.wait_ge(multiplied, NB * i + m + 3)
                    evacuate(m, s, pair).then_inc(evac_d, 1)

                in_pairs(dve, body)
                for m in range(NB - lag, NB):
                    out_of_psum(m, m % 2, m // 2)
                dve.wait_ge(evac_d, NB * (i + 1) + 2)

            def at_block(t, b):
                return t[:, bass.ds(b * P, P)]

            def sage(i, bias):
                block_loop(
                    i, lambda m, s, pair: V.tensor_tensor(at_block(O, m), bank[2 + s][:, 0:P], bias, ALU.add),
                    lambda b, s: V.tensor_scalar(in_st[s][:, 0:P], A[:, bass.ds(b * AW, P)], inv_deg[:, bass.ds(b, 1)], None, ALU.mult))
                ch(V.tensor_tensor(T3, O3, O3, ALU.mult))
                root(V.reduce_sum(stat[:, :], T3, AX.X))
                ch(V.tensor_scalar(stat2[:, :], stat2[:, :], L2_EPS, None, ALU.max))
                ch(V.reciprocal(stat2[:, :], stat2[:, :]))

            dve.wait_ge(x_in, 32)
            layer_norm()
            dve.wait_ge(h_ready, 1)
            sum_pass(0)
            rest_pass(REST_SAGE1, src_i, AW)
            cnt3 = A3[:, :, P:AW]
            inv3 = inv_cnt[:, :].rearrange("p (b r) -> p b r", r=R)
            ch(V.reduce_sum(inv_deg[:, :], cnt3, AX.X))
            ch(V.tensor_scalar(inv_deg[:, :], inv_deg[:, :], 1.0, None, ALU.max))
            ch(V.reciprocal(inv_deg[:, :], inv_deg[:, :]))
            ch(V.tensor_copy(cnt_i[:, :].rearrange("p (b r) -> p b r", r=R), cnt3))
            for d, mask in enumerate((0xFF, 0xFF00, 0xFF0000)):
                ch(V.tensor_scalar(cnt_d[:, :], cnt_i[:, :], mask, None, ALU.bitwise_and))
                ch(V.tensor_copy(digits4[:, :, d, :], cnt_d[:, :].rearrange("p (b r) -> p b r", r=R)))
            ch(V.tensor_scalar(inv3, cnt3, 1.0, None, ALU.max))
            ch(V.reciprocal(inv_cnt[:, :], inv_cnt[:, :]))
            sage(SAGE1, BL1)
            ch(V.scalar_tensor_tensor(O3, O3, 0.0, by_block(stat2[:, :]), ALU.max, ALU.mult))
            normed, beta = batch_norm(GA0, BE0)
            V.tensor_tensor(H3, normed, beta, ALU.add).then_inc(h_ready, 1)
            dve.wait_ge(h_ready, 2)
            sum_pass(1, more=pick_weights)
            dve.wait_ge(wt_done, GROUPS + 2)
            ch(V.tensor_scalar(wt[:, 0:TILES], wt[:, 0:TILES], 1.0, None, ALU.max))
            ch(V.reciprocal(wt[:, 0:TILES], wt[:, 0:TILES]))
            rest_pass(REST_SAGE2, src_i, P)
            rest_weights()
            sage(SAGE2, BL2)
            ch(V.tensor_tensor(T3, O3, by_block(stat2[:, :]), ALU.mult))
            ch(V.tensor_tensor(X3, X3, T3, ALU.add))
            layer_norm()
            for l in range(2):
                def evacuate(m, s, pair):
                    if not (l == 0 and isinstance(pair, int) and pair == 0):
                        dve.wait_ge(xw_stored[s], 16 * ((NB // 2) * l + pair))
                    V.tensor_copy(xw_out[s][:, 0:4 * P], bank[2 + 2 * s][:, :])
                    return V.tensor_tensor(at_block(O, m), bank[s][:, 0:P], (B10, B11)[l], ALU.add)

                block_loop(HOP1 + l, evacuate)
                sum_pass(2 + l, weights=wt)
                rest_pass(REST_HOP1 + l, xw_i, P, wt)
                ch(V.tensor_tensor(T3, AF, O3, ALU.add))
                if l == 0:
                    ch(V.tensor_scalar(T3, T3, 0.0, 0.5, ALU.max, ALU.mult))
                    V.scalar_tensor_tensor(H3, H3, 0.5, T3, ALU.mult, ALU.add).then_inc(h_ready, 1)
                    dve.wait_ge(h_ready, 4)
                else:
                    ch(V.tensor_scalar(T3, T3, 0.5, None, ALU.mult))
                    ch(V.scalar_tensor_tensor(T3, H3, 0.5, T3, ALU.mult, ALU.add))
                    ch(V.tensor_tensor(X3, X3, T3, ALU.add))
            layer_norm()
            dve.wait_ge(h_ready, 5)
            sum_pass(4)
            rest_pass(REST_GIN, src_i, P)
            block_loop(GIN, lambda m, s, pair: V.tensor_tensor(at_block(O, m), bank[2 + s][:, 0:P], B2, ALU.add),
                       lambda b, s: V.tensor_tensor(in_st[s][:, 0:P], A[:, bass.ds(b * AW, P)], at_block(H, b), ALU.add), lag=2)
            normed, beta = batch_norm(GA2, BE2)
            ch(V.tensor_tensor(T3, normed, beta, ALU.add))
            ch(V.tensor_tensor(X3, X3, T3, ALU.add))
            layer_norm()
            dve.wait_ge(h_ready, 6)
            block_loop(PROJ, lambda m, s, pair: V.tensor_copy(T[:, bass.ds(m * 15 + 4096, 15)], bank[2 + s][:, 0:15]))
            anchors_of = lambda t: t.unsqueeze(1).broadcast_to([P, NB, A5])
            ch(V.memset(PT, 0.0))
            V.tensor_copy(PT[:, :, 0:A5], PRo[:, :, A5:2 * A5]).then_inc(p_ready, 1)
            ch(V.tensor_tensor(Q3, PRo[:, :, 2 * A5:3 * A5], anchors_of(ab[:, A5:]), ALU.add))
            split(Q3, n5[2], Qp3, ch)
            ch(V.memset(U[:, :], 0.0))
            V.memset(zeros, 0.0).then_inc(zeros_done, 1)
            ch(V.tensor_tensor(n5[0], PRo[:, :, 0:A5], anchors_of(ab[:, 0:A5]), ALU.add))
            ch(V.reduce_max(stat[:, :], n5[0], AX.X))
            V.tensor_tensor(n5[0], n5[0], over(stat[:, :], NB, A5), ALU.subtract).then_inc(soft_in, 1)
            dve.wait_ge(soft_exp, 1)
            ch(V.reduce_sum(stat[:, :], n5[0], AX.X))
            ch(V.reciprocal(stat2[:, :], stat[:, :]))
            ch(V.tensor_tensor(U3[:, :, 0:A5], n5[0], over(stat2[:, :], NB, A5), ALU.mult))
            STEPS = 9
            with dve.Fori(0, ITERS // 2) as i2:
                for u in range(2):
                    it = i2 * 2 + u
                    step = [0]

                    def then(ins, meanwhile=None):
                        step[0] += 1
                        ins.then_inc(soft_step, 1)
                        if meanwhile:
                            meanwhile()
                        dve.wait_ge(soft_step, it * STEPS + step[0])

                    def columns(g):
                        dve.wait_ge(scattered_d, it * 4 + g + 1)
                        for t in range(g * GT, (g + 1) * GT):
                            V.tensor_scalar(S_l3[:, t, :], iota[:, :], dl[:, bass.ds(it * L16 + t, 1)], None, ALU.is_equal)

                    def source_rows(g):
                        for t in range(g * GT, (g + 1) * GT):
                            V.tensor_scalar(lo_l3[u][:, t, :], iota[:, 0:P], neg_lo[:, bass.ds(it * L16 + t, 1)], 0.0,
                                            ALU.add, ALU.is_equal)

                    def block_columns():
                        dve.wait_ge(parts5, it + 1)
                        V.tensor_tensor(hi_l3, iota[:, 0:49].unsqueeze(1).broadcast_to([P, L16, 49]),
                                        over(src_hi[:, bass.ds(it * L16, L16)], L16, 49), ALU.is_equal)

                    def by_block_and_anchor(g):
                        dve.wait_ge(scattered, it * 4 + g + 1)
                        at = slice(g * GT, (g + 1) * GT)
                        V.tensor_tensor(M_l3[:, at, :].rearrange("p j (d a) -> p j d a", a=A5),
                                        hi_l3[:, at, :].unsqueeze(3).broadcast_to([P, GT, 49, A5]),
                                        b5[:, at, :].unsqueeze(2).broadcast_to([P, GT, 49, A5]), ALU.mult).then_inc(ready5, 1)

                    dve.wait_ge(gathered16[u], 16 * L16 * (i2 + 1))
                    dve.wait_ge(q_looked, it * 4 + 4 + 4)
                    then(V.reduce_sum(z5, bank[4 + u][:, 0:L16 * B5].rearrange("p (j t a) -> p j a t", t=PARTS, a=A5), AX.X),
                         lambda: source_rows(2))
                    V.tensor_tensor(z5, z5, p_rows[u][:, :, 0:A5], ALU.add).then_inc(logits_done, 1)
                    source_rows(3)
                    dve.wait_ge(logits_done, it + 3)
                    then(V.scalar_tensor_tensor(z5, z5, 0.01, z5, ALU.mult, ALU.max), block_columns)
                    then(V.reduce_max(m5, z5, AX.X))
                    V.tensor_tensor(z5, z5, over(m5, L16, A5), ALU.subtract).then_inc(soft_in, 1)
                    for g in range(3):
                        columns(g)
                    dve.wait_ge(soft_exp, it + 2)
                    then(V.reduce_sum(r5, y5, AX.X), lambda: columns(3))
                    then(V.reciprocal(r5, r5))
                    V.tensor_tensor(b5, y5, over(r5, L16, A5), ALU.mult).then_inc(soft_mul, 1)
                    dve.wait_ge(soft_mul, it + 1)
                    groups = iter(range(4))

                    def interleaved(ins):
                        g = next(groups, None)
                        if g is None:
                            ins.then_inc(parts5, 1)
                        else:
                            then(ins, lambda: by_block_and_anchor(g))

                    split(b5, d5, b5p, interleaved)
            dve.wait_ge(lo_ready, 2 * (ITERS + 1))
            rest_attention()
            dve.wait_ge(scat_all, 1)
            in_parts = by_dst.rearrange("p (b c) -> p b c", c=D5)[:, :, 0:B5].rearrange("p b (t a) -> p b a t", a=A5)
            for first, last in ((0, 32), (32, 49)):
                ch(V.reduce_sum(n5[1][:, first:last, :], in_parts[:, first:last], AX.X))
            ch(V.tensor_tensor(n5[1][:, 0:49, :], n5[1][:, 0:49, :], bank[2][:, 0:245].rearrange("p (b a) -> p b a", a=A5), ALU.add))
            V.tensor_scalar(U3[:, 0:49, A5:2 * A5], n5[1][:, 0:49, :], 0.5, None, ALU.mult).then_inc(u_ready, 1)
            block_loop(ANCHOR, lambda m, s, pair: V.tensor_tensor(at_block(X, m), at_block(X, m), bank[2 + s][:, 0:P], ALU.add))
            V.tensor_tensor(X3, X3, H3, ALU.add).then_inc(out_ready, 1)


_INS = ['x', 'src', 'dst', 'edge_type_8', 'L0_gnn_Wl1', 'L0_gnn_bl1', 'L0_gnn_Wr1', 'L0_gnn_gamma', 'L0_gnn_beta',
        'L0_gnn_Wl2', 'L0_gnn_bl2', 'L0_gnn_Wr2', 'L1_gnn_bases', 'L1_gnn_comp', 'L1_gnn_root', 'L1_gnn_bias',
        'L2_gnn_W1', 'L2_gnn_b1', 'L2_gnn_W2', 'L2_gnn_b2', 'L2_gnn_gamma', 'L2_gnn_beta', 'L3_gnn_node_anchor',
        'L3_gnn_attn_w', 'L3_gnn_attn_b', 'L3_gnn_edge_anchor', 'L3_gnn_edge_w', 'L3_gnn_edge_b']


def kernel(**inputs):
    import numpy as _np
    import concourse.bacc as _bacc
    from concourse import mybir as _mybir
    from concourse.bass_utils import run_bass_kernel_spmd as _run

    nc = _bacc.Bacc("TRN2", target_bir_lowering=False, num_devices=1)
    arrays, args = {}, []
    for name in _INS:
        a = _np.ascontiguousarray(inputs[name])
        arrays[f"in_{name}"] = a
        args.append(nc.dram_tensor(f"in_{name}", a.shape, _mybir.dt.from_np(a.dtype), kind="ExternalInput").ap())
    args.append(nc.dram_tensor("out_x", (N, P), FP, kind="ExternalOutput").ap())
    gnn_stack(nc, *args)
    r = _run(nc, [arrays], core_ids=[0])
    return r.results[0]["out_x"]
```

```python
import concourse.bass as bass
from concourse import mybir
from concourse.alu_op_type import AluOpType as ALU
from contextlib import ExitStack

FP = mybir.dt.float32
I32 = mybir.dt.int32
BF = mybir.dt.bfloat16
ACT = mybir.ActivationFunctionType
AX = mybir.AxisListType

P = 128
N = 6250
E = 106250
NB = 50
NPAD = NB * P
PAD_NODE = 49 * P - 1
TILES = 832
CHUNKS = 7
COLS = CHUNKS * P
GT = 4
GROUPS = TILES // GT
LOOK = GROUPS + 1
WINDOWS = NB // 2
ITERS = GROUPS // 4
R = 8
A5 = 5
PARTS = 3
B5 = PARTS * A5
DR = PARTS * R
D5 = 16
AW = P + R
NCHANNELS = float(P)
LAST = N - 48 * P
EPS = 1e-5
L2_EPS = 1e-12
CREDIT = 4
WEIGHT_LOADS = 25
NORM_DVE = 30
UB = 5
UW = UB * 2 * A5


def gnn_stack(nc, x, src, dst, edge_type, Wl1, bl1, Wr1, gamma0, beta0, Wl2, bl2, Wr2,
              bases, comp, root, bias1, W1, b1, W2, b2, gamma2, beta2,
              node_anchor, attn_w, attn_b, edge_anchor, edge_w, edge_b, out):
    ctx = ExitStack()
    with ctx:
        def sb(name, cols, dt=FP, parts=P):
            return ctx.enter_context(nc.sbuf_tensor(name, [parts, cols], dt))

        def sem(name):
            return ctx.enter_context(nc.semaphore(name))

        def dram(name, shape, dt=FP):
            return nc.dram_tensor(name, shape, dt, kind="Internal").ap()

        h_table = dram("h_table", [NPAD, P])
        xw_table = dram("xw_table", [R * NPAD, P])
        p_table = dram("p_table", [NPAD, R])
        cnt_table = dram("cnt_table", [NPAD, R])
        q_table = dram("q_table", [NPAD, A5])
        dst_rows = dram("dst_rows", [COLS * P], I32)

        X = sb("X", NB * P)
        H = sb("H", NB * P)
        O = sb("O", NB * P)
        T = sb("T", NB * P)
        A = sb("A", NB * AW)
        blocks = lambda t: t[:, 0:NB * P].rearrange("p (b f) -> p b f", f=P)
        by_feature = lambda t: t[:, 0:NB * P].rearrange("p (b f) -> p f b", f=P)
        X3, H3, O3, T3 = blocks(X), blocks(H), blocks(O), blocks(T)
        A3 = A[:, :].rearrange("p (b f) -> p b f", f=AW)
        AF = A3[:, :, 0:P]
        inv_deg = sb("inv_deg", NB)
        counts = sb("counts", NB * R)
        digits = sb("digits", NB * PARTS * R, BF)
        digits4 = digits[:, :].rearrange("p (b t r) -> p b t r", t=PARTS, r=R)

        src_i = sb("src_i", COLS, I32)
        xw_i = sb("xw_i", COLS, I32)
        et_f = sb("et_f", COLS)
        dl = sb("dl", COLS)
        wt = sb("wt", COLS)
        neg_lo = sb("neg_lo", COLS)
        src_hi = sb("src_hi", COLS)
        neg_row = [sb(f"neg_row{h}", GROUPS + 4) for h in range(2)]
        blk_i = sb("blk_i", GROUPS + 4, I32)
        lo_g = sb("lo_g", COLS // GT)
        hi_g = sb("hi_g", COLS // GT)

        rest_i = sb("rest_i", 1, I32)
        rest_f = sb("rest_f", 1)
        outside = sb("outside", GT)
        rest4 = sb("rest4", GT)
        rest_base = sb("rest_base", 1)
        rest_w = sb("rest_w", GT)

        stage = [sb(f"stage{g}", GT, I32) for g in range(4)]
        stage16 = [sb(f"stage16_{i}", 4 * GT, I32) for i in range(2)]
        G = [sb(f"G{g}", GT * AW) for g in range(4)]
        G3 = [t[:, :].rearrange("p (j f) -> p j f", f=AW) for t in G]
        S = sb("S", 2 * GT * 2 * P)
        S3 = [S[:, i * GT * 2 * P:(i + 1) * GT * 2 * P].rearrange("p (j d) -> p j d", d=2 * P) for i in range(2)]
        dst_b = [sb(f"dst_b{i}", GT * P, I32) for i in range(2)]

        iota = sb("iota", 2 * P)
        iota_p = sb("iota_p", 1)
        ident = sb("ident", P)
        ones = sb("ones", P)
        row_mask = sb("row_mask", 1)
        WT = sb("WT", 4 * P)
        PRJ = sb("PRJ", P)
        Wcat = [sb(f"Wcat{l}", (R + 1) * P) for l in range(2)]
        W1s, W2s = sb("W1s", P), sb("W2s", P)
        rows = sb("rows", 9 * P)
        BL1, GA0, BE0, BL2, B10, B11, B2, GA2, BE2 = (rows[:, i * P:(i + 1) * P] for i in range(9))
        b1c = sb("b1c", 1)
        comp_b = sb("comp_b", 2 * (R + 1) * 4)
        ab = sb("ab", 2 * A5)
        own_in = sb("own_in", P)
        own_T = sb("own_T", P)
        in_st, tT = ([G[i][:, 0:4 * P], G[i + 1][:, 0:4 * P]] for i in (0, 2))
        zT = [dst_b[i][:, 0:2 * P].bitcast(FP) for i in range(2)]
        stat = sb("stat", NB)
        stat2 = sb("stat2", NB)
        mu = sb("mu", P)
        var = sb("var", P)
        sd = sb("sd", P)
        part = sb("part", P)

        raw_i = [O[:, a * COLS:(a + 1) * COLS].bitcast(I32) for a in range(3)]
        raw3 = [r.rearrange("t (c p) -> t c p", p=P) for r in raw_i]
        raw_f = [O[:, (3 + a) * COLS:(4 + a) * COLS] for a in range(3)]
        blk_t = T[:, 0:COLS].bitcast(I32)
        blk_f = T[:, COLS:2 * COLS]
        tile_lo, tile_hi = T[:, 2 * COLS:2 * COLS + 8], T[:, 2 * COLS + 8:2 * COLS + 16]
        diag = T[:, 2 * COLS + P:2 * COLS + P + 14 * P].rearrange("p (c t) -> p c t", t=P)
        w_raw = T[:, 4800:4800 + 5 * P].rearrange("p (w f) -> p w f", f=P)
        base_s = [t[:, :].bitcast(FP).rearrange("p (n o) -> p n o", n=4) for t in dst_b]
        root_s = T[:, 4000:4000 + 2 * P].rearrange("p (l o) -> p l o", l=2)
        src_t = A[:, 1400:1400 + COLS].bitcast(I32)
        tmp_i = A[:, 1400 + COLS:1400 + 2 * COLS].bitcast(I32)
        src_f = A[:, 1400 + 2 * COLS:1400 + 3 * COLS]
        dst_f = A[:, 1400 + 3 * COLS:1400 + 4 * COLS]
        tmp_f = A[:, 1400 + 4 * COLS:1400 + 5 * COLS]
        row_stats = T[:, 0:NB * 6]
        even_mean, even_var, odd_mean, odd_var = (row_stats.rearrange("p (b s) -> p b s", s=6)[:, :, i] for i in (1, 2, 4, 5))
        mean, total, diff, neg_mean = (T[:, 320 + i * NB:320 + (i + 1) * NB] for i in range(4))
        mix = T[:, 2048:2048 + (R + 1) * P].rearrange("p (r f) -> p r f", f=P)
        xw_out = [T[:, i * R * P:(i + 1) * R * P] for i in range(4)]
        cnt_i, cnt_d = (T[:, 2048 + i * NB * R:2048 + (i + 1) * NB * R].bitcast(I32) for i in range(2))
        oht = [[T[:, (2 * s + h) * GT * P // 2:(2 * s + h + 1) * GT * P // 2].bitcast(BF) for h in range(2)] for s in range(2)]
        ohe = [T[:, 4096 + s * GT * R:4096 + (s + 1) * GT * R].rearrange("p (j r) -> p j r", r=R) for s in range(2)]
        wsel = [T[:, 4224 + s * GT * PARTS * R:4224 + (s + 1) * GT * PARTS * R] for s in range(2)]
        rest_sel = wsel[0][:, 0:GT * R].rearrange("p (j r) -> p j r", r=R)
        L16 = 4 * GT
        S_l3 = T[:, 0:L16 * P].bitcast(BF).rearrange("p (j d) -> p j d", d=2 * P)
        PRo = T[:, 4096:4096 + NB * 15].rearrange("p (b a) -> p b a", a=15)
        PT = T[:, 4900:4900 + NB * R].rearrange("p (b a) -> p b a", a=R)
        U = S[:, 0:NB * 2 * A5]
        U3 = U[:, :].rearrange("p (b a) -> p b a", a=2 * A5)
        M_l3 = O[:, 0:L16 * 245].rearrange("p (j m) -> p j m", m=245)
        lo_l3 = [t.rearrange("p (j d) -> p j d", d=P) for t in (O[:, 3920:3920 + L16 * P], A[:, 2048:2048 + L16 * P])]
        oht_l3 = A[:, 0:2048].bitcast(BF).rearrange("p (g h e) -> p g h e", g=4, h=2)
        hi_l3 = A[:, 4096:4096 + L16 * 49].rearrange("p (j d) -> p j d", d=49)
        Qp = A[:, 4880:4880 + NB * B5 // 2].bitcast(BF)
        Qp3 = Qp.rearrange("p (b a) -> p b a", a=B5)
        Q = A[:, 5260:5260 + NB * A5]
        Q3 = Q.rearrange("p (b a) -> p b a", a=A5)
        of_tiles = lambda at, a: A[:, at:at + L16 * a].rearrange("p (j a) -> p j a", a=a)
        p_rows = [of_tiles(5520 + i * L16 * R, R) for i in range(2)]
        z5, y5, b5, d5 = (of_tiles(5800 + i * L16 * A5, A5) for i in range(4))
        m5 = A[:, 6120:6120 + L16]
        r5 = A[:, 6136:6136 + L16]
        b5p = A[:, 6152:6152 + L16 * B5 // 2].bitcast(BF).rearrange("p (j a) -> p j a", a=B5)
        n5 = [T[:, 5300 + i * NB * A5:5300 + (i + 1) * NB * A5].rearrange("p (b a) -> p b a", a=A5) for i in range(3)]
        zeros = Wcat[0][:, 0:4 * P]
        anchors = Wcat[1][0:UW, 0:UB * P]

        psum = ctx.enter_context(nc.psum_tensor("psum", [P, 8 * 512], FP))
        bank = [psum[:, i * 512:(i + 1) * 512] for i in range(8)]
        by_dst = psum[:, 0:2 * 512]

        consts = sem("consts")
        cleared = sem("cleared")
        x_in = sem("x_in")
        edges_in = sem("edges_in")
        weights_in = sem("weights_in")
        dst_out = sem("dst_out")
        edges_f = sem("edges_f")
        ident_done = sem("ident_done")
        edges_t = sem("edges_t")
        edges_c = sem("edges_c")
        ranges_d = sem("ranges_d")
        ranges_b = sem("ranges_b")
        w_t = sem("w_t")
        w_c = sem("w_c")
        prep_done = sem("prep_done")
        to_root = sem("to_root")
        rooted = sem("rooted")
        h_ready = sem("h_ready")
        h_first = sem("h_first")
        h_act = sem("h_act")
        row_stats_in = sem("row_stats_in")
        scales_ready = sem("scales_ready")
        residual = sem("residual")
        centred = sem("centred")
        squared = sem("squared")
        digits_ready = sem("digits_ready")
        mixed = sem("mixed")
        anchors_clear = sem("anchors_clear")
        anchors_in = sem("anchors_in")
        table_in = sem("table_in")
        to_sum = sem("to_sum")
        summed = sem("summed")
        dve_done = sem("dve_done")
        idx_staged = sem("idx_staged")
        sp_turn = sem("sp_turn")
        pe_turn = sem("pe_turn")
        dve_turn = sem("dve_turn")
        pool_turn = sem("pool_turn")
        gathered = [sem(f"gathered{g}") for g in range(4)]
        windows_ready = sem("windows_ready")
        windows_summed = sem("windows_summed")
        sums_added = sem("sums_added")
        own_staged = sem("own_staged")
        own_transposed = sem("own_transposed")
        own_copied = sem("own_copied")
        own_multiplied = sem("own_multiplied")
        own_added = sem("own_added")
        dst_in = [sem(f"dst_in{i}") for i in range(2)]
        oht_abs = sem("oht_abs")
        oht_ready = sem("oht_ready")
        looked_up = sem("looked_up")
        wt_picked = sem("wt_picked")
        wt_done = sem("wt_done")
        staged_d = sem("staged_d")
        staged_a = sem("staged_a")
        transposed = sem("transposed")
        t_copied = sem("t_copied")
        multiplied = sem("multiplied")
        evac_d = sem("evac_d")
        evac_a = sem("evac_a")
        hidden = sem("hidden")
        hidden_c = sem("hidden_c")
        xw_stored = [sem(f"xw_stored{i}") for i in range(4)]
        p_ready = sem("p_ready")
        idx16 = sem("idx16")
        gathered16 = [sem(f"gathered16_{u}") for u in range(2)]
        q_looked = sem("q_looked")
        logits_done = sem("logits_done")
        soft_step = sem("soft_step")
        soft_in = sem("soft_in")
        soft_exp = sem("soft_exp")
        soft_mul = sem("soft_mul")
        lo_abs = sem("lo_abs")
        lo_ready = sem("lo_ready")
        ready5 = sem("ready5")
        parts5 = sem("parts5")
        scattered = sem("scattered")
        scattered_d = sem("scattered_d")
        zeros_done = sem("zeros_done")
        scat_all = sem("scat_all")
        rest_table = sem("rest_table")
        rest_table_in = sem("rest_table_in")
        rest_staged = sem("rest_staged")
        rest_gathered = [sem(f"rest_gathered{z}") for z in range(7)]
        rest_step = [sem(f"rest_step{z}") for z in range(7)]
        rest_windows = sem("rest_windows")
        rest_summed = sem("rest_summed")
        rest_added = sem("rest_added")
        rest_shift = sem("rest_shift")
        rest_soft = sem("rest_soft")
        rest_exp = sem("rest_exp")
        rest_ready5 = sem("rest_ready5")
        u_ready = sem("u_ready")
        stored = sem("stored")

        block = ctx.enter_context(nc.Block())

        SAGE1, SAGE2, HOP1, HOP2, GIN, PROJ, ANCHOR = range(7)
        BY_DVE, BY_ACT = (SAGE1, SAGE2, GIN, PROJ), (HOP1, HOP2, ANCHOR)
        blocks_in = lambda i: {SAGE1: 2, SAGE2: 2, GIN: 2, PROJ: 2, ANCHOR: UB}.get(i, 1)
        steps_of = lambda i: NB // blocks_in(i)
        steps_before = lambda i, of=range(7): sum(steps_of(l) for l in of if l < i)
        NORM_ACT_STEPS = (NB - NORM_DVE) // 5
        stores_at = lambda place: (NB - place + 3) // 4
        MIX_STEPS = 2 * (4 + 3 + 1)

        def in_fours(eng, body, steps):
            rounds = (steps - 6) // 4
            for b in range(4):
                body(b, b % 2, (0, b))
            with eng.Fori(1, rounds + 1) as it:
                for j in range(4):
                    body(it * 4 + j, j % 2, (it, j))
            for b in range(4 * rounds + 4, steps):
                body(b, b % 2, (b // 4, b % 4))

        def turn_before(turn, lag):
            return (turn[0], turn[1] - lag) if turn[1] >= lag else (turn[0] - 1, turn[1] - lag + 4)

        def is_block(b, *these):
            return isinstance(b, int) and b in these

        class Chain:
            def __init__(self, eng, sem):
                self.eng, self.sem, self.n = eng, sem, 0

            def __call__(self, ins):
                self.n += 1
                ins.then_inc(self.sem, 1)
                self.eng.wait_ge(self.sem, self.n)

        def width_in(i):
            return 2 * P if blocks_in(i) == 2 else P

        REST_SAGE1, REST_SAGE2, REST_WT, REST_HOP1, REST_HOP2, REST_GIN, REST_L3 = range(7)
        rest_sums_before = lambda z: {REST_SAGE1: 0, REST_SAGE2: 1, REST_HOP1: 2, REST_HOP2: 3, REST_GIN: 4, REST_L3: 5}[z]

        def if_rest(eng):
            return eng.If(eng.value_load(rest_i[0:1, 0:1], min_val=0, max_val=1) > 0)

        @block.sync
        def _(sp):
            full = 6 * P * P
            whole = (E - full) // P
            rest = E - full - whole * P
            sp.wait_ge(cleared, 5)
            for a, arr in enumerate((src, dst, edge_type)):
                sp.dma_start(raw3[a][:, 0:6, :], arr[0:full].rearrange("(c t p) -> t c p", p=P, c=6)).then_inc(edges_in, 16)
                sp.dma_start(raw3[a][0:whole, 6, :], arr[full:full + whole * P].rearrange("(t p) -> t p", p=P)).then_inc(edges_in, 16)
                sp.dma_start(raw3[a][whole:whole + 1, 6, 0:rest], arr[full + whole * P:E].rearrange("(o p) -> o p", o=1)).then_inc(edges_in, 16)
            sp.dma_start(X3[:, 0:48, :], x[0:48 * P, :].rearrange("(b p) f -> p b f", p=P)).then_inc(x_in, 16)
            sp.dma_start(X3[0:LAST, 48, :], x[48 * P:N, :]).then_inc(x_in, 16)
            loads = [(w_raw[:, i, :], w) for i, w in enumerate((Wl1, Wr1, Wl2, Wr2))]
            loads += [(w_raw[0:A5, 4, :], attn_w), (w_raw[A5:2 * A5, 4, :], edge_w[:, 0:P]),
                      (w_raw[2 * A5:3 * A5, 4, :], edge_w[:, P:2 * P])]
            loads += [(base_s[l], bases[l].rearrange("n i o -> i n o")) for l in range(2)]
            loads += [(root_s, root.rearrange("l i o -> i l o")),
                      (comp_b[:, :], comp.rearrange("l r n -> (l r n)").partition_broadcast(P)),
                      (W1s[:, :], W1), (W2s[:, :], W2)]
            loads += [(row, v.partition_broadcast(P)) for row, v in (
                (BL1, bl1), (GA0, gamma0), (BE0, beta0), (BL2, bl2), (B10, bias1[0, :]), (B11, bias1[1, :]),
                (B2, b2), (GA2, gamma2), (BE2, beta2), (ab[:, 0:A5], attn_b), (ab[:, A5:], edge_b))]
            loads += [(b1c[:, :], b1.rearrange("(p o) -> p o", o=1))]
            assert len(loads) == WEIGHT_LOADS
            for to, of in loads:
                sp.dma_start(to, of).then_inc(weights_in, 16)
            sp.wait_ge(edges_in, 9 * 16)
            sp.dma_start(dst_rows.rearrange("(c t p) -> t c p", p=P, c=CHUNKS), raw3[1]).then_inc(dst_out, 16)

            def group_destinations(q, groups):
                with sp.Fori(0, groups // 2) as it:
                    for s in range(2):
                        k = it * 2 + s
                        edge = sp.snap(k * (GT * P), min_val=0, max_val=(groups - 1) * GT * P)
                        sp.wait_ge(oht_abs, q * GROUPS + k + 1)
                        sp.dma_start(dst_b[s][:, :], dst_rows[bass.ds(edge, GT * P)].partition_broadcast(P)).then_inc(dst_in[s], 16)

            def store_h(first, last):
                in_table = h_table.rearrange("(b p) f -> p b f", p=P)
                sp.dma_start(in_table[:, first:last, :], H3[:, first:last, :]).then_inc(table_in, 16)

            def store_normed(v, norm, first):
                sp.wait_ge(h_first, first)
                store_h(0, NORM_DVE // 2)
                sp.wait_ge(h_ready, v)
                store_h(NORM_DVE // 2, NORM_DVE)
                sp.wait_ge(h_act, NORM_ACT_STEPS * norm)
                store_h(NORM_DVE, NB)

            store_normed(1, 1, 1)
            sp.wait_ge(h_first, 2)
            store_h(0, NB // 2)
            sp.wait_ge(h_ready, 2)
            store_h(NB // 2, NB)
            sp.wait_ge(dst_out, 16)
            sp.wait_ge(mixed, MIX_STEPS)
            group_destinations(0, GROUPS)
            sp.wait_ge(prep_done, 1)
            with if_rest(sp):
                sp.wait_ge(rest_table, 1)
                sp.dma_start(cnt_table.rearrange("(b p) r -> p b r", p=P),
                             counts[:, :].rearrange("p (b r) -> p b r", r=R)).then_inc(rest_table_in, 16)
            def store_xw(l, b, node, place):
                sp.wait_ge(evac_d, steps_before(HOP1 + l) + b + 3)
                sp.sem_inc(sp_turn, 1)
                sp.wait_ge(evac_a, NB * l + b + 1)
                sp.dma_start(xw_table.rearrange("(r n) f -> n r f", r=R)[bass.ds(node, P), :, :],
                             xw_out[place].rearrange("p (r f) -> p r f", f=P)).then_inc(xw_stored[place], 16)

            for l in range(2):
                with sp.Fori(0, NB // 4) as it:
                    for place in range(4):
                        b = it * 4 + place
                        store_xw(l, b, sp.snap(b * P, min_val=0, max_val=(NB - 1) * P), place)
                for b in range(NB // 4 * 4, NB):
                    store_xw(l, b, b * P, b % 4)
            store_normed(5, 3, 4)
            sp.wait_ge(p_ready, 1)
            sp.dma_start(p_table.rearrange("(b p) a -> p b a", p=P), PT).then_inc(table_in, 16)
            sp.wait_ge(anchors_clear, 1)
            for j in range(UB):
                for i, anchor in enumerate((node_anchor, edge_anchor)):
                    row = (2 * j + i) * A5
                    sp.dma_start(anchors[row:row + A5, j * P:(j + 1) * P], anchor).then_inc(anchors_in, 16)
            group_destinations(1, GROUPS + 4)
            with if_rest(sp):
                sp.wait_ge(rest_table, 2)
                sp.dma_start(q_table.rearrange("(b p) a -> p b a", p=P), Q3).then_inc(rest_table_in, 16)
            sp.wait_ge(evac_d, steps_before(ANCHOR) + steps_of(ANCHOR) // 2 + 2)
            sp.dma_start(out[0:NB // 2 * P, :].rearrange("(b p) f -> p b f", p=P), X3[:, 0:NB // 2, :]).then_inc(stored, 16)
            sp.wait_ge(evac_d, steps_before(ANCHOR) + steps_of(ANCHOR) + 2)
            sp.dma_start(out[NB // 2 * P:48 * P, :].rearrange("(b p) f -> p b f", p=P), X3[:, NB // 2:48, :]).then_inc(stored, 16)
            sp.dma_start(out[48 * P:N, :], X3[0:LAST, 48, :]).then_inc(stored, 16)
            sp.wait_ge(stored, 48)

        @block.gpsimd
        def _(pool):
            nc.gpsimd.iota(iota[:, :], [[1, 2 * P]], base=0, channel_multiplier=0,
                           allow_small_or_imprecise_dtypes=True).then_inc(consts, 1)
            nc.gpsimd.iota(iota_p[:, :], [[0, 1]], base=0, channel_multiplier=1,
                           allow_small_or_imprecise_dtypes=True).then_inc(consts, 1)

            def gather(to, table, idx, done):
                nc.gpsimd.indirect_dma_start(out=to, out_offset=None, in_=table,
                                             in_offset=bass.IndirectOffsetOnAxis(ap=idx, axis=0)).then_inc(done, 16)

            def gather_pass(q, table):
                with pool.Fori(0, ITERS) as it:
                    for g in range(4):
                        pool.wait_ge(idx_staged, GROUPS * q + it * 4 + g + 1)
                        pool.sem_inc(pool_turn, 1)
                        for j in range(GT):
                            gather(G3[g][:, j, 0:P], table, stage[g][:, j:j + 1], gathered[g])

            def gather_rest(z, *tables):
                with if_rest(pool):
                    if z in (REST_WT, REST_L3):
                        pool.wait_ge(rest_table_in, 16 if z == REST_WT else 32)
                    with pool.Fori(0, GROUPS) as k:
                        pool.wait_ge(rest_staged, (k + 1) * len(tables) + z * GROUPS)
                        pool.sem_inc(pool_turn, 1)
                        for i, (t, w) in enumerate(tables):
                            for j in range(GT):
                                gather(G3[i][:, j, 0:w], t, stage[i][:, j:j + 1], rest_gathered[z])

            def mix_weights():
                then = Chain(pool, mixed)
                pool.wait_ge(weights_in, 16 * WEIGHT_LOADS)
                comp4 = comp_b[:, :].rearrange("p (l r n) -> p l r n", l=2, n=4)
                for l in range(2):
                    W3 = Wcat[l][:, :].rearrange("p (r f) -> p r f", f=P)
                    for n in range(4):
                        then(nc.gpsimd.tensor_tensor(mix if n else W3, base_s[l][:, n, :].unsqueeze(1).broadcast_to([P, R + 1, P]),
                                                     comp4[:, l, :, n].unsqueeze(2).broadcast_to([P, R + 1, P]), ALU.mult))
                        if n:
                            then(nc.gpsimd.tensor_tensor(W3, W3, mix, ALU.add))
                    then(nc.gpsimd.tensor_tensor(W3[:, R, :], W3[:, R, :], root_s[:, l, :], ALU.add))
                assert then.n == MIX_STEPS

            pool.wait_ge(prep_done, 1)
            pool.wait_ge(table_in, 48)
            gather_pass(0, h_table)
            gather_rest(REST_SAGE1, (h_table, P))
            mix_weights()
            pool.wait_ge(table_in, 80)
            gather_pass(1, h_table)
            gather_rest(REST_SAGE2, (h_table, P))
            gather_rest(REST_WT, (cnt_table, R))
            for l in range(2):
                for place in range(4):
                    pool.wait_ge(xw_stored[place], 16 * stores_at(place) * (l + 1))
                gather_pass(2 + l, xw_table)
                gather_rest(REST_HOP1 + l, (xw_table, P))
            pool.wait_ge(table_in, 128)
            gather_pass(4, h_table)
            gather_rest(REST_GIN, (h_table, P))
            pool.wait_ge(table_in, 144)
            with pool.Fori(0, ITERS // 2) as i2:
                for u in range(2):
                    it = i2 * 2 + u
                    pool.wait_ge(idx16, it + 1)
                    pool.wait_ge(logits_done, it + 1)
                    pool.sem_inc(pool_turn, 1)
                    for t in range(L16):
                        gather(p_rows[u][:, t, :], p_table, stage16[u][:, t:t + 1], gathered16[u])
            gather_rest(REST_L3, (p_table, R), (q_table, A5))

        @block.scalar
        def _(act):
            def sqrt(to, of, v):
                act.wait_ge(to_root, v)
                nc.scalar.activation(to, of, ACT.Sqrt).then_inc(rooted, 1)

            def stage_pass(q, idx, more=None, own=False):
                def iteration(it, stage_own, copy_own):
                    for g in range(4):
                        act.wait_ge(windows_summed, GROUPS * q + it * 4 + g + 1)
                        nc.scalar.activation(stage[g][:, :], idx[:, bass.ds((it * 4 + g) * GT, GT)],
                                             ACT.Copy).then_inc(idx_staged, 1)
                        if more:
                            more(it, g)
                        if g == 0 and stage_own:
                            act.wait_ge(own_transposed, NB * q + it + 1)
                            nc.scalar.activation(own_in[:, :], H[:, bass.ds(it * P, P)], ACT.Copy).then_inc(own_staged, 1)
                        if g == 1 and copy_own:
                            act.wait_ge(own_transposed, NB * q + it + 1)
                            act.wait_ge(own_multiplied, NB * q + it)
                            nc.scalar.activation(own_T[:, :], bank[6][:, 0:P], ACT.Copy).then_inc(own_copied, 1)

                if own:
                    iteration(0, True, False)
                    with act.Fori(1, NB) as it:
                        iteration(it, True, True)
                    iteration(NB, False, True)
                    with act.Fori(NB + 1, ITERS) as it:
                        iteration(it, False, False)
                else:
                    with act.Fori(0, ITERS) as it:
                        iteration(it, False, False)

            def one_hot_rows(q, it, g, to, used, used_at, meanwhile=None):
                k = it * 4 + g
                act.wait_ge(dst_in[g % 2], 16 * ((GROUPS // 2) * q + it * 2 + g // 2 + 1))
                act.wait_ge(used, used_at)
                nc.scalar.activation(to[0], dst_b[g % 2][:, :], ACT.Abs, bias=neg_row[0][:, bass.ds(k, 1)])
                nc.scalar.activation(to[1], dst_b[g % 2][:, :], ACT.Abs, bias=neg_row[1][:, bass.ds(k, 1)]).then_inc(oht_abs, 1)
                if meanwhile:
                    meanwhile()
                act.wait_ge(oht_abs, q * GROUPS + k + 3)
                nc.scalar.activation(to[0], to[0], ACT.Relu, bias=1.0, scale=-1.0)
                nc.scalar.activation(to[1], to[1], ACT.Relu, bias=1.0, scale=-1.0).then_inc(oht_ready, 1)

            def block_loop(i, stage_block=None, late=None):
                w = width_in(i)
                parts = UW if i == ANCHOR else P
                steps = steps_of(i)

                def body(b, s, turn):
                    n = steps_before(i) + b
                    if stage_block and is_block(b, 0):
                        act.wait_ge(transposed, n + 2)
                        for first in range(2):
                            stage_block(first, first).then_inc(staged_a, 1)
                    act.wait_ge(transposed, n + 3)
                    if i != GIN:
                        act.wait_ge(multiplied, n + 1)
                    elif not is_block(b, 0, 1):
                        act.wait_ge(hidden, b - 1)
                    nc.scalar.activation(tT[s][0:parts, 0:w], bank[6 + s][0:parts, 0:w], ACT.Copy).then_inc(t_copied, 1)
                    if stage_block and not is_block(b, steps - 2, steps - 1):
                        stage_block(b + 2, s).then_inc(staged_a, 1)
                    if late and not is_block(b, 0):
                        late(b - 1, 1 - s, turn_before(turn, 1))

                in_fours(act, body, steps)
                if late:
                    late(steps - 1, (steps - 1) % 2, ((steps - 1) // 4, (steps - 1) % 4))

            def normalise(norm):
                act.wait_ge(scales_ready, norm)
                with act.Fori(0, NORM_ACT_STEPS) as it:
                    for j in range(5):
                        b = it * 5 + NORM_DVE + j
                        last = nc.scalar.activation(H[:, bass.ds(b * P, P)], X[:, bass.ds(b * P, P)], ACT.Relu,
                                                    bias=neg_mean[:, bass.ds(b, 1)], scale=stat2[:, bass.ds(b, 1)])
                    last.then_inc(h_act, 1)

            def squares(norm):
                for half in range(2):
                    act.wait_ge(centred, 2 * (norm - 1) + half + 1)
                    at = slice(half * NB // 2, (half + 1) * NB // 2)
                    nc.scalar.activation(H3[:, at, :], T3[:, at, :], ACT.Square).then_inc(squared, 1)

            def stage_h(b, s):
                return nc.scalar.activation(in_st[s][:, 0:P], H[:, bass.ds(b * P, P)], ACT.Copy)

            act.sem_inc(oht_abs, 2)
            act.sem_inc(t_copied, 2)
            act.sem_inc(own_copied, 1)
            for c in range(6):
                act.wait_ge(edges_t, c + 1)
                to = (src_f, dst_f, et_f)[c // 2]
                w = 4 * P if c % 2 == 0 else 3 * P
                nc.scalar.activation(to[:, (c % 2) * 4 * P:(c % 2) * 4 * P + w], bank[c % 2][:, 0:w], ACT.Copy).then_inc(edges_c, 1)
            act.wait_ge(w_t, 1)
            nc.scalar.activation(WT[:, :], bank[2][:, :], ACT.Copy).then_inc(w_c, 1)
            nc.scalar.activation(PRJ[:, :], bank[3][:, 0:P], ACT.Copy).then_inc(w_c, 1)
            sqrt(stat2[:, :], stat[:, :], 1)
            normalise(1)
            act.wait_ge(prep_done, 1)
            act.wait_ge(h_act, NORM_ACT_STEPS)
            act.wait_ge(h_ready, 1)
            stage_pass(0, src_i, own=True)
            block_loop(SAGE1)
            sqrt(stat2[:, :], stat[:, :], 2)
            squares(1)
            sqrt(sd[:, :], var[:, :], 3)
            act.wait_ge(h_ready, 2)
            stage_pass(1, src_i, lambda it, g: one_hot_rows(0, it, g, oht[g % 2], looked_up, it * 4 + g + 1), own=True)
            block_loop(SAGE2)
            sqrt(stat2[:, :], stat[:, :], 4)
            sqrt(stat2[:, :], stat[:, :], 5)
            normalise(2)
            for l in range(2):
                def evacuate(m, s, turn):
                    act.wait_ge(multiplied, steps_before(HOP1 + l) + m + 3)
                    to = xw_out[turn[1]]
                    if not (l == 0 and is_block(turn[0], 0)):
                        act.wait_ge(xw_stored[turn[1]], 16 * (stores_at(turn[1]) * l + turn[0]))
                    nc.scalar.activation(to[:, 4 * P:8 * P], bank[3 + 2 * s][:, :], ACT.Copy).then_inc(evac_a, 1)

                act.wait_ge(h_ready, 3 + l)
                act.wait_ge(h_act, NORM_ACT_STEPS * 2)
                block_loop(HOP1 + l, stage_h, evacuate)
                stage_pass(2 + l, xw_i, own=True)
            sqrt(stat2[:, :], stat[:, :], 6)
            normalise(3)
            act.wait_ge(h_ready, 5)
            stage_pass(4, src_i)

            def relu_hidden(m, s, turn):
                act.wait_ge(hidden, m + 1)
                act.wait_ge(multiplied, steps_before(GIN) + m + 1)
                nc.scalar.activation(zT[s][:, :], bank[4 + s][:, 0:2 * P], ACT.Relu, bias=b1c[:, :]).then_inc(hidden_c, 1)

            block_loop(GIN, late=relu_hidden)
            squares(2)
            sqrt(sd[:, :], var[:, :], 7)
            sqrt(stat2[:, :], stat[:, :], 8)
            normalise(4)
            act.wait_ge(h_ready, 6)
            block_loop(PROJ)
            act.wait_ge(soft_in, 1)
            nc.scalar.activation(n5[0], n5[0], ACT.Exp).then_inc(soft_exp, 1)

            def stage_16(it, u):
                act.wait_ge(logits_done, it + 1)
                nc.scalar.activation(stage16[u][:, :], src_i[:, bass.ds(it * L16, L16)], ACT.Copy).then_inc(idx16, 1)

            def rows_ahead(it, u, g):
                lo = lo_l3[u][:, g * GT:(g + 1) * GT, :]

                def source_distances():
                    act.wait_ge(scattered, 4 if isinstance(it, int) else it * 4 + g - 3)
                    for j in range(GT):
                        last = nc.scalar.activation(lo[:, j, :], iota[:, 0:P], ACT.Abs,
                                                    bias=neg_lo[:, bass.ds(it * L16 + g * GT + j, 1)])
                    last.then_inc(lo_abs, 1)

                one_hot_rows(1, it, g, [oht_l3[:, g, h, :] for h in range(2)], q_looked, it * 4 + g + 1,
                             source_distances if g < 2 else None)
                if g < 2:
                    act.wait_ge(lo_abs, it * 2 + g + 1)
                    nc.scalar.activation(lo, lo, ACT.Relu, bias=1.0, scale=-1.0).then_inc(lo_ready, 1)

            stage_16(0, 0)
            stage_16(1, 1)
            act.wait_ge(zeros_done, 1)
            for g in range(4):
                rows_ahead(0, 0, g)
            with act.Fori(0, ITERS // 2) as i2:
                for u in range(2):
                    it = i2 * 2 + u
                    rows_ahead(it + 1, 1 - u, 0)
                    act.wait_ge(soft_in, it + 2)
                    nc.scalar.activation(y5, z5, ACT.Exp).then_inc(soft_exp, 1)
                    stage_16(it + 2, u)
                    for g in range(1, 4):
                        rows_ahead(it + 1, 1 - u, g)

            with if_rest(act):
                with act.Fori(0, GROUPS) as k:
                    act.wait_ge(rest_soft, k + 1)
                    nc.scalar.activation(y5[:, 0:GT, :], z5[:, 0:GT, :], ACT.Exp).then_inc(rest_exp, 1)
            act.wait_ge(u_ready, 1)
            block_loop(ANCHOR, lambda b, s: nc.scalar.activation(in_st[s][:, 0:UW], U[:, bass.ds(b * UW, UW)], ACT.Copy))

        @block.tensor
        def _(pe):
            pe.sem_inc(transposed, 2)
            pe.sem_inc(own_transposed, 1)
            pe.sem_inc(own_multiplied, 1)
            pe.sem_inc(multiplied, 2)
            pe.sem_inc(windows_summed, CREDIT)
            pe.sem_inc(looked_up, 2)
            pe.sem_inc(q_looked, 4)
            pe.sem_inc(scattered, 4)
            pe.sem_inc(scattered_d, 4)

            pe.wait_ge(ident_done, 2)
            pe.wait_ge(edges_f, 3)
            for c in range(6):
                if c >= 2:
                    pe.wait_ge(edges_c, c - 1)
                chunks = range(4) if c % 2 == 0 else range(4, CHUNKS)
                for n, ch in enumerate(chunks):
                    last = nc.tensor.transpose(bank[c % 2][:, n * P:(n + 1) * P],
                                               raw_f[c // 2][:, ch * P:(ch + 1) * P], ident[:, :])
                last.then_inc(edges_t, 1)
            pe.wait_ge(ranges_d, 14)
            for i in range(2):
                for c in range(CHUNKS):
                    last = nc.tensor.matmul(bank[4 + 2 * i + c // 4][:, (c % 4) * P:(c % 4 + 1) * P], ones[:, :],
                                            diag[:, i * CHUNKS + c, :], start=True, stop=True)
            last.then_inc(ranges_b, 1)
            pe.wait_ge(weights_in, 16 * WEIGHT_LOADS)
            for i in range(4):
                nc.tensor.transpose(bank[2][:, i * P:(i + 1) * P], w_raw[:, i, :], ident[:, :])
            nc.tensor.transpose(bank[3][:, 0:P], w_raw[:, 4, :], ident[:, :]).then_inc(w_t, 1)

            def first_blocks(k, groups):
                return nc.values_load_multi_w_load_instructions(
                    blk_i[0:1, bass.ds(k, groups)], engines=[mybir.EngineType.PE], min_val=0, max_val=NB - 2)[1]

            def sum_pass(q, cols, more=None, own=None):
                def iteration(it, own):
                    at = first_blocks(it * 4, 4) if more else None
                    for g in range(4):
                        k = it * 4 + g
                        if more:
                            more(k, g, at[g])
                        pe.wait_ge(windows_ready, LOOK * q + k + 1)
                        pe.wait_ge(gathered[g], 64 * (ITERS * q + it + 1))
                        pe.wait_ge(sums_added, LOOK * q + k + 1)
                        for h in range(2):
                            for j in range(GT):
                                last = nc.tensor.matmul(bank[g % 2][:, h * AW:h * AW + cols],
                                                        S3[g % 2][:, j, h * P:(h + 1) * P], G3[g][:, j, 0:cols],
                                                        start=(j == 0), stop=(j == GT - 1))
                        last.then_inc(windows_summed, 1)
                        if own is not None and g == 0:
                            pe.wait_ge(own_staged, NB * q + it + 1)
                            pe.wait_ge(own_copied, NB * q + it + 1)
                            nc.tensor.transpose(bank[6][:, 0:P], own_in[:, :], ident[:, :]).then_inc(own_transposed, 1)
                        if own is not None and g == 3:
                            pe.wait_ge(own_copied, NB * q + it + 2)
                            pe.wait_ge(own_added, NB * q + it + 1)
                            nc.tensor.matmul(bank[7][:, 0:P], own_T[:, :], own, start=True, stop=True).then_inc(own_multiplied, 1)

                if own is not None:
                    with pe.Fori(0, NB) as it:
                        iteration(it, own)
                    with pe.Fori(NB, ITERS) as it:
                        iteration(it, None)
                else:
                    with pe.Fori(0, ITERS) as it:
                        iteration(it, None)

            def rest_pass(z, cols):
                with if_rest(pe):
                    with pe.Fori(0, GROUPS) as k:
                        pe.wait_ge(rest_gathered[z], 16 * GT * (k + 1))
                        pe.sem_inc(pe_turn, 1)
                        with pe.Fori(0, WINDOWS) as w:
                            pe.wait_ge(rest_windows, (k + rest_sums_before(z) * GROUPS) * WINDOWS + w + 1)
                            for h in range(2):
                                for j in range(GT):
                                    last = nc.tensor.matmul(bank[0][:, h * AW:h * AW + cols], S3[0][:, j, h * P:(h + 1) * P],
                                                            G3[0][:, j, 0:cols], start=(j == 0), stop=(j == GT - 1))
                            last.then_inc(rest_summed, 1)

            def look_up_counts(k, g, at):
                pe.wait_ge(oht_ready, k + 1)
                pe.wait_ge(wt_done, k + 1)
                for j in range(GT):
                    for h in range(2):
                        last = nc.tensor.matmul(bank[4 + g % 2][:, j * DR:(j + 1) * DR],
                                                oht[g % 2][h][:, j * P:(j + 1) * P],
                                                digits[:, bass.ds(at * DR + h * DR, DR)], start=(h == 0), stop=(h == 1))
                last.then_inc(looked_up, 1)

            def block_loop(i, products, first=None):
                w = width_in(i)
                lag = 2 if first else 1

                def body(b, s, turn):
                    n = steps_before(i) + b
                    if i in BY_DVE:
                        pe.wait_ge(staged_d, steps_before(i, BY_DVE) + b + 1)
                    if i in BY_ACT:
                        pe.wait_ge(staged_a, steps_before(i, BY_ACT) + b + 1)
                    pe.wait_ge(t_copied, n + 1)
                    for c in range(0, w, P):
                        last = nc.tensor.transpose(bank[6 + s][:, c:c + P], in_st[s][:, c:c + P], ident[:, :])
                    last.then_inc(transposed, 1)
                    if first and not is_block(b, 0):
                        early(b - 1, 1 - s)
                    if not is_block(b, *range(lag)):
                        product(b - lag, (s + lag) % 2)

                def early(m, s):
                    pe.wait_ge(t_copied, steps_before(i) + m + 3)
                    first(m, s)

                def product(m, s):
                    if not first:
                        pe.wait_ge(t_copied, steps_before(i) + m + 3)
                    pe.wait_ge(evac_d, steps_before(i) + m + 1)
                    products(m, s).then_inc(multiplied, 1)

                in_fours(pe, body, steps_of(i))
                if first:
                    early(steps_of(i) - 1, (steps_of(i) - 1) % 2)
                for m in range(steps_of(i) - lag, steps_of(i)):
                    product(m, m % 2)

            def sage(w):
                def products(m, s):
                    for j in range(2):
                        last = nc.tensor.matmul(bank[2 + s][:, j * P:(j + 1) * P], tT[s][:, j * P:(j + 1) * P], w, start=True, stop=True)
                    return last
                return products

            def hop(l):
                def products(m, s):
                    if not (isinstance(m, int) and m < 2):
                        pe.wait_ge(evac_a, NB * l + m - 1)
                    nc.tensor.matmul(bank[2 + 2 * s][:, :], tT[s][:, 0:P], Wcat[l][:, 0:4 * P], start=True, stop=True)
                    return nc.tensor.matmul(bank[3 + 2 * s][:, :], tT[s][:, 0:P], Wcat[l][:, 4 * P:8 * P], start=True, stop=True)
                return products

            def gin_hidden(m, s):
                if not is_block(m, 0, 1):
                    pe.wait_ge(hidden_c, m - 1)
                nc.tensor.matmul(bank[4 + s][:, 0:2 * P], W1s[:, :], tT[s][:, 0:2 * P], start=True, stop=True).then_inc(hidden, 1)

            def gin(m, s):
                pe.wait_ge(hidden_c, m + 1)
                for j in range(2):
                    last = nc.tensor.matmul(bank[2 + s][:, j * P:(j + 1) * P], zT[s][:, j * P:(j + 1) * P], W2s[:, :], start=True, stop=True)
                return last

            def node_sums(v):
                pe.wait_ge(to_sum, v)
                nc.tensor.matmul(bank[4][:, 0:P], ones[:, :], part[:, :], start=True, stop=True).then_inc(summed, 1)

            pe.wait_ge(prep_done, 1)
            weight = lambda i: WT[:, i * P:(i + 1) * P]
            sum_pass(0, AW, own=weight(1))
            rest_pass(REST_SAGE1, AW)
            block_loop(SAGE1, sage(weight(0)))
            node_sums(1)
            node_sums(2)
            pe.wait_ge(digits_ready, 1)
            sum_pass(1, P, look_up_counts, own=weight(3))
            rest_pass(REST_SAGE2, P)
            block_loop(SAGE2, sage(weight(2)))
            pe.wait_ge(mixed, MIX_STEPS)
            for l in range(2):
                block_loop(HOP1 + l, hop(l))
                sum_pass(2 + l, P, own=Wcat[l][:, R * P:(R + 1) * P])
                rest_pass(REST_HOP1 + l, P)
            sum_pass(4, P)
            rest_pass(REST_GIN, P)
            block_loop(GIN, gin, gin_hidden)
            node_sums(3)
            node_sums(4)
            def project(m, s):
                for j in range(2):
                    last = nc.tensor.matmul(bank[2 + s][:, j * 15:(j + 1) * 15], tT[s][:, j * P:(j + 1) * P], PRJ[:, 0:15], start=True, stop=True)
                return last

            block_loop(PROJ, project)

            def look_up_logits(it, u, at):
                def group(g):
                    pe.wait_ge(oht_ready, GROUPS + it * 4 + g + 1)
                    for j in range(GT):
                        t = g * GT + j
                        for h in range(2):
                            last = nc.tensor.matmul(bank[4 + u][:, t * B5:(t + 1) * B5], oht_l3[:, g, h, j * P:(j + 1) * P],
                                                    Qp[:, bass.ds(at[g] * B5 + h * B5, B5)], start=(h == 0), stop=(h == 1))
                    last.then_inc(q_looked, 1)
                return group

            def by_source(u, t):
                return nc.tensor.matmul(bank[2][:, 0:245], lo_l3[u][:, t, :], M_l3[:, t, :],
                                        start=False, stop=False, skip_group_check=True)

            def by_destination(t, at):
                for h in range(2):
                    last = nc.tensor.matmul(by_dst[:, bass.ds(at * D5 + h * D5, B5)], S_l3[:, t, h * P:(h + 1) * P],
                                            b5p[:, t, :], start=False, stop=False, skip_group_check=True)
                return last

            def add_zeros(start):
                for i, cols in enumerate((4 * P, 4 * P, 245)):
                    last = nc.tensor.matmul(bank[i][:, 0:cols], ident[:, :], zeros[:, 0:cols],
                                            start=start, stop=not start, skip_group_check=True)
                return last

            pe.wait_ge(zeros_done, 1)
            add_zeros(True)
            lookup = look_up_logits(0, 0, first_blocks(0, 4))
            for g in range(4):
                lookup(g)
            with pe.Fori(0, ITERS // 2) as i2:
                for u in range(2):
                    it = i2 * 2 + u
                    at = first_blocks(it * 4, 8)
                    pe.wait_ge(logits_done, it + 2)
                    lookup = look_up_logits(it + 1, 1 - u, at[4:])
                    lookup(0)
                    for g in range(4):
                        if g < 3:
                            lookup(g + 1)
                        pe.wait_ge(ready5, it * 4 + g + 1)
                        if g < 2:
                            pe.wait_ge(lo_ready, it * 2 + g + 1)
                        for j in range(GT):
                            last = by_source(u, g * GT + j)
                        last.then_inc(scattered, 1)
                    pe.wait_ge(parts5, it + 2)
                    for g in range(4):
                        for j in range(GT):
                            last = by_destination(g * GT + j, at[g])
                        last.then_inc(scattered_d, 1)
            with if_rest(pe):
                with pe.Fori(0, GROUPS) as k:
                    pe.wait_ge(rest_ready5, k + 1)
                    for j in range(GT):
                        by_source(0, j)
                    with pe.Fori(0, WINDOWS) as w:
                        pe.wait_ge(rest_windows, (k + rest_sums_before(REST_L3) * GROUPS) * WINDOWS + w + 1)
                        for j in range(GT):
                            last = by_destination(j, w * 2)
                        last.then_inc(rest_summed, 1)
            add_zeros(False).then_inc(scat_all, 1)

            def anchor_sums(m, s):
                nc.tensor.matmul(bank[2 + 2 * s][:, 0:3 * P], tT[s][0:UW, 0:P], anchors[:, 0:3 * P], start=True, stop=True)
                return nc.tensor.matmul(bank[3 + 2 * s][:, 0:(UB - 3) * P], tT[s][0:UW, 0:P], anchors[:, 3 * P:UB * P], start=True, stop=True)

            pe.wait_ge(anchors_in, 16 * 2 * UB)
            block_loop(ANCHOR, anchor_sums)

        @block.vector
        def _(dve):
            V = nc.vector
            ch = Chain(dve, dve_done)
            over = lambda t, a, b: t.unsqueeze(2).broadcast_to([P, a, b])
            by_block = lambda t: over(t, NB, P)
            by_feat = lambda t: t.unsqueeze(1).broadcast_to([P, NB, P])
            roots = [0]
            sums = [0]

            def root(ins):
                roots[0] += 1
                ins.then_inc(to_root, 1)
                dve.wait_ge(rooted, roots[0])

            def node_sum(ins):
                sums[0] += 1
                ins.then_inc(to_sum, 1)
                dve.wait_ge(summed, sums[0])

            dve.sem_inc(sums_added, 1)
            dve.sem_inc(wt_done, 2)
            dve.sem_inc(evac_d, 2)
            dve.sem_inc(own_added, 1)
            dve.sem_inc(logits_done, 2)
            dve.sem_inc(parts5, 1)
            V.memset(raw_i[0], PAD_NODE).then_inc(cleared, 1)
            V.memset(raw_i[1], PAD_NODE).then_inc(cleared, 1)
            V.memset(raw_i[2], 0).then_inc(cleared, 1)
            V.memset(X3[:, 48:NB, :], 0.0).then_inc(cleared, 1)
            V.memset(w_raw[:, 4, :], 0.0).then_inc(cleared, 1)
            ch(V.memset(wt[:, :], 0.0))
            V.memset(ones[:, :], 1.0).then_inc(ident_done, 1)
            dve.wait_ge(consts, 2)
            V.tensor_scalar(ident[:, :], iota[:, 0:P], iota_p[:, :], None, ALU.is_equal).then_inc(ident_done, 1)
            ch(V.tensor_scalar(row_mask[:, :], iota_p[:, :], float(LAST), None, ALU.is_lt))

            dve.wait_ge(edges_in, 9 * 16)
            for a in range(3):
                V.tensor_copy(raw_f[a], raw_i[a]).then_inc(edges_f, 1)
            ch(V.tensor_scalar(blk_t, raw_i[1], 7, None, ALU.logical_shift_right))
            ch(V.tensor_copy(blk_f, blk_t))
            blk3 = blk_f.rearrange("t (c p) -> t c p", p=P)
            ch(V.tensor_reduce(tile_lo[:, 0:CHUNKS], blk3, AX.X, ALU.min))
            ch(V.tensor_reduce(tile_hi[:, 0:CHUNKS], blk3, AX.X, ALU.max))
            dve.wait_ge(ident_done, 2)
            for i, t in enumerate((tile_lo, tile_hi)):
                for c in range(CHUNKS):
                    V.tensor_scalar(diag[:, i * CHUNKS + c, :], ident[:, :], t[:, c:c + 1], None, ALU.mult).then_inc(ranges_d, 1)
            stats_taken = [0]
            normed = [0]

            def all_row_stats(of):
                with dve.Fori(0, NB // 10) as it:
                    for j in range(10):
                        b = it * 10 + j
                        last = V.bn_stats(row_stats[:, bass.ds(b * 6, 6)], of[:, bass.ds(b * P, P)])
                    last.then_inc(row_stats_in, 1)
                stats_taken[0] += NB // 10
                dve.wait_ge(row_stats_in, stats_taken[0])

            def layer_norm(part=None):
                normed[0] += 1
                all_row_stats(X)
                V.tensor_tensor(total[:, :], even_var, odd_var, ALU.add)
                V.tensor_tensor(diff[:, :], even_mean, odd_mean, ALU.subtract)
                ch(V.tensor_tensor(mean[:, :], even_mean, odd_mean, ALU.add))
                V.tensor_tensor(diff[:, :], diff[:, :], diff[:, :], ALU.mult)
                ch(V.tensor_scalar(mean[:, :], mean[:, :], 0.5, None, ALU.mult))
                ch(V.scalar_tensor_tensor(total[:, :], diff[:, :], P / 4.0, total[:, :], ALU.mult, ALU.add))
                V.tensor_scalar(stat[:, :], total[:, :], 1.0 / NCHANNELS, EPS, ALU.mult, ALU.add).then_inc(to_root, 1)
                roots[0] += 1
                mine = slice(0, NORM_DVE)
                of_block = lambda t, at: t[:, at].unsqueeze(2).broadcast_to([P, at.stop - at.start, P])
                ch(V.tensor_tensor(H3[:, mine, :], X3[:, mine, :], of_block(mean, mine), ALU.subtract))
                dve.wait_ge(rooted, roots[0])
                ch(V.reciprocal(stat2[:, :], stat2[:, :]))
                V.scalar_tensor_tensor(neg_mean[:, :], mean[:, :], -1.0, stat2[:, :], ALU.mult, ALU.mult).then_inc(scales_ready, 1)
                for at, ready in ((slice(0, NORM_DVE // 2), h_first), (slice(NORM_DVE // 2, NORM_DVE), h_ready)):
                    V.scalar_tensor_tensor(H3[:, at, :], H3[:, at, :], 0.0, of_block(stat2, at), ALU.max, ALU.mult).then_inc(ready, 1)

            def wait_for_normed(v):
                dve.wait_ge(h_ready, v)
                dve.wait_ge(h_act, NORM_ACT_STEPS * normed[0])

            norms = [0]

            def batch_norm(gamma, beta):
                def mask(t3):
                    ch(V.tensor_scalar(t3[:, 48, :], t3[:, 48, :], row_mask[:, :], None, ALU.mult))
                    return V.memset(t3[:, 49, :], 0.0)
                halves = [slice(0, NB // 2), slice(NB // 2, NB)]
                over_blocks = lambda t: t.unsqueeze(1).broadcast_to([P, NB // 2, P])
                ch(mask(O3))
                node_sum(V.reduce_sum(part[:, :], by_feature(O), AX.X))
                ch(V.tensor_scalar(mu[:, :], bank[4][:, 0:P], 1.0 / N, None, ALU.mult))
                dve.wait_ge(mixed, MIX_STEPS)
                V.tensor_tensor(T3[:, halves[0], :], O3[:, halves[0], :], over_blocks(mu[:, :]), ALU.subtract).then_inc(centred, 1)
                ch(V.tensor_tensor(T3[:, halves[1], :], O3[:, halves[1], :], over_blocks(mu[:, :]), ALU.subtract))
                mask(T3).then_inc(centred, 1)
                for half, to in enumerate((part, var)):
                    dve.wait_ge(squared, 2 * norms[0] + half + 1)
                    last = V.reduce_sum(to[:, :], H3[:, halves[half], :].rearrange("p b f -> p f b"), AX.X)
                ch(last)
                norms[0] += 1
                node_sum(V.tensor_tensor(part[:, :], part[:, :], var[:, :], ALU.add))
                root(V.tensor_scalar(var[:, :], bank[4][:, 0:P], 1.0 / N, EPS, ALU.mult, ALU.add))
                ch(V.reciprocal(sd[:, :], sd[:, :]))
                ch(V.tensor_tensor(sd[:, :], sd[:, :], gamma, ALU.mult))
                scale = lambda at: V.tensor_tensor(T3[:, at, :], T3[:, at, :], over_blocks(sd[:, :]), ALU.mult)
                return halves, scale, over_blocks(beta)

            def sum_pass(q, weights=None, more=None, beside=()):
                cols = AW if q == 0 else P

                def windows(k, gslot, s):
                    relation = over(et_f[:, bass.ds(k * GT, GT)], GT, R)
                    if q == 0:
                        V.tensor_tensor(G3[gslot][:, :, P:AW], iota[:, 0:R].unsqueeze(1).broadcast_to([P, GT, R]), relation, ALU.is_equal)
                    if q == 1:
                        V.tensor_tensor(ohe[s], iota[:, 0:R].unsqueeze(1).broadcast_to([P, GT, R]), relation, ALU.is_equal)
                    for j in range(GT):
                        row = dl[:, bass.ds(k * GT + j, 1)]
                        if weights is None:
                            last = V.tensor_scalar(S3[s][:, j, :], iota[:, :], row, None, ALU.is_equal)
                        else:
                            last = V.tensor_scalar(S3[s][:, j, :], iota[:, :], row, weights[:, bass.ds(k * GT + j, 1)], ALU.is_equal, ALU.mult)
                    last.then_inc(windows_ready, 1)

                V.memset(A[:, :], 0.0).then_inc(sums_added, 1)
                windows(0, 0, 0)
                def iteration(it, beside):
                    at = [dve.value_load(blk_i[0:1, bass.ds(it * 4 + g, 1)], min_val=0, max_val=NB - 2) for g in range(4)]
                    for g in range(4):
                        k = it * 4 + g
                        windows(k + 1, (g + 1) % 4, (g + 1) % 2)
                        dve.wait_ge(windows_summed, GROUPS * q + k + 1 + CREDIT)
                        dve.wait_ge(sums_added, LOOK * q + k + 2)
                        to = A[:, bass.ds(at[g] * AW, 2 * AW)].rearrange("p (h f) -> p h f", f=AW)[:, :, 0:cols]
                        V.tensor_tensor(to, to, bank[g % 2][:, 0:2 * AW].rearrange("p (h f) -> p h f", f=AW)[:, :, 0:cols],
                                        ALU.add).then_inc(sums_added, 1)
                        if more:
                            more(k, g)
                        if g < len(beside) and beside[g]:
                            beside[g](it)

                with dve.Fori(0, NB if beside else ITERS) as it:
                    iteration(it, beside)
                if beside:
                    with dve.Fori(NB, ITERS) as it:
                        iteration(it, ())
                dve.wait_ge(sums_added, LOOK * (q + 1) + 1)

            class Steps:
                def __init__(self, sem, k, steps):
                    self.sem, self.at, self.n, self.steps = sem, k * steps, 0, steps

                def __call__(self, ins):
                    self.n += 1
                    assert self.n <= self.steps
                    ins.then_inc(self.sem, 1)
                    dve.wait_ge(self.sem, self.at + self.n)

            def take_rest(then, k):
                dl4 = dl[:, bass.ds(k * GT, GT)]
                then(V.tensor_scalar(outside[:, :], dl4, 2.0 * P, None, ALU.is_ge))
                then(V.tensor_scalar(rest_base[:, :], lo_g[:, bass.ds(k, 1)], float(P), 1.0, ALU.mult, ALU.add))
                then(V.scalar_tensor_tensor(rest4[:, :], dl4, rest_base[:, :], outside[:, :], ALU.add, ALU.mult))
                then(V.tensor_scalar(rest4[:, :], rest4[:, :], 1.0, None, ALU.subtract))

            def rest_window(z, k, w, to, sums, weights=None, columns=None):
                n = (k + rest_sums_before(z) * GROUPS) * WINDOWS + w + 1
                for j in range(GT):
                    if weights is None:
                        last = V.tensor_scalar(columns[:, j, :], iota[:, :], rest4[:, j:j + 1], None, ALU.is_equal)
                    else:
                        last = V.tensor_scalar(columns[:, j, :], iota[:, :], rest4[:, j:j + 1],
                                               weights[:, bass.ds(k * GT + j, 1)], ALU.is_equal, ALU.mult)
                last.then_inc(rest_windows, 1)
                dve.wait_ge(rest_summed, n)
                if to is not None:
                    V.tensor_tensor(to, to, sums, ALU.add).then_inc(rest_added, 1)
                    dve.wait_ge(rest_added, n)
                V.tensor_scalar(rest4[:, :], rest4[:, :], 2.0 * P, None, ALU.subtract).then_inc(rest_shift, 1)
                dve.wait_ge(rest_shift, n)

            def rest_pass(z, idx, cols, weights=None):
                with if_rest(dve):
                    with dve.Fori(0, GROUPS) as k:
                        then = Steps(rest_step[z], k, 5)
                        V.tensor_copy(stage[0][:, :], idx[:, bass.ds(k * GT, GT)]).then_inc(rest_staged, 1)
                        take_rest(then, k)
                        if cols == AW:
                            then(V.tensor_tensor(G3[0][:, :, P:AW], iota[:, 0:R].unsqueeze(1).broadcast_to([P, GT, R]),
                                                 over(et_f[:, bass.ds(k * GT, GT)], GT, R), ALU.is_equal))
                        else:
                            then(V.tensor_copy(rest_w[:, :], rest4[:, :]))
                        dve.sem_inc(dve_turn, 1)
                        with dve.Fori(0, WINDOWS) as w:
                            pair = lambda t: t.rearrange("p (h f) -> p h f", f=AW)[:, :, 0:cols]
                            rest_window(z, k, w, pair(A[:, bass.ds(w * 2 * AW, 2 * AW)]), pair(bank[0][:, 0:2 * AW]), weights, S3[0])

            def rest_weights():
                with if_rest(dve):
                    V.memset(rest_w[:, :], 0.0).then_inc(rest_table, 1)
                    dve.wait_ge(rest_table, 1)
                    with dve.Fori(0, GROUPS) as k:
                        then = Steps(rest_step[REST_WT], k, 10)
                        take_rest(then, k)
                        then(V.tensor_scalar(rest4[:, :], rest4[:, :], 0.0, None, ALU.max))
                        V.tensor_copy(stage[0][:, :], rest4[:, :]).then_inc(rest_staged, 1)
                        then(V.tensor_tensor(ohe[0], iota[:, 0:R].unsqueeze(1).broadcast_to([P, GT, R]),
                                             over(et_f[:, bass.ds(k * GT, GT)], GT, R), ALU.is_equal))
                        dve.wait_ge(rest_gathered[REST_WT], 16 * GT * (k + 1))
                        then(V.tensor_tensor(rest_sel, G3[0][:, :, 0:R], ohe[0], ALU.mult))
                        then(V.reduce_sum(rest_w[:, :], rest_sel, AX.X))
                        then(V.tensor_tensor(rest_w[:, :], rest_w[:, :], outside[:, :], ALU.mult))
                        w4 = wt[:, bass.ds(k * GT, GT)]
                        then(V.tensor_tensor(w4, w4, rest_w[:, :], ALU.add))

            def split(of, rest, parts, then):
                then(V.tensor_copy(parts[:, :, 0:A5], of))
                then(V.tensor_tensor(rest, of, parts[:, :, 0:A5], ALU.subtract))
                then(V.tensor_copy(parts[:, :, A5:2 * A5], rest))
                then(V.tensor_tensor(rest, rest, parts[:, :, A5:2 * A5], ALU.subtract))
                then(V.tensor_copy(parts[:, :, 2 * A5:], rest))

            def rest_attention():
                with if_rest(dve):
                    V.memset(rest_w[:, :], 0.0).then_inc(rest_table, 1)
                    dve.wait_ge(rest_table, 2)
                    with dve.Fori(0, GROUPS) as k:
                        then = Steps(rest_step[REST_L3], k, 21)
                        V.tensor_copy(stage[0][:, :], src_i[:, bass.ds(k * GT, GT)]).then_inc(rest_staged, 1)
                        take_rest(then, k)
                        then(V.tensor_scalar(rest_w[:, :], rest4[:, :], 0.0, None, ALU.max))
                        V.tensor_copy(stage[1][:, :], rest_w[:, :]).then_inc(rest_staged, 1)
                        z4, y4, b4, m4, r4 = z5[:, 0:GT, :], y5[:, 0:GT, :], b5[:, 0:GT, :], m5[:, 0:GT], r5[:, 0:GT]
                        dve.wait_ge(rest_gathered[REST_L3], 32 * GT * (k + 1))
                        then(V.tensor_tensor(z4, G3[0][:, :, 0:A5], G3[1][:, :, 0:A5], ALU.add))
                        then(V.scalar_tensor_tensor(z4, z4, 0.01, z4, ALU.mult, ALU.max))
                        then(V.reduce_max(m4, z4, AX.X))
                        V.tensor_tensor(z4, z4, over(m4, GT, A5), ALU.subtract).then_inc(rest_soft, 1)
                        dve.wait_ge(rest_exp, k + 1)
                        then(V.reduce_sum(r4, y4, AX.X))
                        then(V.reciprocal(r4, r4))
                        then(V.tensor_tensor(b4, y4, over(r4, GT, A5), ALU.mult))
                        split(b4, d5[:, 0:GT, :], b5p[:, 0:GT, :], then)
                        hi4 = src_hi[:, bass.ds(k * GT, GT)]
                        then(V.tensor_scalar(rest_w[:, :], hi4, -float(P), 1.0, ALU.mult, ALU.add))
                        then(V.tensor_tensor(rest_w[:, :], rest_w[:, :], src_i[:, bass.ds(k * GT, GT)], ALU.add))
                        then(V.tensor_tensor(rest_w[:, :], rest_w[:, :], outside[:, :], ALU.mult))
                        then(V.tensor_scalar(rest_w[:, :], rest_w[:, :], 1.0, None, ALU.subtract))
                        then(V.tensor_tensor(hi_l3[:, 0:GT, :], iota[:, 0:49].unsqueeze(1).broadcast_to([P, GT, 49]), over(hi4, GT, 49), ALU.is_equal))
                        for j in range(GT):
                            V.tensor_scalar(lo_l3[0][:, j, :], iota[:, 0:P], rest_w[:, j:j + 1], None, ALU.is_equal)
                            last = V.tensor_tensor(M_l3[:, j, :].rearrange("p (d a) -> p d a", a=A5), over(hi_l3[:, j, :], 49, A5),
                                                   b5[:, j, :].unsqueeze(1).broadcast_to([P, 49, A5]), ALU.mult)
                        last.then_inc(rest_ready5, 1)
                        with dve.Fori(0, WINDOWS) as w:
                            rest_window(REST_L3, k, w, None, None, None, S_l3)

            def pick_weights(k, g):
                dve.wait_ge(looked_up, k + 3)
                by_digit = lambda t: t.rearrange("p (j t r) -> p j t r", t=PARTS, r=R)
                V.tensor_tensor(by_digit(wsel[g % 2]), by_digit(bank[4 + g % 2][:, 0:GT * DR]),
                                ohe[g % 2].unsqueeze(2).broadcast_to([P, GT, PARTS, R]), ALU.mult).then_inc(wt_picked, 1)
                dve.wait_ge(wt_picked, k + 1)
                V.reduce_sum(wt[:, bass.ds(k * GT, GT)], wsel[g % 2].rearrange("p (j d) -> p j d", d=DR), AX.X).then_inc(wt_done, 1)

            def block_loop(i, evacuate, stage_block=None, lag=1):
                def body(b, s, turn):
                    if stage_block and is_block(b, 0):
                        dve.wait_ge(transposed, steps_before(i) + 2)
                        stage_block(b, s).then_inc(staged_d, 1)
                    if stage_block and not is_block(b, steps_of(i) - 1):
                        dve.wait_ge(transposed, steps_before(i) + b + 2)
                        stage_block(b + 1, 1 - s).then_inc(staged_d, 1)
                    if not is_block(b, *range(lag)):
                        out_of_psum(b - lag, (s + lag) % 2, turn_before(turn, lag))

                def out_of_psum(m, s, turn):
                    dve.wait_ge(multiplied, steps_before(i) + m + 3)
                    evacuate(m, s, turn).then_inc(evac_d, 1)

                in_fours(dve, body, steps_of(i))
                for m in range(steps_of(i) - lag, steps_of(i)):
                    out_of_psum(m, m % 2, (m // 4, m % 4))
                dve.wait_ge(evac_d, steps_before(i) + steps_of(i) + 2)

            def at_block(t, b):
                return t[:, bass.ds(b * P, P)]

            in_two = lambda t: t.rearrange("p (b f) -> p b f", f=P)
            two_blocks = lambda t, m: in_two(t[:, bass.ds(m * 2 * P, 2 * P)])
            for_two = lambda t: t.unsqueeze(1).broadcast_to([P, 2, P])

            def own_term(q, bias):
                def add(b):
                    dve.wait_ge(own_multiplied, NB * q + b + 2)
                    V.tensor_tensor(at_block(O, b), bank[7][:, 0:P], bias, ALU.add).then_inc(own_added, 1)
                return (None, None, None, add)

            def sage(i):
                def statistics(m):
                    for j in range(2):
                        last = V.bn_stats(row_stats[:, bass.ds((m * 2 + j) * 6, 6)], at_block(O, m * 2 + j))
                    return last

                def evacuate(m, s, turn):
                    if not is_block(m, 0):
                        dve.wait_ge(evac_d, steps_before(i) + m + 2)
                        statistics(m - 1)
                    return V.tensor_tensor(two_blocks(O, m), in_two(bank[2 + s][:, 0:2 * P]), two_blocks(O, m), ALU.add)

                block_loop(i, evacuate,
                           lambda b, s: V.tensor_tensor(in_two(in_st[s][:, 0:2 * P]), A3[:, bass.ds(b * 2, 2), 0:P],
                                                        over(inv_deg[:, bass.ds(b * 2, 2)], 2, P), ALU.mult))
                ch(statistics(NB // 2 - 1))
                V.tensor_tensor(total[:, :], even_var, odd_var, ALU.add)
                V.tensor_tensor(diff[:, :], even_mean, even_mean, ALU.mult)
                ch(V.tensor_tensor(mean[:, :], odd_mean, odd_mean, ALU.mult))
                ch(V.tensor_tensor(mean[:, :], mean[:, :], diff[:, :], ALU.add))
                root(V.scalar_tensor_tensor(stat[:, :], mean[:, :], P / 2.0, total[:, :], ALU.mult, ALU.add))
                ch(V.tensor_scalar(stat2[:, :], stat2[:, :], L2_EPS, None, ALU.max))
                ch(V.reciprocal(stat2[:, :], stat2[:, :]))

            def edge_columns():
                dve.wait_ge(ranges_b, 1)
                for i, (to, op) in enumerate(((lo_g, ALU.min), (hi_g, ALU.max))):
                    for half, cols in enumerate((4 * P, 3 * P)):
                        ch(V.tensor_reduce(to[:, half * P:half * P + cols // GT],
                                           bank[4 + 2 * i + half][:, 0:cols].rearrange("p (g j) -> p g j", j=GT), AX.X, op))
                ch(V.tensor_copy(blk_i[:, :], lo_g[:, 0:GROUPS + 4]))
                NG = COLS // GT
                dve.wait_ge(edges_c, 6)
                grouped = lambda t: t.rearrange("p (g j) -> p g j", j=GT)
                ch(V.scalar_tensor_tensor(grouped(dl[:, :]), over(lo_g[:, :], NG, GT), -float(P), grouped(dst_f), ALU.mult, ALU.add))
                ch(V.tensor_copy(src_i[:, :], src_f))
                dve.wait_ge(w_c, 2)
                dve.wait_ge(dst_out, 16)
                V.memset(stat[:, :], 0.0).then_inc(prep_done, 1)
                dve.wait_ge(prep_done, 1)

            def source_columns():
                ch(V.scalar_tensor_tensor(tmp_f, et_f[:, :], float(NPAD), src_f, ALU.mult, ALU.add))
                ch(V.tensor_copy(xw_i[:, :], tmp_f))
                ch(V.tensor_scalar(tmp_i, src_i[:, :], 7, None, ALU.logical_shift_right))
                ch(V.tensor_copy(src_hi[:, :], tmp_i))
                ch(V.scalar_tensor_tensor(neg_lo[:, :], src_hi[:, :], -float(P), src_f, ALU.mult, ALU.add))
                ch(V.tensor_scalar(tmp_f, dl[:, :], 2.0 * P, None, ALU.is_lt))
                ch(V.scalar_tensor_tensor(neg_lo[:, :], neg_lo[:, :], 1.0, tmp_f, ALU.add, ALU.mult))
                ch(V.tensor_scalar(neg_lo[:, :], neg_lo[:, :], -1.0, 1.0, ALU.mult, ALU.add))
                for h in range(2):
                    ch(V.tensor_scalar(neg_row[h][:, :], lo_g[:, 0:GROUPS + 4], -float(P), iota_p[:, :], ALU.mult, ALU.subtract))
                    if h:
                        ch(V.tensor_scalar(neg_row[h][:, :], neg_row[h][:, :], float(P), None, ALU.subtract))
                ch(V.tensor_tensor(tmp_f[:, 0:GROUPS], hi_g[:, 0:GROUPS], lo_g[:, 0:GROUPS], ALU.subtract))
                ch(V.reduce_max(rest_f[:, :], tmp_f[:, 0:GROUPS], AX.X))
                ch(V.tensor_scalar(rest_f[:, :], rest_f[:, :], 2.0, None, ALU.is_ge))
                ch(V.tensor_copy(rest_i[:, :], rest_f[:, :]))

            dve.wait_ge(x_in, 32)
            layer_norm()
            edge_columns()
            source_columns()
            dve.wait_ge(weights_in, 16 * WEIGHT_LOADS)
            ch(V.tensor_scalar(rows[:, 4 * P:6 * P], rows[:, 4 * P:6 * P], 0.5, None, ALU.mult))
            wait_for_normed(1)
            sum_pass(0, beside=own_term(0, BL1))
            rest_pass(REST_SAGE1, src_i, AW)
            cnt3 = A3[:, :, P:AW]
            ch(V.reduce_sum(inv_deg[:, :], cnt3, AX.X))
            ch(V.tensor_scalar(inv_deg[:, :], inv_deg[:, :], 1.0, None, ALU.max))
            ch(V.reciprocal(inv_deg[:, :], inv_deg[:, :]))
            sage(SAGE1)
            ch(V.scalar_tensor_tensor(O3, O3, 0.0, by_block(stat2[:, :]), ALU.max, ALU.mult))
            halves, scale, beta = batch_norm(GA0, BE0)
            for at, ready in zip(halves, (h_first, h_ready)):
                ch(scale(at))
                V.tensor_tensor(H3[:, at, :], T3[:, at, :], beta, ALU.add).then_inc(ready, 1)
            dve.wait_ge(h_ready, 2)
            ch(V.tensor_copy(cnt_i[:, :].rearrange("p (b r) -> p b r", r=R), cnt3))
            for d, mask in enumerate((0xFF, 0xFF00, 0xFF0000)):
                ch(V.tensor_scalar(cnt_d[:, :], cnt_i[:, :], mask, None, ALU.bitwise_and))
                ch(V.tensor_copy(digits4[:, :, d, :], cnt_d[:, :].rearrange("p (b r) -> p b r", r=R)))
            V.tensor_copy(counts[:, :].rearrange("p (b r) -> p b r", r=R), cnt3).then_inc(digits_ready, 1)
            dve.wait_ge(digits_ready, 1)
            sum_pass(1, more=pick_weights, beside=own_term(1, BL2))
            dve.wait_ge(wt_done, GROUPS + 2)
            rest_pass(REST_SAGE2, src_i, P)
            rest_weights()
            sage(SAGE2)
            ch(V.tensor_tensor(T3, O3, by_block(stat2[:, :]), ALU.mult))
            ch(V.tensor_tensor(X3, X3, T3, ALU.add))
            layer_norm()
            ch(V.tensor_scalar(wt[:, 0:TILES], wt[:, 0:TILES], 1.0, None, ALU.max))
            ch(V.reciprocal(wt[:, 0:TILES], wt[:, 0:TILES]))
            wait_for_normed(3)
            for l in range(2):
                def evacuate(m, s, turn):
                    if not (l == 0 and is_block(turn[0], 0)):
                        dve.wait_ge(xw_stored[turn[1]], 16 * (stores_at(turn[1]) * l + turn[0]))
                    return V.tensor_copy(xw_out[turn[1]][:, 0:4 * P], bank[2 + 2 * s][:, :])

                def halve_input(b):
                    dve.wait_ge(own_transposed, NB * 2 + b + 2)
                    V.tensor_scalar(at_block(H, b), at_block(H, b), 0.5, None, ALU.mult)

                def half_self(b):
                    dve.wait_ge(own_multiplied, NB * 2 + b + 2)
                    V.scalar_tensor_tensor(at_block(O, b), bank[7][:, 0:P], 0.5, B10, ALU.mult, ALU.add).then_inc(own_added, 1)

                def add_half_input(b):
                    V.scalar_tensor_tensor(at_block(X, b), at_block(H, b), 0.5, at_block(X, b), ALU.mult, ALU.add).then_inc(residual, 1)

                def add_bias(b):
                    dve.wait_ge(residual, 2 * b + 1)
                    V.tensor_tensor(at_block(X, b), at_block(X, b), B11, ALU.add).then_inc(residual, 1)

                def add_half_self(b):
                    dve.wait_ge(residual, 2 * b + 2)
                    dve.wait_ge(own_multiplied, NB * 3 + b + 2)
                    V.scalar_tensor_tensor(at_block(X, b), bank[7][:, 0:P], 0.5, at_block(X, b), ALU.mult, ALU.add).then_inc(own_added, 1)

                block_loop(HOP1 + l, evacuate)
                sum_pass(2 + l, weights=wt, beside=(None, halve_input, None, half_self) if l == 0 else
                         (add_half_input, add_bias, None, add_half_self))
                rest_pass(REST_HOP1 + l, xw_i, P, wt)
                if l == 0:
                    ch(V.scalar_tensor_tensor(T3, AF, 0.5, O3, ALU.mult, ALU.add))
                    V.scalar_tensor_tensor(H3, T3, 0.0, H3, ALU.max, ALU.add).then_inc(h_ready, 1)
                    dve.wait_ge(h_ready, 4)
                else:
                    ch(V.scalar_tensor_tensor(X3, AF, 0.5, X3, ALU.mult, ALU.add))
            layer_norm()
            wait_for_normed(5)
            sum_pass(4, beside=(lambda b: V.tensor_tensor(at_block(X, b), at_block(X, b), BE2, ALU.add),))
            rest_pass(REST_GIN, src_i, P)
            block_loop(GIN, lambda m, s, turn: V.tensor_tensor(two_blocks(O, m), in_two(bank[2 + s][:, 0:2 * P]), for_two(B2), ALU.add),
                       lambda b, s: V.tensor_tensor(in_two(in_st[s][:, 0:2 * P]), A3[:, bass.ds(b * 2, 2), 0:P], two_blocks(H, b), ALU.add), lag=2)
            halves, scale, _ = batch_norm(GA2, BE2)
            for at in halves:
                ch(scale(at))
            ch(V.tensor_tensor(X3, X3, T3, ALU.add))
            layer_norm()
            wait_for_normed(6)
            block_loop(PROJ, lambda m, s, turn: V.tensor_copy(T[:, bass.ds(m * 30 + 4096, 30)], bank[2 + s][:, 0:30]),
                       lambda b, s: V.tensor_copy(in_st[s][:, 0:2 * P], H[:, bass.ds(b * 2 * P, 2 * P)]))
            anchors_of = lambda t: t.unsqueeze(1).broadcast_to([P, NB, A5])
            ch(V.memset(PT, 0.0))
            V.tensor_copy(PT[:, :, 0:A5], PRo[:, :, A5:2 * A5]).then_inc(p_ready, 1)
            ch(V.tensor_tensor(Q3, PRo[:, :, 2 * A5:3 * A5], anchors_of(ab[:, A5:]), ALU.add))
            split(Q3, n5[2], Qp3, ch)
            ch(V.memset(U[:, :], 0.0))
            V.memset(zeros, 0.0).then_inc(zeros_done, 1)
            ch(V.tensor_tensor(n5[0], PRo[:, :, 0:A5], anchors_of(ab[:, 0:A5]), ALU.add))
            ch(V.reduce_max(stat[:, :], n5[0], AX.X))
            V.tensor_tensor(n5[0], n5[0], over(stat[:, :], NB, A5), ALU.subtract).then_inc(soft_in, 1)
            dve.wait_ge(soft_exp, 1)
            ch(V.reduce_sum(stat[:, :], n5[0], AX.X))
            ch(V.reciprocal(stat2[:, :], stat[:, :]))
            ch(V.tensor_tensor(U3[:, :, 0:A5], n5[0], over(stat2[:, :], NB, A5), ALU.mult))
            V.memset(anchors, 0.0).then_inc(anchors_clear, 1)
            ch(V.tensor_tensor(X3, X3, H3, ALU.add))
            STEPS = 9
            with dve.Fori(0, ITERS // 2) as i2:
                for u in range(2):
                    it = i2 * 2 + u
                    step = [0]

                    def then(ins, meanwhile=None):
                        step[0] += 1
                        ins.then_inc(soft_step, 1)
                        if meanwhile:
                            meanwhile()
                        dve.wait_ge(soft_step, it * STEPS + step[0])

                    def columns(g):
                        dve.wait_ge(scattered_d, it * 4 + g + 1)
                        for t in range(g * GT, (g + 1) * GT):
                            V.tensor_scalar(S_l3[:, t, :], iota[:, :], dl[:, bass.ds(it * L16 + t, 1)], None, ALU.is_equal)

                    def source_rows(g):
                        for t in range(g * GT, (g + 1) * GT):
                            V.tensor_scalar(lo_l3[u][:, t, :], iota[:, 0:P], neg_lo[:, bass.ds(it * L16 + t, 1)], 0.0,
                                            ALU.add, ALU.is_equal)

                    def block_columns():
                        dve.wait_ge(parts5, it + 1)
                        V.tensor_tensor(hi_l3, iota[:, 0:49].unsqueeze(1).broadcast_to([P, L16, 49]),
                                        over(src_hi[:, bass.ds(it * L16, L16)], L16, 49), ALU.is_equal)

                    def by_block_and_anchor(g):
                        dve.wait_ge(scattered, it * 4 + g + 1)
                        at = slice(g * GT, (g + 1) * GT)
                        V.tensor_tensor(M_l3[:, at, :].rearrange("p j (d a) -> p j d a", a=A5),
                                        hi_l3[:, at, :].unsqueeze(3).broadcast_to([P, GT, 49, A5]),
                                        b5[:, at, :].unsqueeze(2).broadcast_to([P, GT, 49, A5]), ALU.mult).then_inc(ready5, 1)

                    dve.wait_ge(gathered16[u], 16 * L16 * (i2 + 1))
                    dve.wait_ge(q_looked, it * 4 + 4 + 4)
                    then(V.reduce_sum(z5, bank[4 + u][:, 0:L16 * B5].rearrange("p (j t a) -> p j a t", t=PARTS, a=A5), AX.X),
                         lambda: source_rows(2))
                    V.tensor_tensor(z5, z5, p_rows[u][:, :, 0:A5], ALU.add).then_inc(logits_done, 1)
                    source_rows(3)
                    dve.wait_ge(logits_done, it + 3)
                    then(V.scalar_tensor_tensor(z5, z5, 0.01, z5, ALU.mult, ALU.max), block_columns)
                    then(V.reduce_max(m5, z5, AX.X))
                    V.tensor_tensor(z5, z5, over(m5, L16, A5), ALU.subtract).then_inc(soft_in, 1)
                    for g in range(3):
                        columns(g)
                    dve.wait_ge(soft_exp, it + 2)
                    then(V.reduce_sum(r5, y5, AX.X), lambda: columns(3))
                    then(V.reciprocal(r5, r5))
                    V.tensor_tensor(b5, y5, over(r5, L16, A5), ALU.mult).then_inc(soft_mul, 1)
                    dve.wait_ge(soft_mul, it + 1)
                    groups = iter(range(4))

                    def interleaved(ins):
                        g = next(groups, None)
                        if g is None:
                            ins.then_inc(parts5, 1)
                        else:
                            then(ins, lambda: by_block_and_anchor(g))

                    split(b5, d5, b5p, interleaved)
            dve.wait_ge(lo_ready, 2 * (ITERS + 1))
            dve.wait_ge(scattered_d, GROUPS + 4)
            rest_attention()
            dve.wait_ge(scat_all, 1)
            in_parts = by_dst.rearrange("p (b c) -> p b c", c=D5)[:, :, 0:B5].rearrange("p b (t a) -> p b a t", a=A5)
            for first, last in ((0, 32), (32, 49)):
                ch(V.reduce_sum(n5[1][:, first:last, :], in_parts[:, first:last], AX.X))
            ch(V.tensor_tensor(n5[1][:, 0:49, :], n5[1][:, 0:49, :], bank[2][:, 0:245].rearrange("p (b a) -> p b a", a=A5), ALU.add))
            V.tensor_scalar(U3[:, 0:49, A5:2 * A5], n5[1][:, 0:49, :], 0.5, None, ALU.mult).then_inc(u_ready, 1)

            def add_anchors(m, s, turn):
                for to, sums in ((X[:, bass.ds(m * UB * P, 3 * P)], bank[2 + 2 * s][:, 0:3 * P]),
                                 (X[:, bass.ds(m * UB * P + 3 * P, (UB - 3) * P)], bank[3 + 2 * s][:, 0:(UB - 3) * P])):
                    last = V.tensor_tensor(to, to, sums, ALU.add)
                return last

            block_loop(ANCHOR, add_anchors)


_INS = ['x', 'src', 'dst', 'edge_type_8', 'L0_gnn_Wl1', 'L0_gnn_bl1', 'L0_gnn_Wr1', 'L0_gnn_gamma', 'L0_gnn_beta',
        'L0_gnn_Wl2', 'L0_gnn_bl2', 'L0_gnn_Wr2', 'L1_gnn_bases', 'L1_gnn_comp', 'L1_gnn_root', 'L1_gnn_bias',
        'L2_gnn_W1', 'L2_gnn_b1', 'L2_gnn_W2', 'L2_gnn_b2', 'L2_gnn_gamma', 'L2_gnn_beta', 'L3_gnn_node_anchor',
        'L3_gnn_attn_w', 'L3_gnn_attn_b', 'L3_gnn_edge_anchor', 'L3_gnn_edge_w', 'L3_gnn_edge_b']


def kernel(**inputs):
    import numpy as _np
    import concourse.bacc as _bacc
    from concourse import mybir as _mybir
    from concourse.bass_utils import run_bass_kernel_spmd as _run

    nc = _bacc.Bacc("TRN2", target_bir_lowering=False, num_devices=1)
    arrays, args = {}, []
    for name in _INS:
        a = _np.ascontiguousarray(inputs[name])
        arrays[f"in_{name}"] = a
        args.append(nc.dram_tensor(f"in_{name}", a.shape, _mybir.dt.from_np(a.dtype), kind="ExternalInput").ap())
    args.append(nc.dram_tensor("out_x", (N, P), FP, kind="ExternalOutput").ap())
    gnn_stack(nc, *args)
    r = _run(nc, [arrays], core_ids=[0])
    return r.results[0]["out_x"]
```
